# Optimizing a Trainium2 kernel written in Bass

```python
import numpy as np
import jax
import jax.numpy as jnp

def _softmax(x, axis=-1):
    return jax.nn.softmax(x, axis=axis)
def _gelu(x):
    return jax.nn.gelu(x, approximate=True)
def _silu(x):
    return jax.nn.silu(x)
def _sigmoid(x):
    return jax.nn.sigmoid(x)
def _layernorm(x, axis=-1, eps=1e-5):
    m = jnp.mean(x, axis=axis, keepdims=True)
    v = jnp.var(x, axis=axis, keepdims=True)
    return (x - m) / jnp.sqrt(v + eps)
def _scatter_add(tgt, idx, src, axis=0):
    return tgt.at[idx].add(src)
def _segment_sum(src, seg, n):
    return jax.ops.segment_sum(src, seg, n)

kernel_name = 'mk_conv_preact_d4_conv_nchw32_f53d75'

def setup_inputs(seed: int = 0):
    np.random.seed(seed)
    _w = jnp.asarray
    def _rec_inputs():
        import jax
        import jax.numpy as jnp
        _gk = jax.random.key(seed)
        x = -3.533e-05 + 0.0901 * jax.random.normal(jax.random.fold_in(_gk, 1), (8, 32, 256, 256), jnp.float32)
        return x
    x = _rec_inputs()
    def _L0_conv_setup():
        import jax, jax.numpy as jnp
        import numpy as np
        C_CURV = 1.0
        EPS = 1e-05
        MAX_NORM = (1.0 - 0.0001) / np.sqrt(C_CURV)

        def _artanh(x):
            x = jnp.clip(x, -1.0 + 1e-05, 1.0 - 1e-05)
            return 0.5 * (jnp.log1p(x) - jnp.log1p(-x))

        def _expmap0(v):
            n = jnp.maximum(jnp.linalg.norm(v, axis=1, keepdims=True), EPS)
            sc = np.sqrt(C_CURV)
            return jnp.tanh(sc * n) * v / (sc * n)

        def _logmap0(y):
            n = jnp.maximum(jnp.linalg.norm(y, axis=1, keepdims=True), EPS)
            sc = np.sqrt(C_CURV)
            return _artanh(sc * n) * y / (sc * n)

        def _project(y):
            n = jnp.maximum(jnp.linalg.norm(y, axis=1, keepdims=True), EPS)
            return jnp.where(n > MAX_NORM, y * (MAX_NORM / n), y)

        def _conv3x3(u, w, b):
            y = jax.lax.conv_general_dilated(u, w, window_strides=(1, 1), padding=((1, 1), (1, 1)), dimension_numbers=('NCHW', 'OIHW', 'NCHW'))
            return y + b[None, :, None, None]

        def _hconv(x, w, b):
            return _project(_expmap0(_conv3x3(_logmap0(x), w, b)))

        def _hbn(x, gamma, beta):
            u = _logmap0(x)
            m = u.mean(axis=(0, 2, 3), keepdims=True)
            v = u.var(axis=(0, 2, 3), keepdims=True)
            u = (u - m) / jnp.sqrt(v + 1e-05)
            u = u * gamma[None, :, None, None] + beta[None, :, None, None]
            return _project(_expmap0(u))

        def _hrelu(x):
            return _project(_expmap0(jax.nn.relu(_logmap0(x))))
        key = jax.random.key(seed)
        ks = jax.random.split(key, 8)
        N, Cin, Cmid, Cout, H, W = (8, 32, 32, 32, 256, 256)
        x = _project(_expmap0(0.1 * jax.random.normal(ks[0], (N, Cin, H, W), jnp.float32)))
        fan1 = Cin * 9
        fan2 = Cmid * 9
        w1 = jax.random.normal(ks[1], (Cmid, Cin, 3, 3), jnp.float32) / np.sqrt(fan1)
        b1 = jnp.zeros((Cmid,), jnp.float32)
        g1 = jnp.ones((Cmid,), jnp.float32)
        beta1 = jnp.zeros((Cmid,), jnp.float32)
        w2 = jax.random.normal(ks[2], (Cout, Cmid, 3, 3), jnp.float32) / np.sqrt(fan2)
        b2 = jnp.zeros((Cout,), jnp.float32)
        g2 = jnp.ones((Cout,), jnp.float32)
        beta2 = jnp.zeros((Cout,), jnp.float32)
        return {'x': x, 'w1': w1, 'b1': b1, 'g1': g1, 'beta1': beta1, 'w2': w2, 'b2': b2, 'g2': g2, 'beta2': beta2}
    _L0_conv_all = _L0_conv_setup()
    _L0_conv_in = {k: v for k, v in _L0_conv_all.items() if k in ('w1', 'b1', 'g1', 'beta1', 'w2', 'b2', 'g2', 'beta2', )}
    del _L0_conv_all

    def _L1_conv_setup():
        import jax, jax.numpy as jnp
        import numpy as np

        def _forward(x, t_grid, x_grid, wp1r, wp1i, wp2r, wp2i, wrr, wri):
            xs = x[:, :, ::2, ::2]
            ty = x_grid[:, ::2]
            tx = t_grid[:, ::2]
            dty = ty[0, 1] - ty[0, 0]
            dtx = tx[0, 1] - tx[0, 0]
            Sy, Sx = (xs.shape[-2], xs.shape[-1])
            alpha = jnp.fft.fft2(xs)
            two_pi = 2.0 * jnp.pi
            lam1 = jnp.fft.fftfreq(Sy).astype(jnp.float32) / dty * two_pi * 1j
            lam2 = jnp.fft.fftfreq(Sx).astype(jnp.float32) / dtx * two_pi * 1j
            wp1 = wp1r + 1j * wp1i
            wp2 = wp2r + 1j * wp2i
            res = wrr + 1j * wri
            inv1 = 1.0 / (wp1[None, :, :, :] - lam1[:, None, None, None])
            inv2 = 1.0 / (wp2[None, :, :, :] - lam2[:, None, None, None])
            t1 = jnp.einsum('biox,oikp->bikpx', alpha, inv1)
            res1 = jnp.einsum('bikpx,xikq,ikpq->bkpq', t1, inv2, res)
            zy = x_grid.reshape(-1).astype(jnp.complex64)
            zx = t_grid.reshape(-1).astype(jnp.complex64)
            e1 = jnp.exp(wp1[:, :, :, None] * zy[None, None, None, :])
            e2 = jnp.exp(wp2[:, :, :, None] * zx[None, None, None, :])
            tmp = jnp.einsum('abpq,bipz->abqiz', res1, e1)
            x1 = jnp.real(jnp.einsum('abqiz,biqx->aizx', tmp, e2))
            return x1 / (Sx * Sy)
        key = jax.random.key(seed)
        B, Cin, Cout, Ny, Nx, M1, M2 = (16, 32, 32, 256, 256, 4, 4)
        ks = jax.random.split(key, 7)
        scale = 1.0 / (Cin * Cout)
        x = jax.random.normal(ks[0], (B, Cin, Ny, Nx), dtype=jnp.float32)
        t_grid = jnp.arange(Nx, dtype=jnp.float32).reshape(1, Nx)
        x_grid = jnp.arange(Ny, dtype=jnp.float32).reshape(1, Ny)
        wp1r = scale * jax.random.uniform(ks[1], (Cin, Cout, M1), dtype=jnp.float32)
        wp1i = scale * jax.random.uniform(ks[2], (Cin, Cout, M1), dtype=jnp.float32)
        wp2r = scale * jax.random.uniform(ks[3], (Cin, Cout, M2), dtype=jnp.float32)
        wp2i = scale * jax.random.uniform(ks[4], (Cin, Cout, M2), dtype=jnp.float32)
        wrr = scale * jax.random.uniform(ks[5], (Cin, Cout, M1, M2), dtype=jnp.float32)
        wri = scale * jax.random.uniform(ks[6], (Cin, Cout, M1, M2), dtype=jnp.float32)
        return {'x': x, 't_grid': t_grid, 'x_grid': x_grid, 'wp1r': wp1r, 'wp1i': wp1i, 'wp2r': wp2r, 'wp2i': wp2i, 'wrr': wrr, 'wri': wri}
    _L1_conv_all = _L1_conv_setup()
    _L1_conv_in = {k: v for k, v in _L1_conv_all.items() if k in ('t_grid', 'x_grid', 'wp1r', 'wp1i', 'wp2r', 'wp2i', 'wrr', 'wri', )}
    del _L1_conv_all

    def _L2_conv_setup():
        import jax, jax.numpy as jnp
        import numpy as np
        WS = 8
        S = 2
        GRID = jnp.linspace(-2.0, 2.0, 8)
        DENOM = 4.0 / 7.0

        def _layernorm(x, g, b, eps=1e-05):
            mu = x.mean(-1, keepdims=True)
            var = ((x - mu) ** 2).mean(-1, keepdims=True)
            return (x - mu) * jax.lax.rsqrt(var + eps) * g + b

        def _fastkan(x, ln_g, ln_b, ws, wb, bb):
            ln = _layernorm(x, ln_g, ln_b)
            basis = jnp.exp(-((ln[..., None] - GRID) / DENOM) ** 2)
            flat = basis.reshape(*basis.shape[:-2], -1)
            return flat @ ws.T + jax.nn.silu(x) @ wb.T + bb
        key = jax.random.key(seed)
        ks = jax.random.split(key, 16)
        d = {'x': jax.random.normal(ks[0], (4, 32, 256, 256), dtype=jnp.float32), 'pn_g': jnp.ones((32,), jnp.float32), 'pn_b': jnp.zeros((32,), jnp.float32), 'k1_ln_g': jnp.ones((16,), jnp.float32), 'k1_ln_b': jnp.zeros((16,), jnp.float32), 'k1_ws': jax.random.normal(ks[1], (16, 128), jnp.float32) * 0.1, 'k1_wb': jax.random.normal(ks[2], (16, 16), jnp.float32) * 0.1, 'k1_bb': jnp.zeros((16,), jnp.float32), 'k2_ln_g': jnp.ones((16,), jnp.float32), 'k2_ln_b': jnp.zeros((16,), jnp.float32), 'k2_ws': jax.random.normal(ks[3], (16, 128), jnp.float32) * 0.1, 'k2_wb': jax.random.normal(ks[4], (16, 16), jnp.float32) * 0.1, 'k2_bb': jnp.zeros((16,), jnp.float32), 'k3_ln_g': jnp.ones((32,), jnp.float32), 'k3_ln_b': jnp.zeros((32,), jnp.float32), 'k3_ws': jax.random.normal(ks[5], (32, 256), jnp.float32) * 0.1, 'k3_wb': jax.random.normal(ks[6], (32, 32), jnp.float32) * 0.1, 'k3_bb': jnp.zeros((32,), jnp.float32), 'k4_ln_g': jnp.ones((32,), jnp.float32), 'k4_ln_b': jnp.zeros((32,), jnp.float32), 'k4_ws': jax.random.normal(ks[7], (32, 256), jnp.float32) * 0.1, 'k4_wb': jax.random.normal(ks[8], (32, 32), jnp.float32) * 0.1, 'k4_bb': jnp.zeros((32,), jnp.float32)}
        return d
    _L2_conv_all = _L2_conv_setup()
    _L2_conv_in = {k: v for k, v in _L2_conv_all.items() if k in ('pn_g', 'pn_b', 'k1_ln_g', 'k1_ln_b', 'k1_ws', 'k1_wb', 'k1_bb', 'k2_ln_g', 'k2_ln_b', 'k2_ws', 'k2_wb', 'k2_bb', 'k3_ln_g', 'k3_ln_b', 'k3_ws', 'k3_wb', 'k3_bb', 'k4_ln_g', 'k4_ln_b', 'k4_ws', 'k4_wb', 'k4_bb', )}
    del _L2_conv_all

    def _L3_conv_setup():
        import jax, jax.numpy as jnp
        import numpy as np
        KERNEL_SIZE = 3
        ALPHA = 10.0
        NUM_NEIGHBORS = KERNEL_SIZE ** 2 - 1
        COFF = 2.0 ** NUM_NEIGHBORS - 1.0
        key = jax.random.key(seed)
        in_x = jax.random.normal(key, (8, 32, 256, 256), dtype=jnp.float32)
        return {'in_x': in_x}
    _L3_conv_all = _L3_conv_setup()
    _L3_conv_in = {k: v for k, v in _L3_conv_all.items() if k in ()}
    del _L3_conv_all

    return {
        "x": x,
        "L0_conv_w1": _L0_conv_in["w1"],
        "L0_conv_b1": _L0_conv_in["b1"],
        "L0_conv_g1": _L0_conv_in["g1"],
        "L0_conv_beta1": _L0_conv_in["beta1"],
        "L0_conv_w2": _L0_conv_in["w2"],
        "L0_conv_b2": _L0_conv_in["b2"],
        "L0_conv_g2": _L0_conv_in["g2"],
        "L0_conv_beta2": _L0_conv_in["beta2"],
        "L1_conv_t_grid": _L1_conv_in["t_grid"],
        "L1_conv_x_grid": _L1_conv_in["x_grid"],
        "L1_conv_wp1r": _L1_conv_in["wp1r"],
        "L1_conv_wp1i": _L1_conv_in["wp1i"],
        "L1_conv_wp2r": _L1_conv_in["wp2r"],
        "L1_conv_wp2i": _L1_conv_in["wp2i"],
        "L1_conv_wrr": _L1_conv_in["wrr"],
        "L1_conv_wri": _L1_conv_in["wri"],
        "L2_conv_pn_g": _L2_conv_in["pn_g"],
        "L2_conv_pn_b": _L2_conv_in["pn_b"],
        "L2_conv_k1_ln_g": _L2_conv_in["k1_ln_g"],
        "L2_conv_k1_ln_b": _L2_conv_in["k1_ln_b"],
        "L2_conv_k1_ws": _L2_conv_in["k1_ws"],
        "L2_conv_k1_wb": _L2_conv_in["k1_wb"],
        "L2_conv_k1_bb": _L2_conv_in["k1_bb"],
        "L2_conv_k2_ln_g": _L2_conv_in["k2_ln_g"],
        "L2_conv_k2_ln_b": _L2_conv_in["k2_ln_b"],
        "L2_conv_k2_ws": _L2_conv_in["k2_ws"],
        "L2_conv_k2_wb": _L2_conv_in["k2_wb"],
        "L2_conv_k2_bb": _L2_conv_in["k2_bb"],
        "L2_conv_k3_ln_g": _L2_conv_in["k3_ln_g"],
        "L2_conv_k3_ln_b": _L2_conv_in["k3_ln_b"],
        "L2_conv_k3_ws": _L2_conv_in["k3_ws"],
        "L2_conv_k3_wb": _L2_conv_in["k3_wb"],
        "L2_conv_k3_bb": _L2_conv_in["k3_bb"],
        "L2_conv_k4_ln_g": _L2_conv_in["k4_ln_g"],
        "L2_conv_k4_ln_b": _L2_conv_in["k4_ln_b"],
        "L2_conv_k4_ws": _L2_conv_in["k4_ws"],
        "L2_conv_k4_wb": _L2_conv_in["k4_wb"],
        "L2_conv_k4_bb": _L2_conv_in["k4_bb"],
    }

def reference(x, L0_conv_w1, L0_conv_b1, L0_conv_g1, L0_conv_beta1, L0_conv_w2, L0_conv_b2, L0_conv_g2, L0_conv_beta2, L1_conv_t_grid, L1_conv_x_grid, L1_conv_wp1r, L1_conv_wp1i, L1_conv_wp2r, L1_conv_wp2i, L1_conv_wrr, L1_conv_wri, L2_conv_pn_g, L2_conv_pn_b, L2_conv_k1_ln_g, L2_conv_k1_ln_b, L2_conv_k1_ws, L2_conv_k1_wb, L2_conv_k1_bb, L2_conv_k2_ln_g, L2_conv_k2_ln_b, L2_conv_k2_ws, L2_conv_k2_wb, L2_conv_k2_bb, L2_conv_k3_ln_g, L2_conv_k3_ln_b, L2_conv_k3_ws, L2_conv_k3_wb, L2_conv_k3_bb, L2_conv_k4_ln_g, L2_conv_k4_ln_b, L2_conv_k4_ws, L2_conv_k4_wb, L2_conv_k4_bb):
    import jax
    import jax.numpy as jnp
    def _L0_conv_ref(x, w1, b1, g1, beta1, w2, b2, g2, beta2):
        import jax, jax.numpy as jnp
        import numpy as np
        C_CURV = 1.0
        EPS = 1e-05
        MAX_NORM = (1.0 - 0.0001) / np.sqrt(C_CURV)

        def _artanh(x):
            x = jnp.clip(x, -1.0 + 1e-05, 1.0 - 1e-05)
            return 0.5 * (jnp.log1p(x) - jnp.log1p(-x))

        def _expmap0(v):
            n = jnp.maximum(jnp.linalg.norm(v, axis=1, keepdims=True), EPS)
            sc = np.sqrt(C_CURV)
            return jnp.tanh(sc * n) * v / (sc * n)

        def _logmap0(y):
            n = jnp.maximum(jnp.linalg.norm(y, axis=1, keepdims=True), EPS)
            sc = np.sqrt(C_CURV)
            return _artanh(sc * n) * y / (sc * n)

        def _project(y):
            n = jnp.maximum(jnp.linalg.norm(y, axis=1, keepdims=True), EPS)
            return jnp.where(n > MAX_NORM, y * (MAX_NORM / n), y)

        def _conv3x3(u, w, b):
            y = jax.lax.conv_general_dilated(u, w, window_strides=(1, 1), padding=((1, 1), (1, 1)), dimension_numbers=('NCHW', 'OIHW', 'NCHW'))
            return y + b[None, :, None, None]

        def _hconv(x, w, b):
            return _project(_expmap0(_conv3x3(_logmap0(x), w, b)))

        def _hbn(x, gamma, beta):
            u = _logmap0(x)
            m = u.mean(axis=(0, 2, 3), keepdims=True)
            v = u.var(axis=(0, 2, 3), keepdims=True)
            u = (u - m) / jnp.sqrt(v + 1e-05)
            u = u * gamma[None, :, None, None] + beta[None, :, None, None]
            return _project(_expmap0(u))

        def _hrelu(x):
            return _project(_expmap0(jax.nn.relu(_logmap0(x))))
        out = _hconv(x, w1, b1)
        out = _hbn(out, g1, beta1)
        out = _hrelu(out)
        out = _hconv(out, w2, b2)
        out = _hbn(out, g2, beta2)
        out = _hrelu(out)
        return out

    def _L1_conv_ref(x, t_grid, x_grid, wp1r, wp1i, wp2r, wp2i, wrr, wri):
        import jax, jax.numpy as jnp
        import numpy as np

        def _forward(x, t_grid, x_grid, wp1r, wp1i, wp2r, wp2i, wrr, wri):
            xs = x[:, :, ::2, ::2]
            ty = x_grid[:, ::2]
            tx = t_grid[:, ::2]
            dty = ty[0, 1] - ty[0, 0]
            dtx = tx[0, 1] - tx[0, 0]
            Sy, Sx = (xs.shape[-2], xs.shape[-1])
            alpha = jnp.fft.fft2(xs)
            two_pi = 2.0 * jnp.pi
            lam1 = jnp.fft.fftfreq(Sy).astype(jnp.float32) / dty * two_pi * 1j
            lam2 = jnp.fft.fftfreq(Sx).astype(jnp.float32) / dtx * two_pi * 1j
            wp1 = wp1r + 1j * wp1i
            wp2 = wp2r + 1j * wp2i
            res = wrr + 1j * wri
            inv1 = 1.0 / (wp1[None, :, :, :] - lam1[:, None, None, None])
            inv2 = 1.0 / (wp2[None, :, :, :] - lam2[:, None, None, None])
            t1 = jnp.einsum('biox,oikp->bikpx', alpha, inv1)
            res1 = jnp.einsum('bikpx,xikq,ikpq->bkpq', t1, inv2, res)
            zy = x_grid.reshape(-1).astype(jnp.complex64)
            zx = t_grid.reshape(-1).astype(jnp.complex64)
            e1 = jnp.exp(wp1[:, :, :, None] * zy[None, None, None, :])
            e2 = jnp.exp(wp2[:, :, :, None] * zx[None, None, None, :])
            tmp = jnp.einsum('abpq,bipz->abqiz', res1, e1)
            x1 = jnp.real(jnp.einsum('abqiz,biqx->aizx', tmp, e2))
            return x1 / (Sx * Sy)
        return _forward(x, t_grid, x_grid, wp1r, wp1i, wp2r, wp2i, wrr, wri)

    def _L2_conv_ref(x, pn_g, pn_b, k1_ln_g, k1_ln_b, k1_ws, k1_wb, k1_bb, k2_ln_g, k2_ln_b, k2_ws, k2_wb, k2_bb, k3_ln_g, k3_ln_b, k3_ws, k3_wb, k3_bb, k4_ln_g, k4_ln_b, k4_ws, k4_wb, k4_bb):
        import jax, jax.numpy as jnp
        import numpy as np
        WS = 8
        S = 2
        GRID = jnp.linspace(-2.0, 2.0, 8)
        DENOM = 4.0 / 7.0

        def _layernorm(x, g, b, eps=1e-05):
            mu = x.mean(-1, keepdims=True)
            var = ((x - mu) ** 2).mean(-1, keepdims=True)
            return (x - mu) * jax.lax.rsqrt(var + eps) * g + b

        def _fastkan(x, ln_g, ln_b, ws, wb, bb):
            ln = _layernorm(x, ln_g, ln_b)
            basis = jnp.exp(-((ln[..., None] - GRID) / DENOM) ** 2)
            flat = basis.reshape(*basis.shape[:-2], -1)
            return flat @ ws.T + jax.nn.silu(x) @ wb.T + bb
        B, C, H, W = x.shape
        c = C // S
        xh = jnp.transpose(x, (0, 2, 3, 1))
        wins = xh.reshape(B, H // WS, WS, W // WS, WS, C).transpose(0, 1, 3, 2, 4, 5).reshape(-1, WS, WS, C)
        b = wins.shape[0]
        y = _layernorm(wins, pn_g, pn_b)
        a = y.reshape(b, WS, WS, c, S).transpose(0, 2, 3, 1, 4).reshape(b, WS * c, WS * S)
        a = _fastkan(a, k1_ln_g, k1_ln_b, k1_ws, k1_wb, k1_bb)
        a = a.reshape(b, WS, c, WS, S).transpose(0, 3, 1, 2, 4).reshape(b, WS, WS, C)
        d = y.reshape(b, WS, WS, c, S).transpose(0, 1, 3, 2, 4).reshape(b, WS * c, WS * S)
        d = _fastkan(d, k2_ln_g, k2_ln_b, k2_ws, k2_wb, k2_bb)
        d = d.reshape(b, WS, c, WS, S).transpose(0, 1, 3, 2, 4).reshape(b, WS, WS, C)
        e = _fastkan(y.reshape(b, WS * WS, C), k3_ln_g, k3_ln_b, k3_ws, k3_wb, k3_bb).reshape(b, WS, WS, C)
        z = a + d + e
        z = _fastkan(z.reshape(b, WS * WS, C), k4_ln_g, k4_ln_b, k4_ws, k4_wb, k4_bb).reshape(b, WS, WS, C)
        out = z + wins
        out = out.reshape(B, H // WS, W // WS, WS, WS, C).transpose(0, 1, 3, 2, 4, 5).reshape(B, H, W, C)
        return jnp.transpose(out, (0, 3, 1, 2))

    def _L3_conv_ref(in_x):
        import jax, jax.numpy as jnp
        import numpy as np
        KERNEL_SIZE = 3
        ALPHA = 10.0
        NUM_NEIGHBORS = KERNEL_SIZE ** 2 - 1
        COFF = 2.0 ** NUM_NEIGHBORS - 1.0
        b, c, h, w = in_x.shape
        p = KERNEL_SIZE // 2
        dtype = in_x.dtype
        ci = KERNEL_SIZE // 2
        xp = jnp.pad(in_x, ((0, 0), (0, 0), (p, p), (p, p)))
        offsets = [(i, j) for i in range(KERNEL_SIZE) for j in range(KERNEL_SIZE) if not (i == ci and j == ci)]
        neighbors = jnp.stack([xp[:, :, i:i + h, j:j + w] for i, j in offsets], axis=2)
        center = in_x[:, :, None, :, :]
        binary_codes = jax.nn.sigmoid(jnp.asarray(ALPHA, dtype) * (neighbors - center))
        power_weights = (2.0 ** jnp.arange(NUM_NEIGHBORS, dtype=jnp.float32)).astype(dtype)
        lbp = jnp.einsum('bcnhw,n->bchw', binary_codes, power_weights)
        return lbp / jnp.asarray(COFF, dtype)

    def _gn(v, G=16, eps=1e-5):
        B_, C_, H_, W_ = v.shape
        g = v.reshape(B_, G, C_ // G, H_, W_)
        m = jnp.mean(g, axis=(2, 3, 4), keepdims=True)
        s = jnp.var(g, axis=(2, 3, 4), keepdims=True)
        return ((g - m) / jnp.sqrt(s + eps)).reshape(v.shape)

    def _ln_c(v, eps=1e-6):
        m = jnp.mean(v, axis=1, keepdims=True)
        s = jnp.var(v, axis=1, keepdims=True)
        return (v - m) / jnp.sqrt(s + eps)

    def _ln_t(v, eps=1e-5):
        m = jnp.mean(v, axis=-1, keepdims=True)
        s = jnp.var(v, axis=-1, keepdims=True)
        return (v - m) / jnp.sqrt(s + eps)

    def _to_tokens(v):
        B_, C_, H_, W_ = v.shape
        return v.reshape(B_, C_, H_ * W_).transpose(0, 2, 1)
    def _from_tokens(t, like):
        B_, C_, H_, W_ = like.shape
        return t.transpose(0, 2, 1).reshape(B_, C_, H_, W_)

    x = x + _L0_conv_ref(_gn(x), L0_conv_w1, L0_conv_b1, L0_conv_g1, L0_conv_beta1, L0_conv_w2, L0_conv_b2, L0_conv_g2, L0_conv_beta2)
    x = x + _L1_conv_ref(_gn(x), L1_conv_t_grid, L1_conv_x_grid, L1_conv_wp1r, L1_conv_wp1i, L1_conv_wp2r, L1_conv_wp2i, L1_conv_wrr, L1_conv_wri)
    x = x + _L2_conv_ref(_gn(x), L2_conv_pn_g, L2_conv_pn_b, L2_conv_k1_ln_g, L2_conv_k1_ln_b, L2_conv_k1_ws, L2_conv_k1_wb, L2_conv_k1_bb, L2_conv_k2_ln_g, L2_conv_k2_ln_b, L2_conv_k2_ws, L2_conv_k2_wb, L2_conv_k2_bb, L2_conv_k3_ln_g, L2_conv_k3_ln_b, L2_conv_k3_ws, L2_conv_k3_wb, L2_conv_k3_bb, L2_conv_k4_ln_g, L2_conv_k4_ln_b, L2_conv_k4_ws, L2_conv_k4_wb, L2_conv_k4_bb)
    x = x + _L3_conv_ref(_gn(x))
    return x


_drawn_inputs = setup_inputs


def setup_inputs(seed=0):
    import zlib

    import numpy as np

    out = dict(_drawn_inputs(seed))
    spreads = {'L0_conv_b1': (0.0, 2.0),
     'L0_conv_g1': (1.0, 0.2),
     'L0_conv_beta1': (0.0, 0.477),
     'L0_conv_b2': (0.0, 0.8),
     'L0_conv_g2': (1.0, 0.2),
     'L0_conv_beta2': (0.0, 0.1),
     'L2_conv_pn_g': (1.0, 0.6),
     'L2_conv_pn_b': (0.0, 2.0),
     'L2_conv_k1_ln_g': (1.0, 0.6),
     'L2_conv_k1_ln_b': (0.0, 2.0),
     'L2_conv_k1_bb': (0.0, 2.0),
     'L2_conv_k2_ln_g': (1.0, 0.6),
     'L2_conv_k2_ln_b': (0.0, 2.0),
     'L2_conv_k2_bb': (0.0, 2.0),
     'L2_conv_k3_ln_g': (1.0, 0.6),
     'L2_conv_k3_ln_b': (0.0, 2.0),
     'L2_conv_k3_bb': (0.0, 2.0),
     'L2_conv_k4_ln_g': (1.0, 0.6),
     'L2_conv_k4_ln_b': (0.0, 2.0),
     'L2_conv_k4_bb': (0.0, 2.0)}
    factors = {'L2_conv_k1_ws': 200.0,
     'L2_conv_k1_wb': 200.0,
     'L2_conv_k2_ws': 200.0,
     'L2_conv_k2_wb': 200.0,
     'L2_conv_k3_ws': 200.0,
     'L2_conv_k3_wb': 64.0,
     'L2_conv_k4_ws': 200.0,
     'L2_conv_k4_wb': 64.0}
    for name, (base, spread) in spreads.items():
        noise = np.random.default_rng([zlib.crc32(name.encode()), seed]).standard_normal(out[name].shape)
        drawn = base * np.exp(spread * noise) if base else spread * noise
        out[name] = jnp.asarray(drawn.astype(out[name].dtype))
    for name, factor in factors.items():
        out[name] = (out[name] * factor).astype(out[name].dtype)
    return out
```

```python
from contextlib import ExitStack

import numpy as np

import concourse.bass as bass
from concourse import mybir

F32 = mybir.dt.float32
F32R = mybir.dt.float32r
I32 = mybir.dt.int32
ALU = mybir.AluOpType
ACT = mybir.ActivationFunctionType

P = 128
QUAD = 32
IMAGES, CH, ROWS, COLS = 8, 32, 256, 256
GROUP = P // CH
HALVES = IMAGES // GROUP
BAND = 8
BANDS = ROWS // BAND
TILE = BAND * COLS
BANK = 512
BLOCKS = TILE // P
HALO = BAND + 2
PAD = COLS + 2

MAX_NORM = 1.0 - 0.0001
ATANH_MAX = float(np.arctanh(np.float64(MAX_NORM)))
EPS_NORM = 1e-5
EPS_LN = 1e-5
CLIP = 1.0 - 1e-5


def pipeline(eng, count, stages):
    deep = max(lag for lag, _ in stages)
    for t in range(deep + 1):
        for lag, step in stages:
            if t >= lag:
                step(t - lag)
    with eng.Fori(deep + 1, count) as t:
        for lag, step in stages:
            step(t - lag)
    for t in range(count, count + deep):
        for lag, step in stages:
            if t - lag < count:
                step(t - lag)


def wait_past(eng, sem, value):
    if not isinstance(value, int) or value > 0:
        eng.wait_ge(sem, value)


def rsqrt_steps(dve, y, q, t):
    dve.tensor_scalar(y.bitcast(I32), q.bitcast(I32), -0.5, 1597463007.0, ALU.mult, ALU.add)
    for _ in range(3):
        dve.drain()
        dve.tensor_tensor(t, y, y, ALU.mult)
        dve.drain()
        dve.scalar_tensor_tensor(t, t, -0.5, q, ALU.mult, ALU.mult)
        dve.drain()
        dve.scalar_tensor_tensor(y, t, 1.5, y, ALU.add, ALU.mult)
    dve.drain()


def split_hi_lo(dve, hi, lo, s):
    dve.tensor_copy(hi.bitcast(F32R), s)
    dve.drain()
    return dve.tensor_tensor(lo, s, hi, ALU.subtract)


class Net:

    def __init__(self, nc, ctx, ins):
        self.nc, self.ctx, self.ins = nc, ctx, ins
        self.count, self.sems = 0, {}

    def sb(self, ctx, name, shape, dt=F32):
        self.count += 1
        return ctx.enter_context(self.nc.sbuf_tensor(f"{name}_{self.count}", shape, dt))

    def ps(self, ctx, name, shape):
        self.count += 1
        return ctx.enter_context(self.nc.psum_tensor(f"{name}_{self.count}", shape, F32))

    def sem(self, ctx, name):
        self.count += 1
        if ctx not in self.sems:
            self.sems[ctx] = []
            ctx.callback(self.clear, ctx)
        self.sems[ctx].append(self.nc.alloc_semaphore(f"{name}_{self.count}"))
        return self.sems[ctx][-1]

    def clear(self, ctx):
        self.nc.clear_and_free_semaphores(self.sems.pop(ctx))
        self.nc.all_engine_barrier()

    def scratch(self, name):
        return self.nc.dram_tensor(name, [BANDS, HALVES, P, TILE], F32).ap()


def load_constants(net):
    nc, ctx, ins = net.nc, net.ctx, net.ins
    names = ["ident", "ones4", "pair", "channel", "sel4"]
    net.c = {n: net.sb(ctx, n, list(ins["c_" + n].shape)) for n in names if n != "sel4"}
    net.c["sel4"] = net.sb(ctx, "sel4r", [P, BLOCKS, P], F32R)
    with ExitStack() as local:
        staged = net.sb(local, "staged", [P, BLOCKS, P])
        loaded, copied = net.sem(local, "loaded"), net.sem(local, "copied")
        block = local.enter_context(nc.Block())

        @block.sync
        def _(sp):
            for n in names:
                dst = staged if n == "sel4" else net.c[n]
                sp.dma_start(dst[:], ins["c_" + n]).then_inc(loaded, 16)
            sp.wait_ge(loaded, 16 * len(names))
            sp.wait_ge(copied, 1)

        @block.vector
        def _(dve):
            dve.wait_ge(loaded, 16 * len(names))
            nc.vector.tensor_copy(net.c["sel4"][:], staged[:]).then_inc(copied, 1)


def norm_vectors(net, stats, average, eps, scale, bias, gamma=None, beta=None):
    nc = net.nc
    n = stats.shape[1]
    with ExitStack() as local:
        mv = net.sb(local, "mean_var", [P, n, 2])
        mean = net.sb(local, "mean", [P, n])
        spread = net.sb(local, "spread", [P, n])
        y = net.sb(local, "rstd", [P, n])
        t = net.sb(local, "t", [P, n])
        pm = net.ps(local, "pm", [P, 2, BANK])
        own, gmean, sp_ready, gvar = (net.sem(local, k) for k in ("own", "gmean", "spread", "gvar"))
        block = local.enter_context(nc.Block())

        @block.tensor
        def _(pe):
            pe.wait_ge(own, 1)
            nc.tensor.matmul(pm[:, 0, 0:n], average, mv[:, :, 0], start=True, stop=True).then_inc(gmean, 1)
            pe.wait_ge(sp_ready, 1)
            nc.tensor.matmul(pm[:, 1, 0:n], average, spread[:], start=True, stop=True).then_inc(gvar, 1)

        @block.vector
        def _(dve):
            v = nc.vector
            for h in range(n):
                v.bn_aggr(mv[:, h, :], stats[:, h])
            v.drain()
            v.tensor_copy(t[:], mv[:, :, 0]).then_inc(own, 1)
            dve.wait_ge(gmean, 1)
            v.tensor_copy(mean[:], pm[:, 0, 0:n])
            v.drain()
            v.tensor_tensor(t[:], mv[:, :, 0], mean[:], ALU.subtract)
            v.drain()
            v.tensor_tensor(t[:], t[:], t[:], ALU.mult)
            v.drain()
            v.tensor_tensor(spread[:], t[:], mv[:, :, 1], ALU.add).then_inc(sp_ready, 1)
            dve.wait_ge(gvar, 1)
            v.tensor_scalar(spread[:], pm[:, 1, 0:n], eps, None, ALU.add)
            v.drain()
            rsqrt_steps(v, y[:], spread[:], t[:])
            if gamma is None:
                v.tensor_copy(scale, y[:])
            else:
                v.tensor_scalar(scale, y[:], gamma, None, ALU.mult)
            v.drain()
            v.tensor_tensor(t[:], mean[:], scale, ALU.mult)
            v.drain()
            if beta is None:
                v.tensor_scalar(bias, t[:], -1.0, None, ALU.mult)
            else:
                v.tensor_scalar(bias, t[:], -1.0, beta, ALU.mult, ALU.add)
            v.drain()


def input_stats(net, x_rows, stats):
    nc = net.nc
    span = 2
    with ExitStack() as local:
        xt = net.sb(local, "xt", [P, HALVES, span * TILE])
        part = net.sb(local, "part", [P, HALVES, span * TILE // BANK * 6])
        loaded = [net.sem(local, f"loaded{h}") for h in range(HALVES)]
        used = [net.sem(local, f"used{h}") for h in range(HALVES)]
        block = local.enter_context(nc.Block())
        wide = x_rows.rearrange("p (t n) -> p t n", n=span * TILE)
        into = stats.rearrange("p h (t n) -> p h t n", n=span * TILE // BANK * 6)

        @block.sync
        def _(sp):
            def load(t):
                for h in range(HALVES):
                    wait_past(sp, used[h], t)
                    sp.dma_start(xt[:, h, :], wide[P * h:P * h + P, t, :]).then_inc(loaded[h], 16)
            pipeline(sp, BANDS // span, [(0, load)])

        @block.vector
        def _(dve):
            v = nc.vector

            def measure(t):
                for h in range(HALVES):
                    dve.wait_ge(loaded[h], 16 * t + 16)
                    for k in range(span * TILE // BANK):
                        last = v.bn_stats(part[:, h, 6 * k:6 * k + 6], xt[:, h, BANK * k:BANK * k + BANK])
                    last.then_inc(used[h], 1)
                    v.drain()
                    v.tensor_copy(into[:, h, t, :], part[:, h, :])
            pipeline(dve, BANDS // span, [(0, measure)])


def conv_layer(net, source, scale, bias, weights, conv_bias, target, stats, first):
    nc, c = net.nc, net.c
    HT = HALO * COLS
    HB = HT // P
    HG = HB // 2
    with ExitStack() as local:
        def sb(name, shape, dt=F32):
            return net.sb(local, name, shape, dt)
        xt = sb("xt", [P, HALVES, HALO, COLS])
        xn = sb("xn", [P, HALVES, HT])
        sq = sb("sq", [P, HALVES, HT])
        u = sb("u", [P, HALVES, HALO, PAD])
        uc = sb("uc", [P, HALVES, GROUP, BAND // 2, PAD])
        v_sb = sb("v", [P, HALVES, BAND, COLS])
        sqv = sb("sqv", [P, HALVES, TILE])
        out = sb("out", [P, HALVES, TILE])
        w_sb = sb("w", [P, 2, 3, CH])
        cb = sb("cb", [P, 1])
        top, bot = sb("top", [P, BANDS]), sb("bot", [P, BANDS])
        part = sb("part", [P, HALVES, TILE // BANK * 6])
        n2, q, rn, t_, nc_, l1, l2, sl, pl, xx = (sb(k, [P, HALVES, HB * GROUP]) for k in
                                                  ("n2", "q", "rn", "t", "nclip", "l1", "l2", "sl", "pl", "xx"))
        sp1 = sb("sp1", [P, HALVES, 2, P])
        spT = sb("spT", [P, HALVES, 2, P], F32R)
        m2 = sb("m2", [P, HALVES, BLOCKS * GROUP])
        sp2 = sb("sp2", [P, HALVES, P])
        sp2T = sb("sp2T", [P, HALVES, P], F32R)
        small = net.ps(local, "small", [P, BANK])
        turned = net.ps(local, "turned", [P, HALVES, 2, P])
        spread1 = net.ps(local, "spread1", [P, 2, BANK])
        spread2 = net.ps(local, "spread2", [P, 2, BANK])
        conv = net.ps(local, "conv", [P, 2, BANK])
        NC1 = HB * GROUP
        NC2 = BLOCKS * GROUP
        pc1 = small[:, 0:2 * NC1].rearrange("p (h n) -> p h n", h=2)
        pc2 = small[:, 2 * NC1:2 * NC1 + 2 * NC2].rearrange("p (h n) -> p h n", h=2)
        turned2 = turned[:, :, 0, :]

        def sem(name):
            return net.sem(local, name)
        loaded = [sem(f"loaded{h}") for h in range(2)]
        uc_loaded = [sem(f"uc_loaded{h}") for h in range(2)]
        stored = [sem(f"stored{h}") for h in range(2)]
        ready = sem("params")
        zeroed = sem("zeroed")
        (normed, squared, summed1, normsq, logs, factors1, turned1_ready, turned1_copied, spread1_ready, u_ready,
         conv_ready, evacuated, summed2, factors2, turned2_ready, turned2_copied, spread2_ready, out_ready,
         read1, read2) = (sem(k) for k in (
             "normed", "squared", "summed1", "normsq", "logs", "factors1", "turned1_ready", "turned1_copied",
             "spread1_ready", "u_ready", "conv_ready", "evacuated", "summed2", "factors2", "turned2_ready",
             "turned2_copied", "spread2_ready", "out_ready", "read1", "read2"))
        block = local.enter_context(nc.Block())
        CHUNKS1 = HT // BANK
        CHUNKS2 = TILE // BANK

        @block.sync
        def _(sp):
            sp.dma_start(w_sb[:], weights).then_inc(ready, 16)
            sp.dma_start(cb[:], conv_bias).then_inc(ready, 16)

            def load(r):
                for h in range(HALVES):
                    wait_past(sp, normed if first else squared, 2 * (r - 1) + h + 1)
                    if first:
                        rows = source[P * h:P * h + P, :].rearrange("p (r w) -> p r w", w=COLS)
                        bands = source[P * h:P * h + P, :].rearrange("p (t n) -> p t n", n=TILE)
                        main = bands[:, r, :]
                        above = rows[:, (r * BAND + ROWS - 1) % ROWS, :]
                        below = rows[:, (r * BAND + BAND) % ROWS, :]
                    else:
                        main = source[r, h]
                        above = source[(r + BANDS - 1) % BANDS, h, :, (BAND - 1) * COLS:]
                        below = source[(r + 1) % BANDS, h, :, 0:COLS]
                    sp.dma_start(xt[:, h, 1:BAND + 1, :].rearrange("p r w -> p (r w)"), main).then_inc(loaded[h], 16)
                    sp.dma_start(xt[:, h, 0, :], above).then_inc(loaded[h], 16)
                    sp.dma_start(xt[:, h, BAND + 1, :], below).then_inc(loaded[h], 16)

            def regroup(r):
                for h in range(HALVES):
                    sp.wait_ge(u_ready, (2 * r + h + 1) * CHUNKS1)
                    wait_past(sp, conv_ready, (2 * (r - 1) + h + 1) * 4)
                    for b in range(GROUP):
                        for k in range(4):
                            sp.dma_start(uc[QUAD * k:QUAD * k + QUAD, h, b, :, :],
                                         u[QUAD * b:QUAD * b + QUAD, h, k:k + BAND - 1:2, :]).then_inc(uc_loaded[h], 16)

            def store(r):
                for h in range(HALVES):
                    sp.wait_ge(out_ready, (2 * r + h + 1) * CHUNKS2)
                    sp.dma_start(target[r, h], out[:, h, :]).then_inc(stored[h], 16)
            pipeline(sp, BANDS, [(0, load), (1, regroup), (3, store)])
            for h in range(HALVES):
                sp.wait_ge(stored[h], 16 * BANDS)

        @block.scalar
        def _(act):
            a = nc.scalar
            act.wait_ge(ready, 32)

            def squares(r):
                for h in range(HALVES):
                    wait_past(act, summed1, 2 * (r - 1) + h + 1)
                    if first:
                        act.wait_ge(normed, 2 * r + h + 1)
                        a.activation(sq[:, h, :], xn[:, h, :], ACT.Square).then_inc(squared, 1)
                    else:
                        act.wait_ge(loaded[h], 48 * r + 48)
                        wait_past(act, u_ready, (2 * (r - 1) + h + 1) * CHUNKS1)
                        src = xt[:, h].rearrange("p r w -> p (r w)")
                        a.activation(xn[:, h, :], src, ACT.Relu, bias=bias, scale=scale).then_inc(normed, 1)
                        a.activation(sq[:, h, :], src, ACT.Square, bias=bias, scale=scale).then_inc(squared, 1)

            def logarithms(r):
                act.wait_ge(normsq, r + 1)
                a.activation(l1[:], nc_[:], ACT.Ln, bias=1.0, scale=1.0)
                a.activation(l2[:], nc_[:], ACT.Ln, bias=1.0, scale=-1.0).then_inc(logs, 1)

            def evacuate(r):
                for h in range(HALVES):
                    wait_past(act, out_ready, (2 * (r - 1) + h + 1) * CHUNKS2)
                    wait_past(act, summed2, 2 * (r - 1) + h + 1)
                    for k in range(4):
                        p, o = k // 2, k % 2
                        act.wait_ge(conv_ready, (2 * r + h) * 4 + k + 1)
                        src = conv[:, k % 2, :].rearrange("p (i w) -> p i w", i=2)
                        rows = slice(4 * p + o, 4 * p + o + 3, 2)
                        a.activation(v_sb[:, h, rows, :], src, ACT.Identity, bias=cb[:, 0:1])
                        a.activation(sqv[:, h, :].rearrange("p (r w) -> p r w", w=COLS)[:, rows, :], src, ACT.Square,
                                     bias=cb[:, 0:1]).then_inc(evacuated, 1)
            if first:
                pipeline(act, BANDS, [(0, squares), (0, logarithms), (1, evacuate)])
            else:
                pipeline(act, BANDS, [(0, squares), (1, evacuate)])

        @block.tensor
        def _(pe):
            m = nc.tensor
            pe.wait_ge(ready, 32)

            def sum_squares(r):
                wait_past(pe, read2, r - 1)
                for h in range(HALVES):
                    pe.wait_ge(squared, 2 * r + h + 1)
                    for k in range(HB):
                        last = m.matmul(pc1[:, h, GROUP * k:GROUP * k + GROUP], sq[:, h, P * k:P * k + P],
                                        c["ones4"][:], start=True, stop=True)
                    last.then_inc(summed1, 1)

            def spread_out(r):
                pe.wait_ge(turned2_copied, r + 1)
                for h in range(HALVES):
                    for k in range(CHUNKS2):
                        n = (2 * r + h) * CHUNKS2 + k
                        wait_past(pe, out_ready, n - 1)
                        for j in range(4):
                            last = m.matmul(spread2[:, k % 2, P * j:P * j + P], c["sel4"][:, 4 * k + j, :], sp2T[:, h, :],
                                            start=True, stop=True)
                        last.then_inc(spread2_ready, 1)

            def turn_out(r):
                pe.wait_ge(factors2, r + 1)
                for h in range(HALVES):
                    last = m.transpose(turned2[:, h, :], sp2[:, h, :], c["ident"][:])
                last.then_inc(turned2_ready, 1)

            def convolve(r, h):
                pe.wait_ge(uc_loaded[h], (r + 1) * 256)
                for k in range(4):
                    p, o = k // 2, k % 2
                    wait_past(pe, evacuated, (2 * r + h) * 4 + k - 1)
                    for d in range(3):
                        for b in range(GROUP):
                            last = m.matmul(conv[QUAD * b:QUAD * b + QUAD, k % 2, :], w_sb[:, o, d, :],
                                            uc[:, h, b, 2 * p:2 * p + 2, d:d + COLS], start=(d == 0), stop=(d == 2),
                                            tile_position=(0, QUAD * b))
                    last.then_inc(conv_ready, 1)

            def spread_u(r):
                pe.wait_ge(factors1, r + 1)
                wait_past(pe, turned1_copied, r)
                for h in range(HALVES):
                    for g in range(2):
                        last = m.transpose(turned[:, h, g, :], sp1[:, h, g, :], c["ident"][:])
                last.then_inc(turned1_ready, 1)
                pe.wait_ge(turned1_copied, r + 1)
                for h in range(HALVES):
                    for k in range(CHUNKS1):
                        n = (2 * r + h) * CHUNKS1 + k
                        wait_past(pe, u_ready, n - 1)
                        for j in range(4):
                            blk = 4 * k + j
                            last = m.matmul(spread1[:, (h * CHUNKS1 + k) % 2, P * j:P * j + P], c["sel4"][:, blk % HG, :],
                                            spT[:, h, blk // HG, :], start=True, stop=True)
                        last.then_inc(spread1_ready, 1)

            def sum_out(r):
                pe.wait_ge(read1, r + 1)
                for h in range(HALVES):
                    pe.wait_ge(evacuated, (2 * r + h + 1) * 4)
                    for k in range(BLOCKS):
                        last = m.matmul(pc2[:, h, GROUP * k:GROUP * k + GROUP], sqv[:, h, P * k:P * k + P],
                                        c["ones4"][:], start=True, stop=True)
                    last.then_inc(summed2, 1)
            pipeline(pe, BANDS, [(0, sum_squares), (2, turn_out), (2, spread_out), (1, lambda r: convolve(r, 0)),
                                 (0, spread_u), (1, lambda r: convolve(r, 1)), (1, sum_out)])

        @block.vector
        def _(dve):
            v = nc.vector
            v.memset(u[:, :, :, 0:1], 0.0)
            v.memset(u[:, :, :, PAD - 1:PAD], 0.0)
            v.memset(sp1[:], 0.0)
            v.memset(top[:], 1.0)
            v.memset(bot[:], 1.0)
            v.drain()
            v.memset(top[:, 0:1], 0.0)
            v.memset(bot[:, BANDS - 1:BANDS], 0.0)
            v.drain()

            def affine(r):
                for h in range(HALVES):
                    dve.wait_ge(loaded[h], 48 * r + 48)
                    wait_past(dve, squared, 2 * (r - 1) + h + 1)
                    wait_past(dve, u_ready, (2 * (r - 1) + h + 1) * CHUNKS1)
                    v.tensor_scalar(xn[:, h, :], xt[:, h].rearrange("p r w -> p (r w)"), scale[:, h:h + 1],
                                    bias[:, h:h + 1], ALU.mult, ALU.add).then_inc(normed, 1)

            def factors_u(r):
                dve.wait_ge(summed1, 2 * r + 2)
                v.tensor_copy(n2[:], pc1).then_inc(read1, 1)
                v.drain()
                v.tensor_scalar(q[:], n2[:], EPS_NORM * EPS_NORM, None, ALU.max)
                v.drain()
                rsqrt_steps(v, rn[:], q[:], t_[:])
                if first:
                    v.tensor_tensor(nc_[:], q[:], rn[:], ALU.mult)
                    v.drain()
                    v.tensor_scalar(nc_[:], nc_[:], CLIP, None, ALU.min).then_inc(normsq, 1)
                    v.tensor_scalar(xx[:], q[:], 0.05, None, ALU.min)
                    v.drain()
                    v.tensor_scalar(pl[:], xx[:], 1.0 / 11, None, ALU.mult)
                    for k in (9, 7, 5, 3):
                        v.drain()
                        v.scalar_tensor_tensor(pl[:], pl[:], 1.0 / k, xx[:], ALU.add, ALU.mult)
                    dve.wait_ge(logs, r + 1)
                    v.tensor_tensor(sl[:], l1[:], l2[:], ALU.subtract)
                    v.drain()
                    v.scalar_tensor_tensor(sl[:], sl[:], 0.5, rn[:], ALU.mult, ALU.mult)
                    v.tensor_scalar(t_[:], q[:], 0.04, None, ALU.is_lt)
                    v.drain()
                    v.scalar_tensor_tensor(pl[:], pl[:], 1.0, sl[:], ALU.add, ALU.subtract)
                    v.drain()
                    v.tensor_tensor(pl[:], pl[:], t_[:], ALU.mult)
                    v.drain()
                    v.tensor_tensor(sl[:], sl[:], pl[:], ALU.add)
                else:
                    v.tensor_scalar(sl[:], rn[:], ATANH_MAX, 1.0, ALU.mult, ALU.min).then_inc(normsq, 1)
                v.drain()
                edge = 2 * GROUP
                v.tensor_scalar(sl[:, :, 0:edge], sl[:, :, 0:edge], top[:, bass.ds(r, 1)], None, ALU.mult)
                v.tensor_scalar(sl[:, :, NC1 - edge:], sl[:, :, NC1 - edge:], bot[:, bass.ds(r, 1)], None, ALU.mult)
                v.drain()
                wait_past(dve, turned1_ready, r)
                half = sl[:].rearrange("p h (g n) -> p h g n", g=2)
                split_hi_lo(v, sp1[:, :, :, 0:HG * GROUP], sp1[:, :, :, P // 2:P // 2 + HG * GROUP], half).then_inc(factors1, 1)

            def products_out(r):
                dve.wait_ge(turned2_ready, r + 1)
                wait_past(dve, spread2_ready, 2 * r * CHUNKS2)
                v.tensor_copy(sp2T[:], turned2).then_inc(turned2_copied, 1)
                for h in range(HALVES):
                    wait_past(dve, stored[h], 16 * r)
                    for k in range(CHUNKS2):
                        dve.wait_ge(spread2_ready, (2 * r + h) * CHUNKS2 + k + 1)
                        cols = slice(BANK * k, BANK * k + BANK)
                        v.tensor_tensor(out[:, h, cols], v_sb[:, h].rearrange("p r w -> p (r w)")[:, cols],
                                        spread2[:, k % 2, :], ALU.mult).then_inc(out_ready, 1)
                    v.drain()
                    for k in range(CHUNKS2):
                        v.bn_stats(part[:, h, 6 * k:6 * k + 6], out[:, h, BANK * k:BANK * k + BANK])
                    v.drain()
                    v.tensor_copy(stats[:, h, r, :], part[:, h, :])

            def products_u(r):
                dve.wait_ge(turned1_ready, r + 1)
                wait_past(dve, spread1_ready, 2 * r * CHUNKS1)
                v.tensor_copy(spT[:], turned[:]).then_inc(turned1_copied, 1)
                for h in range(HALVES):
                    wait_past(dve, uc_loaded[h], 256 * r)
                    if not first:
                        dve.wait_ge(normed, 2 * r + h + 1)
                    for k in range(CHUNKS1):
                        dve.wait_ge(spread1_ready, (2 * r + h) * CHUNKS1 + k + 1)
                        v.tensor_tensor(u[:, h, 2 * k:2 * k + 2, 1:COLS + 1],
                                        xn[:, h, BANK * k:BANK * k + BANK].rearrange("p (r w) -> p r w", w=COLS),
                                        spread1[:, (h * CHUNKS1 + k) % 2, :].rearrange("p (r w) -> p r w", w=COLS),
                                        ALU.mult).then_inc(u_ready, 1)

            def factors_out(r):
                dve.wait_ge(summed2, 2 * r + 2)
                s, q2, y2, t2 = m2[:], q[:, :, 0:NC2], rn[:, :, 0:NC2], t_[:, :, 0:NC2]
                v.tensor_scalar(q2, pc2, EPS_NORM * EPS_NORM, None, ALU.max).then_inc(read2, 1)
                v.drain()
                rsqrt_steps(v, y2, q2, t2)
                v.tensor_scalar(s, y2, ATANH_MAX, 1.0, ALU.mult, ALU.min)
                v.drain()
                wait_past(dve, turned2_ready, r)
                split_hi_lo(v, sp2[:, :, 0:NC2], sp2[:, :, P // 2:], s).then_inc(factors2, 1)
            stages = [(0, factors_u), (2, products_out), (0, products_u), (1, factors_out)]
            pipeline(dve, BANDS, ([(0, affine)] if first else []) + stages)


def residual_layer(net, x_rows, source, scale, bias, target, stats):
    nc, c = net.nc, net.c
    NC = BLOCKS * GROUP
    CHUNKS = TILE // BANK
    with ExitStack() as local:
        def sb(name, shape, dt=F32):
            return net.sb(local, name, shape, dt)
        tt, xt, r_sb, sqh, sqr, o_sb, x1 = (sb(k, [P, HALVES, TILE]) for k in ("tt", "xt", "r", "sqh", "sqr", "o", "x1"))
        nh, nr, y, t_, m, n, th = (sb(k, [P, HALVES, NC]) for k in ("nh", "nr", "y", "t", "m", "n", "th"))
        parts = sb("parts", [P, HALVES, P])
        partsT = sb("partsT", [P, HALVES, P], F32R)
        part = sb("part", [P, HALVES, CHUNKS * 6])
        sums = net.ps(local, "sums", [P, 2, HALVES, NC])
        turned = net.ps(local, "turned", [P, HALVES, P])
        spread = net.ps(local, "spread", [P, 2, BANK])

        def sem(name):
            return net.sem(local, name)
        loaded, x_loaded, stored = ([sem(f"{k}{h}") for h in range(2)] for k in ("loaded", "x_loaded", "stored"))
        rectified, squared, summed, read, norms, tanhs, factors, turned_ready, copied, spread_ready, o_ready, x1_ready, measured = (
            sem(k) for k in ("rectified", "squared", "summed", "read", "norms", "tanhs", "factors", "turned_ready",
                             "copied", "spread_ready", "o_ready", "x1_ready", "measured"))
        block = local.enter_context(nc.Block())

        @block.sync
        def _(sp):
            def load(r):
                for h in range(HALVES):
                    wait_past(sp, squared, 2 * (r - 1) + h + 1)
                    sp.dma_start(tt[:, h, :], source[r, h]).then_inc(loaded[h], 16)

            def load_x(r):
                for h in range(HALVES):
                    wait_past(sp, x1_ready, 2 * (r - 1) + h + 1)
                    bands = x_rows[P * h:P * h + P, :].rearrange("p (t n) -> p t n", n=TILE)
                    sp.dma_start(xt[:, h, :], bands[:, r, :]).then_inc(x_loaded[h], 16)

            def store(r):
                for h in range(HALVES):
                    sp.wait_ge(x1_ready, 2 * r + h + 1)
                    sp.dma_start(target[r, h], x1[:, h, :]).then_inc(stored[h], 16)
            pipeline(sp, BANDS, [(0, load), (1, load_x), (2, store)])
            for h in range(HALVES):
                sp.wait_ge(stored[h], 16 * BANDS)

        @block.scalar
        def _(act):
            a = nc.scalar

            def squares(r):
                for h in range(HALVES):
                    act.wait_ge(loaded[h], 16 * r + 16)
                    wait_past(act, o_ready, (2 * (r - 1) + h + 1) * CHUNKS)
                    wait_past(act, squared, 2 * (r - 1) + h + 1)
                    a.activation(r_sb[:, h, :], tt[:, h, :], ACT.Relu, bias=bias, scale=scale).then_inc(rectified, 1)
                for h in range(HALVES):
                    wait_past(act, summed, 2 * (r - 1) + h + 1)
                    a.activation(sqh[:, h, :], tt[:, h, :], ACT.Square, bias=bias, scale=scale)
                    act.wait_ge(rectified, 2 * r + h + 1)
                    a.activation(sqr[:, h, :], r_sb[:, h, :], ACT.Square).then_inc(squared, 1)

            def tangents(r):
                act.wait_ge(norms, r + 1)
                a.activation(th[:], n[:], ACT.Tanh).then_inc(tanhs, 1)
            pipeline(act, BANDS, [(0, squares), (0, tangents)])

        @block.tensor
        def _(pe):
            mm = nc.tensor

            def sum_squares(r):
                wait_past(pe, read, r)
                for h in range(HALVES):
                    pe.wait_ge(squared, 2 * r + h + 1)
                    for kind, src in enumerate((sqh, sqr)):
                        for k in range(BLOCKS):
                            last = mm.matmul(sums[:, kind, h, GROUP * k:GROUP * k + GROUP], src[:, h, P * k:P * k + P],
                                             c["ones4"][:], start=True, stop=True)
                    last.then_inc(summed, 1)

            def spread_factors(r):
                pe.wait_ge(factors, r + 1)
                for h in range(HALVES):
                    last = mm.transpose(turned[:, h, :], parts[:, h, :], c["ident"][:])
                last.then_inc(turned_ready, 1)
                pe.wait_ge(copied, r + 1)
                for h in range(HALVES):
                    for k in range(CHUNKS):
                        wait_past(pe, o_ready, (2 * r + h) * CHUNKS + k - 1)
                        for j in range(4):
                            last = mm.matmul(spread[:, k % 2, P * j:P * j + P], c["sel4"][:, 4 * k + j, :], partsT[:, h, :],
                                             start=True, stop=True)
                        last.then_inc(spread_ready, 1)
            pipeline(pe, BANDS, [(1, spread_factors), (0, sum_squares)])

        @block.gpsimd
        def _(pool):
            def add(r):
                for h in range(HALVES):
                    pool.wait_ge(o_ready, (2 * r + h + 1) * CHUNKS)
                    pool.wait_ge(x_loaded[h], 16 * r + 16)
                    wait_past(pool, stored[h], 16 * r)
                    wait_past(pool, measured, 2 * (r - 1) + h + 1)
                    nc.gpsimd.tensor_tensor(x1[:, h, :], o_sb[:, h, :], xt[:, h, :], ALU.add).then_inc(x1_ready, 1)
            pipeline(pool, BANDS, [(0, add)])

        @block.vector
        def _(dve):
            v = nc.vector
            v.memset(parts[:], 0.0)
            v.drain()

            def products(r):
                dve.wait_ge(turned_ready, r + 1)
                wait_past(dve, spread_ready, 2 * r * CHUNKS)
                v.tensor_copy(partsT[:], turned[:]).then_inc(copied, 1)
                for h in range(HALVES):
                    wait_past(dve, x1_ready, 2 * (r - 1) + h + 1)
                    for k in range(CHUNKS):
                        cols = slice(BANK * k, BANK * k + BANK)
                        dve.wait_ge(spread_ready, (2 * r + h) * CHUNKS + k + 1)
                        v.tensor_tensor(o_sb[:, h, cols], r_sb[:, h, cols], spread[:, k % 2, :], ALU.mult).then_inc(o_ready, 1)

            def factor(r):
                dve.wait_ge(summed, 2 * r + 2)
                v.tensor_scalar(nh[:], sums[:, 0], EPS_NORM * EPS_NORM, None, ALU.max)
                v.tensor_scalar(nr[:], sums[:, 1], 1e-30, None, ALU.max).then_inc(read, 1)
                v.drain()
                rsqrt_steps(v, y[:], nh[:], t_[:])
                v.tensor_scalar(m[:], y[:], ATANH_MAX, 1.0, ALU.mult, ALU.min)
                v.drain()
                rsqrt_steps(v, y[:], nr[:], t_[:])
                v.tensor_tensor(nr[:], nr[:], y[:], ALU.mult)
                v.drain()
                v.tensor_tensor(nr[:], nr[:], m[:], ALU.mult)
                v.drain()
                v.tensor_scalar(n[:], nr[:], EPS_NORM, None, ALU.max).then_inc(norms, 1)
                v.drain()
                v.reciprocal(y[:], n[:])
                v.drain()
                v.tensor_tensor(m[:], m[:], y[:], ALU.mult)
                v.drain()
                dve.wait_ge(tanhs, r + 1)
                v.scalar_tensor_tensor(m[:], th[:], MAX_NORM, m[:], ALU.min, ALU.mult)
                v.drain()
                wait_past(dve, turned_ready, r)
                split_hi_lo(v, parts[:, :, 0:NC], parts[:, :, P // 2:], m[:]).then_inc(factors, 1)

            def measure(r):
                for h in range(HALVES):
                    dve.wait_ge(x1_ready, 2 * r + h + 1)
                    for k in range(CHUNKS):
                        last = v.bn_stats(part[:, h, 6 * k:6 * k + 6], x1[:, h, BANK * k:BANK * k + BANK])
                    last.then_inc(measured, 1)
                    v.drain()
                    v.tensor_copy(stats[:, h, r, :], part[:, h, :])
            pipeline(dve, BANDS, [(1, products), (0, factor), (2, measure)])


MODES = 4
KP = CH * MODES
SUB = ROWS // 2


def spread_table(net, vectors, table):
    nc = net.nc
    with ExitStack() as local:
        wide = net.sb(local, "wide", [P, HALVES, P])
        rows = net.ps(local, "rows", [P, HALVES, P])
        ready, done = net.sem(local, "wide_ready"), net.sem(local, "rows_ready")
        block = local.enter_context(nc.Block())

        @block.vector
        def _(dve):
            nc.vector.tensor_copy(wide[:], vectors.unsqueeze(2).to_broadcast([P, HALVES, P])).then_inc(ready, 1)
            dve.wait_ge(done, 1)
            nc.vector.tensor_copy(table.rearrange("p (h n) -> p h n", h=HALVES), rows[:])

        @block.tensor
        def _(pe):
            pe.wait_ge(ready, 1)
            for h in range(HALVES):
                last = nc.tensor.matmul(rows[:, h, :], wide[:, h, :], net.c["ident"][:], start=True, stop=True)
            last.then_inc(done, 1)


def pole_kernels(net, g1, g2):
    nc, ins = net.nc, net.ins
    N = CH * KP
    with ExitStack() as local:
        wr, wi, den, re, im = (net.sb(local, k, [P, N]) for k in ("wr", "wi", "den", "re", "im"))
        dft = net.sb(local, "dft", [P, 3, P])
        grid, lam = net.sb(local, "grid", [P, 2, 3]), net.sb(local, "lam", [P, 2])
        freq = net.sb(local, "freq", [P, 1])
        acc = net.ps(local, "acc", [P, 2, 2, BANK])
        consts, poles, inverse, transformed, kept = (net.sem(local, k) for k in
                                                     ("consts", "poles", "inverse", "transformed", "kept"))
        block = local.enter_context(nc.Block())
        CHUNKS = N // BANK
        PER = BANK // KP

        @block.sync
        def _(sp):
            sp.dma_start(dft[:], ins["c_dft"]).then_inc(consts, 16)
            sp.dma_start(freq[:], ins["c_freq"]).then_inc(consts, 16)
            for n, name in enumerate(("x_grid", "t_grid")):
                sp.dma_start(grid[:, n, :], ins[name][:, 0:3].to_broadcast([P, 3])).then_inc(consts, 16)
            for n, name in enumerate(("wp1", "wp2")):
                wait_past(sp, inverse, n)
                sp.dma_start(wr[:], ins[name + "r"].to_broadcast([P, N])).then_inc(poles, 16)
                sp.dma_start(wi[:], ins[name + "i"].to_broadcast([P, N])).then_inc(poles, 16)

        @block.vector
        def _(dve):
            v = nc.vector
            dve.wait_ge(consts, 64)
            v.tensor_tensor(lam[:], grid[:, :, 2], grid[:, :, 0], ALU.subtract)
            v.drain()
            v.reciprocal(lam[:], lam[:])
            v.drain()
            v.tensor_scalar(lam[:], lam[:], freq[:, 0:1], 2.0 * np.pi, ALU.mult, ALU.mult)
            v.drain()
            for n in range(2):
                dve.wait_ge(poles, 32 * n + 32)
                wait_past(dve, transformed, n * CHUNKS)
                v.tensor_scalar(wi[:], wi[:], lam[:, n:n + 1], None, ALU.subtract)
                v.tensor_tensor(re[:], wr[:], wr[:], ALU.mult)
                v.drain()
                v.tensor_tensor(den[:], wi[:], wi[:], ALU.mult)
                v.drain()
                v.tensor_tensor(den[:], den[:], re[:], ALU.add)
                v.drain()
                v.reciprocal(den[:], den[:])
                v.drain()
                v.tensor_tensor(re[:], wr[:], den[:], ALU.mult)
                v.scalar_tensor_tensor(im[:], wi[:], -1.0, den[:], ALU.mult, ALU.mult).then_inc(inverse, 1)
                v.drain()

        @block.tensor
        def _(pe):
            m = nc.tensor
            for n in range(2):
                pe.wait_ge(inverse, n + 1)
                for k in range(CHUNKS):
                    wait_past(pe, kept, n * CHUNKS + k - 1)
                    cols = slice(BANK * k, BANK * k + BANK)
                    m.matmul(acc[:, k % 2, 0, :], dft[:, 0, :], re[:, cols], start=True, stop=False)
                    m.matmul(acc[:, k % 2, 0, :], dft[:, 1, :], im[:, cols], start=False, stop=True)
                    m.matmul(acc[:, k % 2, 1, :], dft[:, 0, :], im[:, cols], start=True, stop=False)
                    m.matmul(acc[:, k % 2, 1, :], dft[:, 2, :], re[:, cols], start=False, stop=True).then_inc(transformed, 1)

        @block.scalar
        def _(act):
            a = nc.scalar
            for n in range(2):
                for k in range(CHUNKS):
                    act.wait_ge(transformed, n * CHUNKS + k + 1)
                    i = slice(PER * k, PER * k + PER)
                    real, imag = (acc[:, k % 2, z, :].rearrange("p (i m) -> p i m", m=KP) for z in range(2))
                    if n == 0:
                        a.copy(g1[:, i, 0, :], real)
                        a.copy(g1[:, i, 1, :], imag).then_inc(kept, 1)
                    else:
                        a.mul(g2[:, i, 0, :], imag, -1.0)
                        a.copy(g2[:, i, 1, :], real)
                        a.copy(g2[:, i, 2, :], imag).then_inc(kept, 1)


def residues(net, source, scale_table, bias_table, g1, g2, coef):
    nc, ins = net.nc, net.ins
    with ExitStack() as local:
        rows = net.sb(local, "rows", [P, 2, IMAGES, COLS])
        xs = net.sb(local, "xs", [P, IMAGES, SUB])
        t_sb = net.sb(local, "t_sb", [P, IMAGES, 2, KP])
        res = net.sb(local, "res", [P, CH, 2, MODES])
        prod = net.sb(local, "prod", [P, 4, 2, 2, 2, KP])
        acc = net.sb(local, "acc", [P, 4, 2, 2, 2, KP])
        mask = net.sb(local, "mask", [P, KP])
        t_ps = net.ps(local, "t_ps", [P, 2, 2, 2, KP])
        o_ps = net.ps(local, "o_ps", [P, 4, 2, 2, KP])
        consts, t_ready, t_kept, o_ready, weighted, added, sampled = (net.sem(local, k) for k in (
            "consts", "t_ready", "t_kept", "o_ready", "weighted", "added", "sampled"))
        cleared = net.sem(local, "cleared")
        loaded = [net.sem(local, f"loaded{j}") for j in range(2)]
        block = local.enter_context(nc.Block())
        PAIRS = CH // 2

        @block.sync
        def _(sp):
            sp.dma_start(res[:], ins["res"]).then_inc(consts, 16)
            sp.dma_start(mask[:], ins["c_mask"]).then_inc(consts, 16)

            def load(t):
                for j in range(2):
                    wait_past(sp, sampled, (2 * (t - 1) + j + 1))
                    for b in range(IMAGES):
                        src = source[:, b // GROUP, CH * (b % GROUP) + 2 * t + j, :]
                        src = src.rearrange("r (y z w) -> r y z w", z=2, w=COLS)[:, :, 0, :]
                        sp.dma_start(rows[:, j, b, :], src).then_inc(loaded[j], 16)
            pipeline(sp, PAIRS, [(0, load)])

        @block.vector
        def _(dve):
            v = nc.vector

            def sample(t, j):
                dve.wait_ge(loaded[j], 128 * t + 128)
                wait_past(dve, t_ready, 4 * (2 * t + j))
                for b in range(IMAGES):
                    col = b * CH + 2 * t + j
                    last = v.tensor_scalar(xs[:, b, :], rows[:, j, b, :].rearrange("p (x z) -> p x z", z=2)[:, :, 0],
                                           scale_table[:, bass.ds(col, 1)], bias_table[:, bass.ds(col, 1)], ALU.mult, ALU.add)
                last.then_inc(sampled, 1)

            def weight(t, j):
                i = 2 * t + j
                for b in range(4):
                    dve.wait_ge(o_ready, 4 * i + b + 1)
                    wait_past(dve, added, 4 * (i - 1) + b + 1)
                    for z in range(2):
                        last = v.tensor_tensor(prod[:, b, z].rearrange("p c z (k q) -> p (c z) k q", q=MODES),
                                               o_ps[:, b].rearrange("p c z (k q) -> p (c z) k q", q=MODES),
                                               res[:, i, z, :].unsqueeze(1).unsqueeze(1).to_broadcast([P, 4, CH, MODES]),
                                               ALU.mult)
                    last.then_inc(weighted, 1)
            dve.wait_ge(consts, 32)

            def both(t):
                sample(t, 0)
                weight(t, 0)
                sample(t, 1)
                weight(t, 1)
            v.memset(acc[:], 0.0).then_inc(cleared, 1)
            pipeline(dve, PAIRS, [(0, both)])
            dve.wait_ge(added, 4 * CH)
            for b in range(4):
                re, im = coef[:, 2 * b:2 * b + 2, 0, :], coef[:, 2 * b:2 * b + 2, 1, :]
                v.tensor_tensor(re, acc[:, b, 0, :, 0, :], acc[:, b, 1, :, 1, :], ALU.subtract)
                v.tensor_tensor(im, acc[:, b, 0, :, 1, :], acc[:, b, 1, :, 0, :], ALU.add)
            v.drain()
            flat = coef.rearrange("p a z n -> p (a z) n")
            v.tensor_tensor(flat, flat, mask[:].unsqueeze(1).to_broadcast([P, 2 * IMAGES, KP]), ALU.mult)
            v.drain()

        @block.gpsimd
        def _(pool):
            pool.wait_ge(cleared, 1)

            def add(t):
                for j in range(2):
                    i = 2 * t + j
                    for b in range(4):
                        pool.wait_ge(weighted, 4 * i + b + 1)
                        wait_past(pool, added, 4 * (i - 1) + b + 1)
                        dst = acc[:, b].rearrange("p z c y n -> p (z c y n)")
                        nc.gpsimd.tensor_tensor(dst, dst, prod[:, b].rearrange("p z c y n -> p (z c y n)"),
                                                ALU.add).then_inc(added, 1)
            pipeline(pool, PAIRS, [(0, add)])

        @block.scalar
        def _(act):
            def keep(t):
                for j in range(2):
                    i = 2 * t + j
                    for b in range(4):
                        act.wait_ge(t_ready, 4 * i + b + 1)
                        wait_past(act, o_ready, 4 * (i - 1) + b + 1)
                        nc.scalar.copy(t_sb[:, 2 * b:2 * b + 2], t_ps[:, b % 2]).then_inc(t_kept, 1)
            pipeline(act, PAIRS, [(0, keep)])

        @block.tensor
        def _(pe):
            m = nc.tensor

            def first(t, j):
                i = 2 * t + j
                pe.wait_ge(sampled, i + 1)
                for b in range(4):
                    wait_past(pe, t_kept, 4 * i + b - 1)
                    for k in range(2):
                        last = m.matmul(t_ps[:, b % 2, k].rearrange("p z n -> p (z n)"), xs[:, 2 * b + k, :],
                                        g1[:, i].rearrange("p z n -> p (z n)"), start=True, stop=True)
                    last.then_inc(t_ready, 1)

            def second(t, j):
                i = 2 * t + j
                for b in range(4):
                    pe.wait_ge(t_kept, 4 * i + b + 1)
                    wait_past(pe, weighted, 4 * (i - 1) + b + 1)
                    for k in range(2):
                        dst = o_ps[:, b, k].rearrange("p z n -> p (z n)")
                        m.matmul(dst, t_sb[:, 2 * b + k, 0, :], g2[:, i, 1:3].rearrange("p z n -> p (z n)"),
                                 start=True, stop=False)
                        last = m.matmul(dst, t_sb[:, 2 * b + k, 1, :], g2[:, i, 0:2].rearrange("p z n -> p (z n)"),
                                        start=False, stop=True)
                    last.then_inc(o_ready, 1)

            def both(t):
                first(t, 0)
                second(t, 0)
                first(t, 1)
                second(t, 1)
            pipeline(pe, PAIRS, [(0, both)])


TWO_PI_1 = 6.28125
TWO_PI_2 = float(np.float32(np.round((2 * np.pi - TWO_PI_1) * 2 ** 21) / 2 ** 21))
TWO_PI_3 = float(2 * np.pi - TWO_PI_1 - TWO_PI_2)
ROUND = 1.5 * 2 ** 23
PI_BELOW = 3.1415925


def evaluate_residues(net, source, coef, target, stats):
    nc, ins = net.nc, net.ins
    with ExitStack() as local:
        w = net.sb(local, "w", [P, 2, 2, CH])
        z = net.sb(local, "z", [P, 2, COLS])
        grow, ang, turns, sine, cosine = (net.sb(local, k, [P, 2, COLS]) for k in ("grow", "ang", "turns", "sin", "cos"))
        e1, e2 = net.sb(local, "e1", [P, 2, 3, COLS]), net.sb(local, "e2", [P, 2, 2, COLS])
        tmp = net.sb(local, "tmp", [P, 2, 2, COLS])
        xin, xout = net.sb(local, "xin", [P, 2, IMAGES, BANK]), net.sb(local, "xout", [P, 2, IMAGES, BANK])
        part = net.sb(local, "part", [P, IMAGES * 6])
        half_pi = net.sb(local, "half_pi", [P, 1])
        t_ps, o_ps = net.ps(local, "t_ps", [P, 2, BANK]), net.ps(local, "o_ps", [P, 2, BANK])
        consts, angles, sines, grown, waves, t_ready, t_kept, o_ready, summed, measured = (net.sem(local, k) for k in (
            "consts", "angles", "sines", "grown", "waves", "t_ready", "t_kept", "o_ready", "summed", "measured"))
        loaded = [net.sem(local, f"loaded{j}") for j in range(2)]
        stored = [net.sem(local, f"stored{j}") for j in range(2)]
        block = local.enter_context(nc.Block())
        PAIRS = CH // 2

        def rows_of(tensor, a, i):
            return tensor[:, a // GROUP, CH * (a % GROUP) + i, :].rearrange("r (z n) -> r z n", n=2 * COLS)

        @block.sync
        def _(sp):
            sp.dma_start(w[:], ins["poles"]).then_inc(consts, 16)
            sp.dma_start(z[:, 0, :], ins["x_grid"].to_broadcast([P, COLS])).then_inc(consts, 16)
            sp.dma_start(z[:, 1, :], ins["t_grid"].to_broadcast([P, COLS])).then_inc(consts, 16)

            def load(t):
                for j in range(2):
                    wait_past(sp, summed, IMAGES * (2 * (t - 1) + j + 1))
                    for a in range(IMAGES):
                        sp.dma_start(xin[:, j, a, :], rows_of(source, a, 2 * t + j)).then_inc(loaded[j], 16)

            def store(t):
                for j in range(2):
                    for a in range(IMAGES):
                        sp.wait_ge(summed, IMAGES * (2 * t + j) + a + 1)
                        sp.dma_start(rows_of(target, a, 2 * t + j), xout[:, j, a, :]).then_inc(stored[j], 16)
            pipeline(sp, PAIRS, [(0, load), (1, store)])
            for j in range(2):
                sp.wait_ge(stored[j], 16 * IMAGES * PAIRS)

        @block.scalar
        def _(act):
            s = nc.scalar
            act.wait_ge(consts, 48)

            def exponentials(t, j):
                i = 2 * t + j
                wait_past(act, waves, i)
                for n in range(2):
                    last = s.activation(grow[:, n, :], z[:, n, :], ACT.Exp, scale=w[:, n, 0, bass.ds(i, 1)])
                last.then_inc(grown, 1)
                act.wait_ge(angles, i + 1)
                s.activation(sine[:], ang[:], ACT.Sin)
                s.activation(cosine[:], turns[:], ACT.Sin, bias=half_pi[:, 0:1], scale=-1.0).then_inc(sines, 1)

            def keep(t, j):
                for a in range(IMAGES):
                    n = IMAGES * (2 * t + j) + a
                    act.wait_ge(t_ready, n + 1)
                    wait_past(act, o_ready, n - 1)
                    s.copy(tmp[:, a % 2].rearrange("p z n -> p (z n)"), t_ps[:, a % 2, :]).then_inc(t_kept, 1)
            pipeline(act, PAIRS, [(0, lambda t: exponentials(t, 0)), (1, lambda t: keep(t, 0)),
                                  (0, lambda t: exponentials(t, 1)), (1, lambda t: keep(t, 1))])

        @block.vector
        def _(dve):
            v = nc.vector
            v.memset(half_pi[:], 0.5 * np.pi)
            v.drain()
            dve.wait_ge(consts, 48)

            def prepare(t, j):
                i = 2 * t + j
                wait_past(dve, sines, i)
                for n in range(2):
                    v.tensor_scalar(ang[:, n, :], z[:, n, :], w[:, n, 1, bass.ds(i, 1)], None, ALU.mult)
                v.drain()
                v.tensor_scalar(turns[:], ang[:], float(1 / (2 * np.pi)), ROUND, ALU.mult, ALU.add)
                v.drain()
                v.tensor_scalar(turns[:], turns[:], ROUND, None, ALU.subtract)
                for c in (TWO_PI_1, TWO_PI_2, TWO_PI_3):
                    v.drain()
                    v.scalar_tensor_tensor(ang[:], turns[:], -c, ang[:], ALU.mult, ALU.add)
                v.drain()
                v.tensor_scalar(ang[:], ang[:], PI_BELOW, -PI_BELOW, ALU.min, ALU.max)
                v.drain()
                v.scalar_tensor_tensor(turns[:], ang[:], -1.0, ang[:], ALU.mult, ALU.max).then_inc(angles, 1)

            def combine(t, j):
                i = 2 * t + j
                dve.wait_ge(sines, i + 1)
                dve.wait_ge(grown, i + 1)
                wait_past(dve, o_ready, IMAGES * (i - 1))
                v.tensor_tensor(e1[:, j, 1, :], grow[:, 0, :], cosine[:, 0, :], ALU.mult)
                v.tensor_tensor(e1[:, j, 2, :], grow[:, 0, :], sine[:, 0, :], ALU.mult)
                v.scalar_tensor_tensor(e1[:, j, 0, :], grow[:, 0, :], -1.0, sine[:, 0, :], ALU.mult, ALU.mult)
                v.tensor_tensor(e2[:, j, 0, :], grow[:, 1, :], cosine[:, 1, :], ALU.mult)
                v.scalar_tensor_tensor(e2[:, j, 1, :], grow[:, 1, :], -1.0, sine[:, 1, :], ALU.mult, ALU.mult).then_inc(waves, 1)

            def add(t, j):
                dve.wait_ge(loaded[j], 16 * IMAGES * (t + 1))
                wait_past(dve, stored[j], 16 * IMAGES * t)
                for a in range(IMAGES):
                    dve.wait_ge(o_ready, IMAGES * (2 * t + j) + a + 1)
                    v.scalar_tensor_tensor(xout[:, j, a, :], o_ps[:, a % 2, :], 1.0 / (SUB * SUB), xin[:, j, a, :],
                                           ALU.mult, ALU.add).then_inc(summed, 1)
                v.drain()
                for a in range(IMAGES):
                    v.bn_stats(part[:, 6 * a:6 * a + 6], xout[:, j, a, :])
                v.drain()
                v.tensor_copy(stats[:, 2 * t + j, :], part[:])
                v.drain()
            pipeline(dve, PAIRS, [(0, lambda t: prepare(t, 0)), (1, lambda t: add(t, 0)), (0, lambda t: combine(t, 0)),
                                  (0, lambda t: prepare(t, 1)), (1, lambda t: add(t, 1)), (0, lambda t: combine(t, 1))])

        @block.tensor
        def _(pe):
            m = nc.tensor

            def contract(t, j):
                i = 2 * t + j
                pe.wait_ge(waves, i + 1)

                def modes(a):
                    n = IMAGES * i + a
                    wait_past(pe, t_kept, n - 1)
                    m.matmul(t_ps[:, a % 2, :], coef[:, a, 0, :], e1[:, j, 1:3].rearrange("p z n -> p (z n)"),
                             start=True, stop=False)
                    m.matmul(t_ps[:, a % 2, :], coef[:, a, 1, :], e1[:, j, 0:2].rearrange("p z n -> p (z n)"),
                             start=False, stop=True).then_inc(t_ready, 1)

                def image(a):
                    n = IMAGES * i + a
                    pe.wait_ge(t_kept, n + 1)
                    wait_past(pe, summed, n - 1)
                    for s in range(2):
                        dst = o_ps[:, a % 2, COLS * s:COLS * s + COLS]
                        m.matmul(dst, tmp[:, a % 2, 0, s::2], e2[:, j, 0, :], start=True, stop=False)
                        last = m.matmul(dst, tmp[:, a % 2, 1, s::2], e2[:, j, 1, :], start=False, stop=True)
                    last.then_inc(o_ready, 1)
                modes(0)
                for a in range(IMAGES):
                    if a + 1 < IMAGES:
                        modes(a + 1)
                    image(a)
            pipeline(pe, PAIRS, [(1, lambda t: contract(t, 0)), (1, lambda t: contract(t, 1))])


def norm_vectors_by_image(net, stats, scale, bias):
    nc, c = net.nc, net.c
    N = CH * IMAGES
    GROUPS = CH // 2
    with ExitStack() as local:
        mean, var, d, e, g, y, t = (net.sb(local, k, [P, CH, IMAGES]) for k in ("mean", "var", "d", "e", "g", "y", "t"))
        ones = net.sb(local, "ones", [P, P])
        pick = net.sb(local, "pick", [P, P])
        pm = net.ps(local, "pm", [P, 2, BANK])
        s_mean, s_gm, s_e, s_gv = (net.sem(local, k) for k in ("mean", "gmean", "spread", "gvar"))
        block = local.enter_context(nc.Block())
        flat = lambda a: a[:].rearrange("p i a -> p (i a)")

        @block.tensor
        def _(pe):
            pe.wait_ge(s_mean, 1)
            nc.tensor.matmul(pm[:, 0, 0:N], ones[:], flat(mean), start=True, stop=True).then_inc(s_gm, 1)
            pe.wait_ge(s_e, 1)
            nc.tensor.matmul(pm[:, 1, 0:N], ones[:], flat(e), start=True, stop=True).then_inc(s_gv, 1)

        @block.vector
        def _(dve):
            v = nc.vector
            six = stats.rearrange("p i (a s) -> p i a s", s=6)

            def over_pairs(dst, src):
                s4 = src.rearrange("p (g two a) -> p g two a", two=2, a=IMAGES)
                d4 = dst[:].rearrange("p (g two) a -> p g two a", two=2)
                v.tensor_copy(flat(t), src)
                v.drain()
                t4 = t[:].rearrange("p (g two) a -> p g two a", two=2)
                for k in range(2):
                    v.tensor_tensor(d4[:, :, k, :], t4[:, :, 0, :], t4[:, :, 1, :], ALU.add)
                v.drain()
            v.memset(ones[:], 0.5 / P)
            v.tensor_tensor(mean[:], six[:, :, :, 1], six[:, :, :, 4], ALU.add)
            v.tensor_tensor(d[:], six[:, :, :, 1], six[:, :, :, 4], ALU.subtract)
            v.tensor_tensor(var[:], six[:, :, :, 2], six[:, :, :, 5], ALU.add)
            v.drain()
            v.tensor_scalar(mean[:], mean[:], 0.5, None, ALU.mult).then_inc(s_mean, 1)
            v.tensor_tensor(d[:], d[:], d[:], ALU.mult)
            v.drain()
            v.tensor_scalar(d[:], d[:], 0.25, None, ALU.mult)
            v.drain()
            v.scalar_tensor_tensor(var[:], var[:], 1.0 / BANK, d[:], ALU.mult, ALU.add)
            dve.wait_ge(s_gm, 1)
            over_pairs(g, pm[:, 0, 0:N])
            v.tensor_tensor(e[:], mean[:], g[:], ALU.subtract)
            v.drain()
            v.tensor_tensor(e[:], e[:], e[:], ALU.mult)
            v.drain()
            v.tensor_tensor(e[:], e[:], var[:], ALU.add).then_inc(s_e, 1)
            dve.wait_ge(s_gv, 1)
            over_pairs(d, pm[:, 1, 0:N])
            v.tensor_scalar(d[:], d[:], 1e-5, None, ALU.add)
            v.drain()
            rsqrt_steps(v, flat(y), flat(d), flat(t))
            v.scalar_tensor_tensor(g[:], g[:], -1.0, y[:], ALU.mult, ALU.mult)
            v.drain()
            for src, dst in ((y, scale), (g, bias)):
                for h in range(HALVES):
                    own = src[:, :, GROUP * h:GROUP * h + GROUP].rearrange("p i a -> p a i")
                    v.tensor_tensor(pick[:].rearrange("p (a i) -> p a i", a=GROUP), own,
                                    c["ident"][:].rearrange("p (a i) -> p a i", a=GROUP), ALU.mult)
                    v.drain()
                    v.reduce_sum(dst[:, h:h + 1], pick[:], axis=mybir.AxisListType.X)
                    v.drain()


def kan_constants(net, ctx):
    nc, ins = net.nc, net.ins
    k = {n: net.sb(ctx, n, list(ins[n].shape)) for n in ("kan_vec", "kan_basis", "kan_silu", "c_grid", "c_ones8",
                                                        "c_center")}
    k["sel8"] = net.sb(ctx, "sel8", [P, BLOCKS, P], F32R)
    k["pn_center"] = net.sb(ctx, "pn_center", [P, HALVES, P])
    k["pn_shift"] = net.sb(ctx, "pn_shift", [P, HALVES])
    k["grown"] = net.sb(ctx, "grown", [P, HALVES])
    return k


def prepare_kan(net, k, scale, bias):
    nc, ins = net.nc, net.ins
    with ExitStack() as local:
        staged = net.sb(local, "staged", [P, BLOCKS, P])
        shift = net.ps(local, "shift", [P, HALVES])
        loaded, shifted, done = (net.sem(local, s) for s in ("loaded", "shifted", "done"))
        names = [n for n in k if n in ins]
        block = local.enter_context(nc.Block())

        @block.sync
        def _(sp):
            for n in names:
                sp.dma_start(k[n][:], ins[n]).then_inc(loaded, 16)
            sp.dma_start(staged[:], ins["c_sel8"]).then_inc(loaded, 16)
            sp.wait_ge(loaded, 16 * len(names) + 16)

        @block.tensor
        def _(pe):
            pe.wait_ge(loaded, 16 * len(names) + 16)
            nc.tensor.matmul(shift[:], k["c_center"][:, 0, :], bias, start=True, stop=True).then_inc(shifted, 1)

        @block.vector
        def _(dve):
            v = nc.vector
            dve.wait_ge(loaded, 16 * len(names) + 16)
            v.tensor_copy(k["sel8"][:], staged[:])
            for h in range(HALVES):
                v.tensor_scalar(k["pn_center"][:, h, :], k["c_center"][:, 0, :], scale[:, h:h + 1], None, ALU.mult)
            v.tensor_scalar(k["grown"][:], scale, 1.0, None, ALU.add)
            for n in range(4):
                v.tensor_scalar(k["kan_vec"][:, 2 + 3 * n:4 + 3 * n], k["kan_vec"][:, 2 + 3 * n:4 + 3 * n], 1.75, None, ALU.mult)
            v.tensor_scalar(k["kan_silu"][:], k["kan_silu"][:], 0.5, None, ALU.mult)
            dve.wait_ge(shifted, 1)
            v.tensor_copy(k["pn_shift"][:], shift[:])
            v.drain()


PN, K1, K2, K3, K4 = range(5)


def window_layer(net, k, source, bias, target, stats):
    nc, c = net.nc, net.c
    TILES = BANDS * HALVES
    CHUNKS = TILE // BANK
    RING = 4
    with ExitStack() as local:
        def sb(name, shape, dt=F32):
            return net.sb(local, name, shape, dt)
        X, R = sb("X", [P, TILE]), sb("R", [P, TILE])
        Y, U = sb("Y", [P, 2, TILE]), sb("U", [P, 2, TILE])
        kin, ku = sb("kin", [P, 2, TILE]), sb("ku", [P, 2, TILE])
        back = {K1: sb("back", [P, TILE])[:], K2: kin[:, 1]}
        turned_y = sb("columns_first", [P, 2, TILE])
        sq = sb("sq", [P, TILE])
        srep = sb("srep", [P, CHUNKS, GROUP, BANK])
        ex = sb("ex", [P, RING, GROUP, BANK])
        y = sb("rstd", [P, P])
        hilo = sb("hilo", [P, 2, P])
        hiloT = sb("hiloT", [P, 2, P], F32R)
        part = sb("part", [P, CHUNKS * 6])
        one = sb("one", [P, 1])
        cen, spread, out = (net.ps(local, n, [P, 2, BANK]) for n in ("cen", "spread", "out"))
        var, turned = net.ps(local, "var", [P, BANK]), net.ps(local, "turned", [P, 2, P])
        (centered, squared, var_ready, factors, turned_ready, copied, spread_ready, scaled, normed, args, exps, used,
         evacuated, tanh_ready, u_ready, copied_y, copied_u, summed, x3_ready, measured, regrown, half_sum) = (
            net.sem(local, n) for n in (
                "centered", "squared", "var_ready", "factors", "turned_ready", "copied", "spread_ready", "scaled",
                "normed", "args", "exps", "used", "evacuated", "tanh_ready", "u_ready", "copied_y",
                "copied_u", "summed", "x3_ready", "measured", "regrown", "half_sum"))
        x_loaded, r_loaded, stored = (net.sem(local, n) for n in ("x_loaded", "r_loaded", "stored"))
        kin_loaded = [net.sem(local, f"kin_loaded{j}") for j in range(2)]
        ku_loaded = [net.sem(local, f"ku_loaded{j}") for j in range(2)]
        back_loaded = [net.sem(local, f"back_loaded{j}") for j in range(2)]
        rep_loaded = [net.sem(local, f"rep_loaded{j}") for j in range(CHUNKS)]
        block = local.enter_context(nc.Block())

        def prep_no(kind, t):
            if kind in (PN, K1):
                first = {PN: 0, K1: 1}[kind]
                return first if isinstance(t, int) and t == 0 else 5 * (t - 1) + 4 + first
            last = isinstance(t, int) and t == TILES - 1
            return 5 * t + {K2: 2, K3: 3, K4: 4 if last else 6}[kind]

        def slot_no(kind, t):
            if kind == K1:
                return 0 if isinstance(t, int) and t == 0 else 4 * (t - 1) + 3
            last = isinstance(t, int) and t == TILES - 1
            return 4 * t + {K2: 1, K3: 2, K4: 3 if last else 4}[kind]

        def silu_no(kind, t):
            if kind == PN:
                return 0 if isinstance(t, int) and t == 0 else 2 * (t - 1) + 1
            last = isinstance(t, int) and t == TILES - 1
            return 2 * t + (1 if last else 2)

        def t_past(t, first):
            return not isinstance(t, int) or t >= first

        def band(t, h):
            return t // 2 if isinstance(t, int) else (t - h) // 2

        def norm_in(kind, h):
            return {PN: X[:], K1: kin[:, 0], K2: kin[:, 1], K3: Y[:, h], K4: U[:, h]}[kind]

        def norm_out(kind, h):
            return Y[:, h] if kind == PN else norm_in(kind, h)

        def silu_of(kind, h):
            return {K1: ku[:, 0], K2: ku[:, 1], K3: U[:, h], K4: Y[:, h]}[kind]

        def groups(kind):
            return 2 * GROUP if kind in (K1, K2) else GROUP

        vec = k["kan_vec"]
        ln_g, ln_b, out_b = ({PN: vec[:, 0:1], **{n: vec[:, 3 * n - 1:3 * n] for n in (K1, K2, K3, K4)}},
                             {PN: vec[:, 1:2], **{n: vec[:, 3 * n:3 * n + 1] for n in (K1, K2, K3, K4)}},
                             {n: vec[:, 3 * n + 1:3 * n + 2] for n in (K1, K2, K3, K4)})

        def cols(n):
            return slice(BANK * n, BANK * n + BANK)

        def program(slot, steps):
            def run(kind, t, h, inner):
                placed = sorted((s for p in inner for s in steps(*p)), key=lambda s: s[0])
                slot(kind, t, h, lambda at: [f() for pos, f in placed if pos == at or (at == CHUNKS and pos > CHUNKS)])

            def alone(kind, t, h):
                for _, f in steps(kind, t, h, 0):
                    f()

            def round_(t, h, last=False):
                o = 1 - h
                run(K2, t, h, [(K3, t, h, 0)] if last else [(K3, t, h, 0), (PN, t + 1, o, 1)])
                run(K3, t, h, [] if last else [(K1, t + 1, o, 1)])
                if last:
                    alone(K4, t, h)
                else:
                    run(K1, t + 1, o, [(K4, t, h, 1)])
                run(K4, t, h, [] if last else [(K2, t + 1, o, 0)])
            return run, alone, round_

        def rounds(eng, slot, steps, begin=None):
            run, alone, round_ = program(slot, steps)
            alone(PN, 0, 0)
            alone(K1, 0, 0)
            run(K1, 0, 0, [(K2, 0, 0, 0)])
            round_(0, 0)
            round_(1, 1)
            with eng.Fori(1, BANDS - 1) as r:
                for h in range(HALVES):
                    round_(r * 2 + h, h)
            round_(TILES - 2, 0)
            round_(TILES - 1, 1, True)

        @block.sync
        def _(sp):
            def regroup(dst, src, sem, backwards=False):
                for i in range(2 * GROUP):
                    wide = (dst if backwards else src)[QUAD // 2 * i:QUAD // 2 * i + QUAD // 2]
                    wide = wide.rearrange("p (z n) -> p z n", z=BAND)
                    deep = (src if backwards else dst)[:, cols_of(i)]
                    sp.dma_start(wide if backwards else deep, deep if backwards else wide).then_inc(sem, 16)

            def cols_of(i):
                return slice(COLS * i, COLS * i + COLS)

            def load_x(t, h):
                tile_ = source[band(t, h), h]
                wait_past(sp, centered, CHUNKS * prep_no(PN, t - 1) + CHUNKS if t_past(t, 1) else 0)
                sp.dma_start(X[:], tile_).then_inc(x_loaded, 16)

            def load_r(t, h):
                tile_ = source[band(t, h), h]
                wait_past(sp, stored, 16 * t)
                wait_past(sp, measured, t)
                sp.dma_start(R[:], tile_).then_inc(r_loaded, 16)

            def store(t, h):
                tile_ = target[band(t, h), h]
                sp.wait_ge(x3_ready, t + 1)
                sp.dma_start(tile_, R[:]).then_inc(stored, 16)

            def feed_k1(t, h):
                sp.wait_ge(normed, prep_no(PN, t) + 1)
                regroup(kin[:, 0], Y[:, h], kin_loaded[0])
                wait_past(sp, back_loaded[0], 128 * t)
                sp.wait_ge(u_ready, silu_no(PN, t) + 1)
                regroup(ku[:, 0], U[:, h], ku_loaded[0])

            def feed_k2(t):
                sp.wait_ge(copied_y, t + 1)
                wait_past(sp, summed, t)
                wait_past(sp, back_loaded[1], 128 * t)
                regroup(kin[:, 1], turned_y[:, 0], kin_loaded[1])
                sp.wait_ge(copied_u, t + 1)
                regroup(ku[:, 1], turned_y[:, 1], ku_loaded[1])

            def give_back(kind, t):
                sp.wait_ge(evacuated, CHUNKS * slot_no(kind, t) + CHUNKS)
                wait_past(sp, summed, t)
                regroup(back[kind], ku[:, kind - K1], back_loaded[kind - K1], True)

            def repeat(kind, t, h, chunks=range(CHUNKS)):
                b = slot_no(kind, t)
                s = norm_out(kind, h)
                sp.wait_ge(normed, prep_no(kind, t) + 1)
                for n in chunks:
                    wait_past(sp, args, 8 * (b - 1) + 2 * n + 2)
                    for g in range(GROUP):
                        src = s[QUAD * g:QUAD * g + QUAD, cols(n)].unsqueeze(1).to_broadcast([QUAD, GROUP, BANK])
                        sp.dma_start(srep[:, n, g, :], src).then_inc(rep_loaded[n], 16)

            def round_(t, h, left=2):
                o = 1 - h
                repeat(K2, t, h)
                if t_past(t, 1):
                    store(t - 1, o)
                load_r(t, h)
                repeat(K3, t, h)
                if left > 1:
                    load_x(t + 2, h)
                if left:
                    feed_k1(t + 1, o)
                give_back(K2, t)
                if left:
                    repeat(K1, t + 1, o)
                    feed_k2(t + 1)
                repeat(K4, t, h)
                if left:
                    give_back(K1, t + 1)
            load_x(0, 0)
            load_x(1, 1)
            feed_k1(0, 0)
            feed_k2(0)
            repeat(K1, 0, 0)
            give_back(K1, 0)
            round_(0, 0)
            round_(1, 1)
            with sp.Fori(1, BANDS - 1) as r:
                for h in range(HALVES):
                    round_(r * 2 + h, h)
            round_(TILES - 2, 0, 1)
            round_(TILES - 1, 1, 0)
            store(TILES - 1, 1)
            sp.wait_ge(stored, 16 * TILES)

        @block.scalar
        def _(act):
            a = nc.scalar

            def steps(kind, t, h, start):
                no = prep_no(kind, t)
                src, dst = norm_in(kind, h), norm_out(kind, h)

                def evacuate():
                    if kind == K4:
                        act.wait_ge(u_ready, silu_no(K4, t) + 1)
                    if kind == PN:
                        wait_past(act, x3_ready, t - 1)
                    wait_past(act, var_ready, no)
                    for n in range(CHUNKS):
                        act.wait_ge(centered, CHUNKS * no + n + 1)
                        shift = k["pn_shift"][:, h:h + 1] if kind == PN else 0.0
                        a.activation(dst[:, cols(n)], cen[:, n % 2, :], ACT.Identity, bias=shift)
                        a.activation(sq[:, cols(n)], cen[:, n % 2, :], ACT.Square, bias=shift).then_inc(squared, 1)

                def tanh(kind, t, h):
                    if kind == PN:
                        act.wait_ge(normed, prep_no(PN, t) + 1)
                    else:
                        act.wait_ge(summed, t + 1)
                    x_, u_ = (Y, U) if kind == PN else (U, Y)
                    a.activation(u_[:, h], x_[:, h], ACT.Tanh, scale=0.5).then_inc(tanh_ready, 1)
                if kind == K1:
                    return [(start - 1, lambda: tanh(PN, t, h)), (start, evacuate)]
                if kind == K4:
                    return [(start, lambda: tanh(K4, t, h)), (start, evacuate)]
                return [(start, evacuate)]

            def slot(kind, t, h, inner):
                b = slot_no(kind, t)
                dst = silu_of(kind, h)

                def evacuate(n):
                    act.wait_ge(used, 8 * b + 2 * n + 2)
                    a.activation(dst[:, cols(n)], out[:, n % 2, :], ACT.Identity, bias=out_b[kind]).then_inc(evacuated, 1)
                for n in range(CHUNKS):
                    inner(n)
                    for j in range(2):
                        unit = 8 * b + 2 * n + j
                        act.wait_ge(args, unit + 1)
                        e = ex[:, (2 * n + j) % RING].rearrange("p g n -> p (g n)")
                        a.activation(e, e, ACT.Exp, bias=k["c_grid"][:, j, 1:2], scale=-1.0).then_inc(exps, 1)
                    if n:
                        evacuate(n - 1)
                inner(CHUNKS)
                evacuate(CHUNKS - 1)
            rounds(act, slot, steps)

        @block.vector
        def _(dve):
            v = nc.vector

            def steps(kind, t, h, start):
                no = prep_no(kind, t)
                dst = norm_out(kind, h)
                G = groups(kind)
                N = G * BLOCKS

                def chain():
                    dve.wait_ge(var_ready, no + 1)
                    flat = hilo[:].rearrange("p z n -> p (z n)")
                    hi, lo = flat[:, 0:N], flat[:, N:2 * N]
                    v.tensor_scalar(hi, var[:, 0:N], float(G) / P, EPS_LN, ALU.mult, ALU.add)
                    v.drain()
                    rsqrt_steps(v, y[:, 0:N], hi, lo)
                    split_hi_lo(v, hi, lo, y[:, 0:N]).then_inc(factors, 1)

                def copy():
                    dve.wait_ge(turned_ready, no + 1)
                    z = N // (P // 2)
                    v.tensor_copy(hiloT[:, 0:z], turned[:, 0:z]).then_inc(copied, 1)

                def scale():
                    for n in range(CHUNKS):
                        dve.wait_ge(spread_ready, CHUNKS * no + n + 1)
                        v.scalar_tensor_tensor(dst[:, cols(n)], dst[:, cols(n)], ln_g[kind], spread[:, n % 2, :],
                                               ALU.mult, ALU.mult).then_inc(scaled, 1)
                    dve.wait_ge(scaled, CHUNKS * no + CHUNKS)
                    v.tensor_scalar(dst, dst, ln_b[kind], None, ALU.add).then_inc(normed, 1)

                def regrow():
                    dve.wait_ge(r_loaded, 16 * t + 16)
                    v.tensor_scalar(R[:], R[:], k["grown"][:, h:h + 1], bias[:, h:h + 1], ALU.mult,
                                    ALU.add).then_inc(regrown, 1)

                def silu(kind, t, h):
                    dve.wait_ge(tanh_ready, silu_no(kind, t) + 1)
                    x_, u_ = (Y[:, h], U[:, h]) if kind == PN else (U[:, h], Y[:, h])
                    v.scalar_tensor_tensor(u_, u_, 1.0, x_, ALU.add, ALU.mult).then_inc(u_ready, 1)

                def measure(t, h):
                    dve.wait_ge(x3_ready, t + 1)
                    for n in range(CHUNKS):
                        last = v.bn_stats(part[:, 6 * n:6 * n + 6], R[:, cols(n)])
                    last.then_inc(measured, 1)
                    v.drain()
                    v.tensor_copy(stats[:, h, band(t, h), :], part[:])
                    v.drain()
                s = [(start + 2, chain), (start + 3, copy), (start + 4, scale)]
                if kind == K1:
                    s.insert(0, (start - 1, lambda: silu(PN, t, h)))
                if kind == K4:
                    s.insert(0, (start, lambda: silu(K4, t, h)))
                    s.append((start + 2, regrow))
                if kind == K3 and not (isinstance(t, int) and t == 0):
                    s.insert(0, (start + 1, lambda: measure(t - 1, 1 - h)))
                return s

            def slot(kind, t, h, inner):
                b = slot_no(kind, t)
                for n in range(CHUNKS):
                    inner(n)
                    dve.wait_ge(rep_loaded[n], 64 * b + 64)
                    for j in range(2):
                        unit = 8 * b + 2 * n + j
                        wait_past(dve, used, unit - RING + 1)
                        v.scalar_tensor_tensor(ex[:, (2 * n + j) % RING].rearrange("p g n -> p (g n)"),
                                               srep[:, n].rearrange("p g n -> p (g n)"), k["c_grid"][:, j, 0:1],
                                               srep[:, n].rearrange("p g n -> p (g n)"), ALU.add, ALU.mult).then_inc(args, 1)
                inner(CHUNKS)
                if kind == K4 and isinstance(t, int) and t == TILES - 1:
                    steps(K3, t + 1, 1 - h, 0)[0][1]()
            rounds(dve, slot, steps)

        @block.tensor
        def _(pe):
            m = nc.tensor

            def steps(kind, t, h, start):
                no = prep_no(kind, t)
                src = norm_in(kind, h)
                G = groups(kind)
                ones = k["c_ones8"][:] if kind in (K1, K2) else c["ones4"][:]

                def center():
                    if kind == PN:
                        pe.wait_ge(x_loaded, 16 * t + 16)
                    elif kind in (K1, K2):
                        pe.wait_ge(kin_loaded[kind - K1], 128 * t + 128)
                    elif kind == K4:
                        pe.wait_ge(summed, t + 1)
                    weights = k["pn_center"][:, h, :] if kind == PN else k["c_center"][:, 1 if kind in (K1, K2) else 0, :]
                    for n in range(CHUNKS):
                        wait_past(pe, squared, CHUNKS * no + n - 1)
                        m.matmul(cen[:, n % 2, :], weights, src[:, cols(n)], start=True, stop=True).then_inc(centered, 1)

                def variance():
                    pe.wait_ge(squared, CHUNKS * no + CHUNKS)
                    for i in range(BLOCKS):
                        last = m.matmul(var[:, G * i:G * i + G], sq[:, P * i:P * i + P], ones, start=True, stop=True)
                    last.then_inc(var_ready, 1)

                def turn():
                    pe.wait_ge(factors, no + 1)
                    for z in range(G // GROUP):
                        last = m.transpose(turned[:, z, :], hilo[:, z, :], c["ident"][:])
                    last.then_inc(turned_ready, 1)

                def spread_out():
                    pe.wait_ge(copied, no + 1)
                    for n in range(CHUNKS):
                        wait_past(pe, scaled, CHUNKS * no + n - 1)
                        for i in range(GROUP):
                            dst = spread[:, n % 2, P * i:P * i + P]
                            if G == GROUP:
                                last = m.matmul(dst, c["sel4"][:, GROUP * n + i, :], hiloT[:, 0, :], start=True, stop=True)
                            else:
                                for z in range(2):
                                    last = m.matmul(dst, k["sel8"][:, GROUP * n + i, :], hiloT[:, z, :], start=(z == 0),
                                                    stop=(z == 1))
                        last.then_inc(spread_ready, 1)
                return [(start, center), (start + 1, variance), (start + 2, turn), (start + 3, spread_out)]

            def slot(kind, t, h, inner):
                b = slot_no(kind, t)
                u = silu_of(kind, h)
                for n in range(CHUNKS):
                    inner(n)
                    if n == 0:
                        if kind in (K1, K2):
                            pe.wait_ge(ku_loaded[kind - K1], 128 * t + 128)
                        else:
                            pe.wait_ge(u_ready, silu_no(PN if kind == K3 else K4, t) + 1)
                    wait_past(pe, evacuated, CHUNKS * b + n - 1)
                    m.matmul(out[:, n % 2, :], k["kan_silu"][:, kind - 1, :], u[:, cols(n)], start=True, stop=False)
                    for j in range(2):
                        pe.wait_ge(exps, 8 * b + 2 * n + j + 1)
                        for g in range(GROUP):
                            last = m.matmul(out[QUAD * g:QUAD * g + QUAD, n % 2, :], k["kan_basis"][:, kind - 1, j, :],
                                            ex[:, (2 * n + j) % RING, g, :], start=False, stop=(j == 1),
                                            tile_position=(0, QUAD * g))
                        last.then_inc(used, 1)
                inner(CHUNKS)
            rounds(pe, slot, steps)

        @block.gpsimd
        def _(pool):
            g = nc.gpsimd

            def columns_first(tile_):
                return tile_.rearrange("p (rw x) -> p x rw", x=BAND)

            def turn(t, h):
                for j, (src, sem) in enumerate(((Y, copied_y), (U, copied_u))):
                    if j:
                        pool.wait_ge(u_ready, silu_no(PN, t) + 1)
                        wait_past(pool, ku_loaded[1], 128 * t)
                    else:
                        pool.wait_ge(normed, prep_no(PN, t) + 1)
                        wait_past(pool, kin_loaded[1], 128 * t)
                    g.tensor_tensor(turned_y[:, j].rearrange("p (x r w) -> p x (r w)", x=BAND, r=BAND),
                                    columns_first(src[:, h]), one[:].unsqueeze(1).to_broadcast([P, BAND, BAND * QUAD]),
                                    ALU.mult).then_inc(sem, 1)

            def total(t, h):
                pool.wait_ge(back_loaded[0], 128 * t + 128)
                pool.wait_ge(evacuated, CHUNKS * slot_no(K3, t) + CHUNKS)
                g.tensor_tensor(U[:, h], U[:, h], back[K1], ALU.add).then_inc(half_sum, 1)
                pool.wait_ge(back_loaded[1], 128 * t + 128)
                pool.wait_ge(half_sum, t + 1)
                z = U[:, h].rearrange("p (r w x) -> p r w x", r=BAND, x=BAND)
                g.tensor_tensor(z, z, back[K2].rearrange("p (x r w) -> p r w x", x=BAND, r=BAND), ALU.add).then_inc(summed, 1)

            def finish(t, h):
                pool.wait_ge(regrown, t + 1)
                pool.wait_ge(evacuated, CHUNKS * slot_no(K4, t) + CHUNKS)
                g.tensor_tensor(R[:], R[:], Y[:, h], ALU.add).then_inc(x3_ready, 1)

            def round_(t, h, last=False):
                if not last:
                    turn(t + 1, 1 - h)
                total(t, h)
                finish(t, h)
            g.memset(one[:], 1.0)
            g.drain()
            turn(0, 0)
            round_(0, 0)
            round_(1, 1)
            with pool.Fori(1, BANDS - 1) as r:
                for h in range(HALVES):
                    round_(r * 2 + h, h)
            round_(TILES - 2, 0)
            round_(TILES - 1, 1, True)


PATTERN = {(1, 1): (128, 1), (1, 0): (64, 2), (1, -1): (32, 4), (0, 1): (16, 8)}


def pattern_layer(net, source, scale, bias, out):
    nc, c = net.nc, net.c
    WEIGHT = 0.5 / 255
    ON_PE, ON_DVE = [(1, 1), (1, 0)], [(1, -1), (0, 1)]
    DIRS = ON_PE + ON_DVE
    TILES = BANDS * HALVES
    CHUNKS = TILE // BANK
    with ExitStack() as local:
        xt = net.sb(local, "xt", [P, HALVES, HALO, COLS])
        z = net.sb(local, "z", [P, HALVES, HALO, PAD])
        d = net.sb(local, "d", [P, HALVES, len(DIRS), BAND + 1, PAD])
        ot = net.sb(local, "ot", [P, HALVES, BAND, COLS])
        weights = net.sb(local, "weights", [P, 2 * len(ON_PE), P])
        acc = net.ps(local, "acc", [P, HALVES, CHUNKS, BANK])
        padded, weighted, z_ready, diff_dve, diff_pool, tanh_ready, acc_ready, begun, added, out_ready = (
            net.sem(local, n) for n in ("padded", "weighted", "z_ready", "diff_dve", "diff_pool", "tanh_ready", "acc_ready",
                                        "begun", "added", "out_ready"))
        loaded = [net.sem(local, f"loaded{h}") for h in range(HALVES)]
        stored = [net.sem(local, f"stored{h}") for h in range(HALVES)]
        block = local.enter_context(nc.Block())
        bands = out.rearrange("b c r w -> (b c) (r w)").rearrange("p (t n) -> p t n", n=TILE)

        def region(dr, dc):
            return slice(1 - dr, BAND + 1), slice(0 if dc > 0 else 1, PAD if dc < 0 else PAD - 1)

        def difference(engine, h, direction):
            (dr, dc), n = direction, DIRS.index(direction)
            rows, columns = region(dr, dc)
            there = z[:, h, rows.start + dr:rows.stop + dr, columns.start + dc:columns.stop + dc]
            return engine.tensor_tensor(d[:, h, n, rows, columns], there, z[:, h, rows, columns], ALU.subtract)

        def term(h, direction, opposite, rows):
            (dr, dc), n = direction, DIRS.index(direction)
            back = (dr, dc) if opposite else (0, 0)
            return d[:, h, n, rows.start + 1 - back[0]:rows.stop + 1 - back[0], 1 - back[1]:1 - back[1] + COLS]

        def factor(direction, opposite):
            return (-WEIGHT if opposite else WEIGHT) * PATTERN[direction][int(opposite)]

        @block.sync
        def _(sp):
            def load(r):
                for h in range(HALVES):
                    wait_past(sp, out_ready, 2 * (r - 1) + h + 1)
                    for rows, src in ((slice(1, BAND + 1), source[r, h]),
                                      (slice(0, 1), source[(r + BANDS - 1) % BANDS, h, :, TILE - COLS:]),
                                      (slice(HALO - 1, HALO), source[(r + 1) % BANDS, h, :, 0:COLS])):
                        sp.dma_start(xt[:, h, rows, :].rearrange("p r w -> p (r w)"), src).then_inc(loaded[h], 16)

            def store(r):
                for h in range(HALVES):
                    sp.wait_ge(out_ready, 2 * r + h + 1)
                    sp.dma_start(bands[P * h:P * h + P, r, :], ot[:, h].rearrange("p r w -> p (r w)")).then_inc(stored[h], 16)
            pipeline(sp, BANDS, [(0, load), (1, store)])
            for h in range(HALVES):
                sp.wait_ge(stored[h], 16 * BANDS)

        @block.scalar
        def _(act):
            a = nc.scalar
            act.wait_ge(padded, 1)

            def normalise(r, h):
                i = 2 * r + h
                first, last = (isinstance(r, int) and r == e for e in (0, BANDS - 1))
                act.wait_ge(loaded[h], 48 * r + 48)
                wait_past(act, diff_dve, i - 1)
                wait_past(act, diff_pool, i - 1)
                inner = slice(1 if first else 0, HALO - 1 if last else HALO)
                n = a.activation(z[:, h, inner, 1:COLS + 1], xt[:, h, inner, :], ACT.Identity, bias=bias[:, h:h + 1],
                                 scale=scale[:, h:h + 1])
                if last:
                    n = a.activation(z[:, h, HALO - 1, 1:COLS + 1], xt[:, h, HALO - 1, :], ACT.Copy, scale=0.0)
                n.then_inc(z_ready, 1)

            def tanh(r, h):
                i = 2 * r + h
                for n, (dr, dc) in enumerate(DIRS):
                    if n == 0:
                        act.wait_ge(diff_dve, i + 1)
                    if n == 2:
                        act.wait_ge(diff_pool, i + 1)
                    rows, columns = region(dr, dc)
                    t = d[:, h, n, rows, columns]
                    a.activation(t, t, ACT.Tanh, scale=5.0).then_inc(tanh_ready, 1)
            normalise(0, 0)
            normalise(0, 1)
            tanh(0, 0)
            with act.Fori(1, BANDS - 1) as r:
                normalise(r, 0)
                tanh(r - 1, 1)
                normalise(r, 1)
                tanh(r, 0)
            normalise(BANDS - 1, 0)
            tanh(BANDS - 2, 1)
            normalise(BANDS - 1, 1)
            tanh(BANDS - 1, 0)
            tanh(BANDS - 1, 1)

        @block.gpsimd
        def _(pool):
            g = nc.gpsimd

            def differences(r):
                for h in range(HALVES):
                    i = 2 * r + h
                    wait_past(pool, out_ready, i - 1)
                    pool.wait_ge(z_ready, i + 1)
                    difference(g, h, ON_DVE[0])
                    difference(g, h, ON_DVE[1]).then_inc(diff_pool, 1)
            g.memset(z[:], 0.0).then_inc(padded, 1)
            pipeline(pool, BANDS, [(0, differences)])

        @block.vector
        def _(dve):
            v = nc.vector
            for n, (direction, opposite) in enumerate((p, o) for p in ON_PE for o in (False, True)):
                last = v.tensor_scalar(weights[:, n, :], c["ident"][:], factor(direction, opposite), None, ALU.mult)
            last.then_inc(weighted, 1)

            def differences(r, h):
                i = 2 * r + h
                wait_past(dve, acc_ready, CHUNKS * (i - 1))
                dve.wait_ge(z_ready, i + 1)
                difference(v, h, ON_PE[0])
                difference(v, h, ON_PE[1]).then_inc(diff_dve, 1)

            def add(r, h):
                i = 2 * r + h
                wait_past(dve, stored[h], 16 * r)
                dve.wait_ge(acc_ready, CHUNKS * i + CHUNKS)
                whole = slice(0, BAND)
                into = ot[:, h]
                sums = acc[:, h].rearrange("p k (r w) -> p (k r) w", w=COLS)
                v.scalar_tensor_tensor(into, xt[:, h, 1:BAND + 1, :], 0.5, sums, ALU.add, ALU.add).then_inc(begun, 1)
                dve.wait_ge(begun, i + 1)
                for n, (direction, opposite) in enumerate((p, o) for p in ON_DVE for o in (False, True)):
                    dve.wait_ge(tanh_ready, len(DIRS) * i + len(ON_PE) + n // 2 + 1)
                    if n:
                        dve.wait_ge(added, 3 * i + n)
                    v.scalar_tensor_tensor(into, term(h, direction, opposite, whole), factor(direction, opposite), into,
                                           ALU.mult, ALU.add).then_inc(added if n < 3 else out_ready, 1)
            differences(0, 0)
            differences(0, 1)
            add(0, 0)
            with dve.Fori(1, BANDS) as r:
                differences(r, 0)
                add(r - 1, 1)
                differences(r, 1)
                add(r, 0)
            add(BANDS - 1, 1)

        @block.tensor
        def _(pe):
            m = nc.tensor
            pe.wait_ge(weighted, 1)

            def sums(r):
                for h in range(HALVES):
                    i = 2 * r + h
                    pe.wait_ge(tanh_ready, len(DIRS) * i + len(ON_PE))
                    wait_past(pe, begun, i - 1)
                    for k in range(CHUNKS):
                        rows = slice(2 * k, 2 * k + 2)
                        for n, (direction, opposite) in enumerate((p, o) for p in ON_PE for o in (False, True)):
                            last = m.matmul(acc[:, h, k, :], weights[:, n, :], term(h, direction, opposite, rows),
                                            start=(n == 0), stop=(n == 3))
                        last.then_inc(acc_ready, 1)
            pipeline(pe, BANDS, [(0, sums)])


def build_program(nc, ins, out):
    with ExitStack() as ctx:
        net = Net(nc, ctx, ins)
        load_constants(net)
        x_rows = ins["x"].rearrange("b c r w -> (b c) (r w)")
        t1, t2, x1, x2, x3 = (net.scratch(k) for k in ("t1", "t2", "x1", "x2", "x3"))
        SW = BANDS * TILE // BANK * 6
        stats = net.sb(ctx, "stats", [P, HALVES, SW])
        by_band = stats[:].rearrange("p h (r n) -> p h r n", r=BANDS)
        merged = stats[:].rearrange("p h n -> p (h n)").rearrange("p (o n) -> p o n", o=1)
        scale, bias = net.sb(ctx, "scale", [P, HALVES]), net.sb(ctx, "bias", [P, HALVES])
        bn = net.sb(ctx, "bn", [P, 4])
        with ExitStack() as local:
            loaded = net.sem(local, "bn_loaded")
            block = local.enter_context(nc.Block())

            @block.sync
            def _(sp):
                sp.dma_start(bn[:], ins["bn"]).then_inc(loaded, 16)
                sp.wait_ge(loaded, 16)
        input_stats(net, x_rows, stats[:])
        norm_vectors(net, stats[:], net.c["pair"][:], 1e-5, scale[:], bias[:])
        conv_layer(net, x_rows, scale, bias, ins["w1"], ins["b1"], t1, by_band, True)
        norm_vectors(net, merged, net.c["channel"][:], 1e-5, scale[:, 0:1], bias[:, 0:1], bn[:, 0:1], bn[:, 1:2])
        conv_layer(net, t1, scale[:, 0:1], bias[:, 0:1], ins["w2"], ins["b2"], t2, by_band, False)
        norm_vectors(net, merged, net.c["channel"][:], 1e-5, scale[:, 0:1], bias[:, 0:1], bn[:, 2:3], bn[:, 3:4])
        residual_layer(net, x_rows, t2, scale[:, 0:1], bias[:, 0:1], x1, by_band)
        norm_vectors(net, stats[:], net.c["pair"][:], 1e-5, scale[:], bias[:])
        with ExitStack() as local:
            coef = net.sb(local, "coef", [P, IMAGES, 2, KP])
            with ExitStack() as inner:
                tables = net.sb(inner, "tables", [P, 2, HALVES * P])
                g1 = net.sb(inner, "g1", [P, CH, 2, KP])
                g2 = net.sb(inner, "g2", [P, CH, 3, KP])
                spread_table(net, scale[:], tables[:, 0, :])
                spread_table(net, bias[:], tables[:, 1, :])
                pole_kernels(net, g1, g2)
                residues(net, x1, tables[:, 0, :], tables[:, 1, :], g1, g2, coef[:])
            image_stats = stats[:].rearrange("p h n -> p (h n)").rearrange("p (i n) -> p i n", i=CH)
            evaluate_residues(net, x1, coef, x2, image_stats)
            norm_vectors_by_image(net, image_stats, scale, bias)
        with ExitStack() as local:
            k = kan_constants(net, local)
            prepare_kan(net, k, scale[:], bias[:])
            window_layer(net, k, x2, bias, x3, by_band)
        norm_vectors(net, stats[:], net.c["pair"][:], 1e-5, scale[:], bias[:])
        pattern_layer(net, x3, scale, bias, out)


def shape_constants():
    p = np.arange(P)
    f = lambda a: np.ascontiguousarray(a, dtype=np.float32)
    sel4 = np.zeros((P, BLOCKS, P), np.float32)
    for k in range(P // 2):
        sel4[k, k // GROUP, QUAD * (k % GROUP):QUAD * (k % GROUP) + QUAD] = 1.0
    sel4[P // 2:] = sel4[:P // 2]
    sel8 = np.zeros((P, BLOCKS, P), np.float32)
    for k in range(P):
        sel8[k, k // 8, 16 * (k % 8):16 * (k % 8) + 16] = 1.0
    same = lambda n: p[:, None] // n == p[None] // n
    near = (p % GROUP)[:, None] + GROUP * np.arange(2)[None] - 3.5
    turn = 2 * np.pi * ((p[:, None] * p[None]) % SUB) / SUB
    return {
        "c_ident": np.eye(P, dtype=np.float32),
        "c_ones4": f(p[:, None] // QUAD == np.arange(GROUP)[None]),
        "c_pair": f(0.5 * (p[:, None] // 2 == p[None] // 2)),
        "c_channel": f((p[:, None] % CH == p[None] % CH) / GROUP),
        "c_sel4": sel4,
        "c_sel8": sel8,
        "c_ones8": f(p[:, None] // 16 == np.arange(8)[None]),
        "c_center": f(np.stack([np.eye(P) - same(n) / n for n in (32, 16)], axis=1)),
        "c_grid": f(np.stack([-2 * near, -near ** 2], axis=2)),
        "c_dft": np.stack([np.cos(turn), np.sin(turn), -np.sin(turn)], axis=1).astype(np.float32),
        "c_freq": np.fft.fftfreq(SUB).astype(np.float32)[:, None],
        "c_mask": f(p[:, None] // MODES == p[None] // MODES),
    }


def conv_weights(w):
    out = np.zeros((4, CH, 2, 3, CH), w.dtype)
    for o in range(2):
        for dy in range(3):
            out[o + dy, :, o] = w[:, :, dy, :].transpose(1, 2, 0)
    return np.ascontiguousarray(out.reshape(P, 2, 3, CH))


def kan_arrays(a):
    place = np.arange(16).reshape(8, 2).T.ravel()
    vec, basis, silu = [np.tile(a["L2_conv_pn_" + n], GROUP) for n in "gb"], [], []
    for n in range(1, 5):
        get = lambda name: a[f"L2_conv_k{n}_{name}"]
        order = place if n < 3 else np.arange(CH)
        F = len(order)
        vec += [np.tile(get(name)[order], P // F) for name in ("ln_g", "ln_b", "bb")]
        ws = get("ws").reshape(F, F, 2, GROUP)[order][:, order]
        b = np.zeros((QUAD // F, F, GROUP, 2, QUAD // F, F), ws.dtype)
        u = np.zeros((P // F, F, P // F, F), ws.dtype)
        for d in range(QUAD // F):
            b[d, :, :, :, d, :] = ws.transpose(1, 3, 2, 0)
        for d in range(P // F):
            u[d, :, d, :] = get("wb")[order][:, order].T
        basis.append(b.reshape(P, 2, QUAD))
        silu.append(u.reshape(P, P))
    return {"kan_vec": np.stack(vec, axis=1), "kan_basis": np.stack(basis, axis=1), "kan_silu": np.stack(silu, axis=1)}


def lay_out(inputs):
    a = {k: np.asarray(v) for k, v in inputs.items()}
    per_channel = lambda v: np.ascontiguousarray(np.tile(v, GROUP)[:, None])
    d = {"x": np.ascontiguousarray(a["x"])}
    d["w1"], d["w2"] = conv_weights(a["L0_conv_w1"]), conv_weights(a["L0_conv_w2"])
    d["b1"], d["b2"] = per_channel(a["L0_conv_b1"]), per_channel(a["L0_conv_b2"])
    d["bn"] = np.concatenate([per_channel(a["L0_conv_" + k]) for k in ("g1", "beta1", "g2", "beta2")], axis=1)
    for n in ("wp1", "wp2"):
        for z in "ri":
            d[n + z] = np.ascontiguousarray(a[f"L1_conv_{n}{z}"].reshape(1, CH * KP))
    d["poles"] = np.ascontiguousarray(np.stack([np.stack([a[f"L1_conv_{n}{z}"].transpose(0, 2, 1).reshape(KP, CH)
                                                          for z in "ri"], axis=1) for n in ("wp1", "wp2")], axis=1))
    d["res"] = np.ascontiguousarray(np.stack([a[f"L1_conv_wr{z}"].transpose(1, 2, 0, 3).reshape(KP, CH, MODES)
                                              for z in "ri"], axis=2))
    d["x_grid"], d["t_grid"] = a["L1_conv_x_grid"], a["L1_conv_t_grid"]
    d.update(kan_arrays(a))
    d.update(shape_constants())
    return d


def kernel(**inputs):
    import concourse.bacc as bacc
    from concourse.bass_utils import run_bass_kernel_spmd

    arrays = lay_out(inputs)
    nc = bacc.Bacc("TRN2", target_bir_lowering=False, num_devices=1)
    ins = {n: nc.dram_tensor("in_" + n, v.shape, mybir.dt.from_np(v.dtype), kind="ExternalInput").ap()
           for n, v in arrays.items()}
    out = nc.dram_tensor("out", (IMAGES, CH, ROWS, COLS), F32, kind="ExternalOutput").ap()
    build_program(nc, ins, out)
    r = run_bass_kernel_spmd(nc, [{"in_" + n: v for n, v in arrays.items()}], core_ids=[0])
    return r.results[0]["out"]
```

```python
from contextlib import ExitStack

import numpy as np

import concourse.bass as bass
from concourse import mybir

F32 = mybir.dt.float32
F32R = mybir.dt.float32r
I32 = mybir.dt.int32
ALU = mybir.AluOpType
ACT = mybir.ActivationFunctionType

P = 128
QUAD = 32
IMAGES, CH, ROWS, COLS = 8, 32, 256, 256
GROUP = P // CH
HALVES = IMAGES // GROUP
BAND = 8
BANDS = ROWS // BAND
TILE = BAND * COLS
BANK = 512
BLOCKS = TILE // P
HALO = BAND + 2
PAD = COLS + 2

MAX_NORM = 1.0 - 0.0001
ATANH_MAX = float(np.arctanh(np.float64(MAX_NORM)))
EPS_NORM = 1e-5
EPS_LN = 1e-5
CLIP = 1.0 - 1e-5


def pipeline(eng, count, stages):
    deep = max(lag for lag, _ in stages)
    for t in range(deep + 1):
        for lag, step in stages:
            if t >= lag:
                step(t - lag)
    with eng.Fori(deep + 1, count) as t:
        for lag, step in stages:
            step(t - lag)
    for t in range(count, count + deep):
        for lag, step in stages:
            if t - lag < count:
                step(t - lag)


def pipeline_by_two(eng, count, stages):
    deep = max(lag for lag, _ in stages)
    first = deep + 2 - deep % 2

    def round_(number, parity):
        for lag, step in stages:
            if not isinstance(number, int) or 0 <= number - lag < count:
                step(number - lag, (parity - lag) % 2)
    for number in range(first):
        round_(number, number % 2)
    with eng.Fori(first // 2, count // 2) as t:
        for parity in range(2):
            round_(t * 2 + parity, parity)
    for number in range(count, count + deep):
        round_(number, number % 2)


def wait_past(eng, sem, value):
    if not isinstance(value, int) or value > 0:
        eng.wait_ge(sem, value)


def wait_both(eng, sem_a, value_a, sem_b, value_b):
    value_a, value_b = (v if isinstance(v, int) else eng.to_reg(v) for v in (value_a, value_b))
    wait_past(eng, sem_a, value_a)
    wait_past(eng, sem_b, value_b)


def rsqrt_steps(dve, y, q, t):
    dve.tensor_scalar(y.bitcast(I32), q.bitcast(I32), -0.5, 1597463007.0, ALU.mult, ALU.add)
    for _ in range(3):
        dve.drain()
        dve.tensor_tensor(t, y, y, ALU.mult)
        dve.drain()
        dve.scalar_tensor_tensor(t, t, -0.5, q, ALU.mult, ALU.mult)
        dve.drain()
        dve.scalar_tensor_tensor(y, t, 1.5, y, ALU.add, ALU.mult)
    dve.drain()


def split_hi_lo(dve, hi, lo, s):
    dve.tensor_copy(hi.bitcast(F32R), s)
    dve.drain()
    return dve.tensor_tensor(lo.bitcast(F32R), s, hi, ALU.subtract)


class Net:

    def __init__(self, nc, ctx, ins):
        self.nc, self.ctx, self.ins = nc, ctx, ins
        self.count, self.sems, self.c = 0, {}, {}

    def sb(self, ctx, name, shape, dt=F32):
        self.count += 1
        return ctx.enter_context(self.nc.sbuf_tensor(f"{name}_{self.count}", shape, dt))

    def ps(self, ctx, name, shape):
        self.count += 1
        return ctx.enter_context(self.nc.psum_tensor(f"{name}_{self.count}", shape, F32))

    def sem(self, ctx, name):
        self.count += 1
        if ctx not in self.sems:
            self.sems[ctx] = []
            ctx.callback(self.clear, ctx)
        self.sems[ctx].append(self.nc.alloc_semaphore(f"{name}_{self.count}"))
        return self.sems[ctx][-1]

    def clear(self, ctx):
        self.nc.clear_and_free_semaphores(self.sems.pop(ctx))
        self.nc.all_engine_barrier()

    def scratch(self, name):
        return self.nc.dram_tensor(name, [BANDS, HALVES, P, TILE], F32).ap()


def load_constants(net, ctx, names):
    nc, ins = net.nc, net.ins
    selections = [n for n in names if n.startswith("c_sel")]
    own = {n: net.sb(ctx, n, list(ins[n].shape), F32R if n in selections else F32) for n in names}
    net.c.update({n.removeprefix("c_"): tile for n, tile in own.items()})
    with ExitStack() as local:
        staged = {n: net.sb(local, "staged", list(ins[n].shape)) for n in selections}
        loaded = net.sem(local, "loaded")
        block = local.enter_context(nc.Block())

        @block.sync
        def _(sp):
            for n in names:
                sp.dma_start(staged.get(n, own[n])[:], ins[n]).then_inc(loaded, 16)

        @block.vector
        def _(dve):
            dve.wait_ge(loaded, 16 * len(names))
            for n in selections:
                nc.vector.tensor_copy(own[n][:], staged[n][:])
            nc.vector.drain()


def norm_vectors(net, stats, average, eps, scale, bias, gamma=None, beta=None):
    nc = net.nc
    n = stats.shape[1]
    with ExitStack() as local:
        mv = net.sb(local, "mean_var", [P, n, 2])
        mean = net.sb(local, "mean", [P, n])
        spread = net.sb(local, "spread", [P, n])
        y = net.sb(local, "rstd", [P, n])
        t = net.sb(local, "t", [P, n])
        pm = net.ps(local, "pm", [P, 2, BANK])
        matrix = net.sb(local, "average", [P, P])
        loaded, own, gmean, sp_ready, gvar = (net.sem(local, k) for k in ("loaded", "own", "gmean", "spread", "gvar"))
        block = local.enter_context(nc.Block())

        @block.sync
        def _(sp):
            sp.dma_start(matrix[:], net.ins["c_" + average]).then_inc(loaded, 16)

        @block.tensor
        def _(pe):
            pe.wait_ge(loaded, 16)
            pe.wait_ge(own, 1)
            nc.tensor.matmul(pm[:, 0, 0:n], matrix[:], mv[:, :, 0], start=True, stop=True).then_inc(gmean, 1)
            pe.wait_ge(sp_ready, 1)
            nc.tensor.matmul(pm[:, 1, 0:n], matrix[:], spread[:], start=True, stop=True).then_inc(gvar, 1)

        @block.vector
        def _(dve):
            v = nc.vector
            for h in range(n):
                v.bn_aggr(mv[:, h, :], stats[:, h])
            v.drain()
            v.tensor_copy(t[:], mv[:, :, 0]).then_inc(own, 1)
            dve.wait_ge(gmean, 1)
            v.tensor_copy(mean[:], pm[:, 0, 0:n])
            v.drain()
            v.tensor_tensor(t[:], mv[:, :, 0], mean[:], ALU.subtract)
            v.drain()
            v.tensor_tensor(t[:], t[:], t[:], ALU.mult)
            v.drain()
            v.tensor_tensor(spread[:], t[:], mv[:, :, 1], ALU.add).then_inc(sp_ready, 1)
            dve.wait_ge(gvar, 1)
            v.tensor_scalar(spread[:], pm[:, 1, 0:n], eps, None, ALU.add)
            v.drain()
            rsqrt_steps(v, y[:], spread[:], t[:])
            if gamma is None:
                v.tensor_copy(scale, y[:])
            else:
                v.tensor_scalar(scale, y[:], gamma, None, ALU.mult)
            v.drain()
            v.tensor_tensor(t[:], mean[:], scale, ALU.mult)
            v.drain()
            if beta is None:
                v.tensor_scalar(bias, t[:], -1.0, None, ALU.mult)
            else:
                v.tensor_scalar(bias, t[:], -1.0, beta, ALU.mult, ALU.add)
            v.drain()


def input_stats(net, x_rows, stats):
    nc = net.nc
    span = 2
    with ExitStack() as local:
        xt = net.sb(local, "xt", [P, HALVES, span * TILE])
        part = net.sb(local, "part", [P, HALVES, span * TILE // BANK * 6])
        loaded = [net.sem(local, f"loaded{h}") for h in range(HALVES)]
        used = [net.sem(local, f"used{h}") for h in range(HALVES)]
        block = local.enter_context(nc.Block())
        wide = x_rows.rearrange("p (t n) -> p t n", n=span * TILE)
        into = stats.rearrange("p h (t n) -> p h t n", n=span * TILE // BANK * 6)

        @block.sync
        def _(sp):
            def load(t):
                for h in range(HALVES):
                    wait_past(sp, used[h], t)
                    sp.dma_start(xt[:, h, :], wide[P * h:P * h + P, t, :]).then_inc(loaded[h], 16)
            pipeline(sp, BANDS // span, [(0, load)])

        @block.vector
        def _(dve):
            v = nc.vector

            def measure(t):
                for h in range(HALVES):
                    dve.wait_ge(loaded[h], 16 * t + 16)
                    for k in range(span * TILE // BANK):
                        last = v.bn_stats(part[:, h, 6 * k:6 * k + 6], xt[:, h, BANK * k:BANK * k + BANK])
                    last.then_inc(used[h], 1)
                    v.drain()
                    v.tensor_copy(into[:, h, t, :], part[:, h, :])
            pipeline(dve, BANDS // span, [(0, measure)])


def conv_layer(net, source, scale, bias, weights, conv_bias, target, stats, first):
    nc, c = net.nc, net.c
    HT = HALO * COLS
    HB = HT // P
    with ExitStack() as local:
        def sb(name, shape, dt=F32):
            return net.sb(local, name, shape, dt)
        xt = sb("xt", [P, HALVES, HALO, COLS])
        xn = sb("xn", [P, HALVES, HT])
        sq = sb("sq", [P, HALVES, HT])
        u = sb("u", [P, HALVES, HALO, PAD])
        uc = sb("uc", [P, HALVES, GROUP, BAND // 2, PAD])
        v_sb = sb("v", [P, HALVES, BAND, COLS])
        sqv = sb("sqv", [P, HALVES, TILE])
        out = sb("out", [P, HALVES, TILE])
        w_sb = sb("w", [P, 2, 3, CH])
        cb = sb("cb", [P, 1])
        edge = sb("edge", [P, BANDS])
        part = sb("part", [P, HALVES, TILE // BANK * 6])
        n2, q, rn, t_, nc_, l1, l2, sl, pl, xx = (sb(k, [P, HALVES, P]) for k in
                                                  ("n2", "q", "rn", "t", "nclip", "l1", "l2", "sl", "pl", "xx"))
        sp1 = sb("sp1", [P, 2, HALVES, P])
        m2 = sb("m2", [P, P])
        sp2 = sb("sp2", [P, 2, P])
        pc1 = net.ps(local, "pc1", [P, HALVES, P])
        pc2 = net.ps(local, "pc2", [P, BANK])[:, 0:P]
        spread1 = net.ps(local, "spread1", [P, 2, BANK])
        spread2 = net.ps(local, "spread2", [P, 2, BANK])
        conv = net.ps(local, "conv", [P, 2, BANK])

        def sem(name):
            return net.sem(local, name)
        loaded = [sem(f"loaded{h}") for h in range(2)]
        uc_loaded = [sem(f"uc_loaded{h}") for h in range(2)]
        stored = [sem(f"stored{h}") for h in range(2)]
        ready = sem("params")
        zeroed = sem("zeroed")
        (normed, squared, summed1, normsq, logs, factors1, spread1_ready, u_ready, conv_ready, evacuated, summed2,
         factors2, spread2_ready, out_ready, read1, read2) = (sem(k) for k in (
             "normed", "squared", "summed1", "normsq", "logs", "factors1", "spread1_ready", "u_ready", "conv_ready",
             "evacuated", "summed2", "factors2", "spread2_ready", "out_ready", "read1", "read2"))
        block = local.enter_context(nc.Block())
        CHUNKS1 = HT // BANK
        CHUNKS2 = TILE // BANK

        @block.sync
        def _(sp):
            sp.dma_start(w_sb[:], weights).then_inc(ready, 16)
            sp.dma_start(cb[:], conv_bias).then_inc(ready, 16)
            sp.dma_start(edge[:], net.ins["c_edge"]).then_inc(ready, 16)

            def load(r):
                for h in range(HALVES):
                    wait_past(sp, normed if first else squared, 2 * (r - 1) + h + 1)
                    if first:
                        rows = source[P * h:P * h + P, :].rearrange("p (r w) -> p r w", w=COLS)
                        bands = source[P * h:P * h + P, :].rearrange("p (t n) -> p t n", n=TILE)
                        main = bands[:, r, :]
                        above = rows[:, (r * BAND + ROWS - 1) % ROWS, :]
                        below = rows[:, (r * BAND + BAND) % ROWS, :]
                    else:
                        main = source[r, h]
                        above = source[(r + BANDS - 1) % BANDS, h, :, (BAND - 1) * COLS:]
                        below = source[(r + 1) % BANDS, h, :, 0:COLS]
                    sp.dma_start(xt[:, h, 1:BAND + 1, :].rearrange("p r w -> p (r w)"), main).then_inc(loaded[h], 16)
                    sp.dma_start(xt[:, h, 0, :], above).then_inc(loaded[h], 16)
                    sp.dma_start(xt[:, h, BAND + 1, :], below).then_inc(loaded[h], 16)

            def regroup(r):
                for h in range(HALVES):
                    sp.wait_ge(u_ready, (2 * r + h + 1) * CHUNKS1)
                    wait_past(sp, conv_ready, (2 * (r - 1) + h + 1) * 4)
                    for b in range(GROUP):
                        for k in range(4):
                            sp.dma_start(uc[QUAD * k:QUAD * k + QUAD, h, b, :, :],
                                         u[QUAD * b:QUAD * b + QUAD, h, k:k + BAND - 1:2, :]).then_inc(uc_loaded[h], 16)

            def store(r):
                for h in range(HALVES):
                    sp.wait_ge(out_ready, (2 * r + h + 1) * CHUNKS2)
                    sp.dma_start(target[r, h], out[:, h, :]).then_inc(stored[h], 16)
            pipeline(sp, BANDS, [(3, store), (0, load), (1, regroup)])
            for h in range(HALVES):
                sp.wait_ge(stored[h], 16 * BANDS)

        @block.scalar
        def _(act):
            a = nc.scalar
            act.wait_ge(ready, 48)

            def squares(r):
                for h in range(HALVES):
                    wait_past(act, summed1, 2 * (r - 1) + h + 1)
                    if first:
                        act.wait_ge(normed, 2 * r + h + 1)
                        a.activation(sq[:, h, :], xn[:, h, :], ACT.Square).then_inc(squared, 1)
                    else:
                        act.wait_ge(loaded[h], 48 * r + 48)
                        wait_past(act, u_ready, (2 * (r - 1) + h + 1) * CHUNKS1)
                        src = xt[:, h].rearrange("p r w -> p (r w)")
                        a.activation(xn[:, h, :], src, ACT.Relu, bias=bias, scale=scale).then_inc(normed, 1)
                        a.activation(sq[:, h, :], src, ACT.Square, bias=bias, scale=scale).then_inc(squared, 1)

            def logarithms(r):
                act.wait_ge(normsq, r + 1)
                a.activation(l1[:], nc_[:], ACT.Ln, bias=1.0, scale=1.0)
                a.activation(l2[:], nc_[:], ACT.Ln, bias=1.0, scale=-1.0).then_inc(logs, 1)

            def evacuate(r, h):
                wait_past(act, out_ready, (2 * (r - 1) + h + 1) * CHUNKS2)
                wait_past(act, summed2, 2 * (r - 1) + h + 1)
                for k in range(4):
                    p, o = k // 2, k % 2
                    act.wait_ge(conv_ready, (2 * r + h) * 4 + k + 1)
                    src = conv[:, k % 2, :].rearrange("p (i w) -> p i w", i=2)
                    rows = slice(4 * p + o, 4 * p + o + 3, 2)
                    a.activation(v_sb[:, h, rows, :], src, ACT.Identity, bias=cb[:, 0:1])
                    a.activation(sqv[:, h, :].rearrange("p (r w) -> p r w", w=COLS)[:, rows, :], src, ACT.Square,
                                 bias=cb[:, 0:1]).then_inc(evacuated, 1)
            pipeline(act, BANDS, [(2, lambda r: evacuate(r, 0))] + ([(1, logarithms)] if first else []) +
                     [(2, lambda r: evacuate(r, 1)), (0, squares)])

        @block.tensor
        def _(pe):
            m = nc.tensor
            pe.wait_ge(ready, 48)

            def sum_squares(r):
                wait_past(pe, read1, r)
                for h in range(HALVES):
                    pe.wait_ge(squared, 2 * r + h + 1)
                    for k in range(HB):
                        q4 = QUAD * (k % 4)
                        last = m.matmul(pc1[q4:q4 + QUAD, h, :], c["ones"][:, k // 4, :], sq[:, h, P * k:P * k + P],
                                        start=(k < 4), stop=(k >= HB - 4), tile_position=(0, q4))
                    last.then_inc(summed1, 1)

            def spread_out(r):
                pe.wait_ge(factors2, r + 1)
                for h in range(HALVES):
                    for k in range(CHUNKS2):
                        n = (2 * r + h) * CHUNKS2 + k
                        wait_past(pe, out_ready, n - 1)
                        for j in range(4):
                            for z in range(2):
                                last = m.matmul(spread2[:, k % 2, P * j:P * j + P], c["sel"][:, BLOCKS * h + 4 * k + j, :],
                                                sp2[:, z, :].bitcast(F32R), start=(z == 0), stop=(z == 1))
                        last.then_inc(spread2_ready, 1)

            def convolve(r, h):
                pe.wait_ge(uc_loaded[h], (r + 1) * 256)
                for k in range(4):
                    p, o = k // 2, k % 2
                    wait_past(pe, evacuated, (2 * r + h) * 4 + k - 1)
                    for d in range(3):
                        for b in range(GROUP):
                            last = m.matmul(conv[QUAD * b:QUAD * b + QUAD, k % 2, :], w_sb[:, o, d, :],
                                            uc[:, h, b, 2 * p:2 * p + 2, d:d + COLS], start=(d == 0), stop=(d == 2),
                                            tile_position=(0, QUAD * b))
                    last.then_inc(conv_ready, 1)

            def spread_u(r):
                pe.wait_ge(factors1, r + 1)
                for h in range(HALVES):
                    for k in range(CHUNKS1):
                        n = (2 * r + h) * CHUNKS1 + k
                        wait_past(pe, u_ready, n - 1)
                        for j in range(4):
                            for z in range(2):
                                last = m.matmul(spread1[:, (h * CHUNKS1 + k) % 2, P * j:P * j + P], c["sel"][:, 4 * k + j, :],
                                                sp1[:, z, h, :].bitcast(F32R), start=(z == 0), stop=(z == 1))
                        last.then_inc(spread1_ready, 1)

            def sum_out(r):
                wait_past(pe, read2, r)
                for h in range(HALVES):
                    pe.wait_ge(evacuated, (2 * r + h + 1) * 4)
                    for k in range(BLOCKS):
                        b = BLOCKS * h + k
                        q4 = QUAD * (b % 4)
                        last = m.matmul(pc2[q4:q4 + QUAD, :], c["ones"][:, b // 4, :], sqv[:, h, P * k:P * k + P],
                                        start=(b < 4), stop=(b >= 2 * BLOCKS - 4), tile_position=(0, q4))
                    last.then_inc(summed2, 1)
            pipeline(pe, BANDS, [(1, sum_squares), (3, spread_out), (2, lambda r: convolve(r, 0)),
                                 (2, lambda r: convolve(r, 1)), (1, spread_u), (2, sum_out)])

        @block.vector
        def _(dve):
            v = nc.vector
            v.memset(u[:, :, :, 0:1], 0.0)
            v.memset(u[:, :, :, PAD - 1:PAD], 0.0)
            v.drain()
            dve.wait_ge(ready, 48)

            def affine(r):
                for h in range(HALVES):
                    dve.wait_ge(loaded[h], 48 * r + 48)
                    wait_past(dve, squared, 2 * (r - 1) + h + 1)
                    wait_past(dve, u_ready, (2 * (r - 1) + h + 1) * CHUNKS1)
                    v.tensor_scalar(xn[:, h, :], xt[:, h].rearrange("p r w -> p (r w)"), scale[:, h:h + 1],
                                    bias[:, h:h + 1], ALU.mult, ALU.add).then_inc(normed, 1)

            def factors_u(r):
                dve.wait_ge(summed1, 2 * r + 2)
                v.tensor_copy(n2[:], pc1[:]).then_inc(read1, 1)
                v.drain()
                v.tensor_scalar(q[:], n2[:], EPS_NORM * EPS_NORM, None, ALU.max)
                v.drain()
                rsqrt_steps(v, rn[:], q[:], t_[:])
                if first:
                    v.tensor_tensor(nc_[:], q[:], rn[:], ALU.mult)
                    v.drain()
                    v.tensor_scalar(nc_[:], nc_[:], CLIP, None, ALU.min).then_inc(normsq, 1)
                    v.tensor_scalar(xx[:], q[:], 0.05, None, ALU.min)
                    v.drain()
                    v.tensor_scalar(pl[:], xx[:], 1.0 / 11, None, ALU.mult)
                    for k in (9, 7, 5, 3):
                        v.drain()
                        v.scalar_tensor_tensor(pl[:], pl[:], 1.0 / k, xx[:], ALU.add, ALU.mult)
                    dve.wait_ge(logs, r + 1)
                    v.tensor_tensor(sl[:], l1[:], l2[:], ALU.subtract)
                    v.drain()
                    v.scalar_tensor_tensor(sl[:], sl[:], 0.5, rn[:], ALU.mult, ALU.mult)
                    v.tensor_scalar(t_[:], q[:], 0.04, None, ALU.is_lt)
                    v.drain()
                    v.scalar_tensor_tensor(pl[:], pl[:], 1.0, sl[:], ALU.add, ALU.subtract)
                    v.drain()
                    v.tensor_tensor(pl[:], pl[:], t_[:], ALU.mult)
                    v.drain()
                    v.tensor_tensor(sl[:], sl[:], pl[:], ALU.add)
                else:
                    v.tensor_scalar(sl[:], rn[:], ATANH_MAX, 1.0, ALU.mult, ALU.min).then_inc(normsq, 1)
                v.drain()
                v.tensor_scalar(sl[:], sl[:], edge[:, bass.ds(r, 1)], None, ALU.mult)
                v.drain()
                wait_past(dve, spread1_ready, 2 * r * CHUNKS1)
                split_hi_lo(v, sp1[:, 0], sp1[:, 1], sl[:]).then_inc(factors1, 1)

            def products_out(r):
                for h in range(HALVES):
                    wait_past(dve, stored[h], 16 * r)
                    for k in range(CHUNKS2):
                        dve.wait_ge(spread2_ready, (2 * r + h) * CHUNKS2 + k + 1)
                        cols = slice(BANK * k, BANK * k + BANK)
                        v.tensor_tensor(out[:, h, cols], v_sb[:, h].rearrange("p r w -> p (r w)")[:, cols],
                                        spread2[:, k % 2, :], ALU.mult).then_inc(out_ready, 1)
                    v.drain()
                    for k in range(CHUNKS2):
                        v.bn_stats(part[:, h, 6 * k:6 * k + 6], out[:, h, BANK * k:BANK * k + BANK])
                    v.drain()
                    v.tensor_copy(stats[:, h, r, :], part[:, h, :])

            def products_u(r):
                for h in range(HALVES):
                    wait_past(dve, uc_loaded[h], 256 * r)
                    if not first:
                        dve.wait_ge(normed, 2 * r + h + 1)
                    for k in range(CHUNKS1):
                        dve.wait_ge(spread1_ready, (2 * r + h) * CHUNKS1 + k + 1)
                        v.tensor_tensor(u[:, h, 2 * k:2 * k + 2, 1:COLS + 1],
                                        xn[:, h, BANK * k:BANK * k + BANK].rearrange("p (r w) -> p r w", w=COLS),
                                        spread1[:, (h * CHUNKS1 + k) % 2, :].rearrange("p (r w) -> p r w", w=COLS),
                                        ALU.mult).then_inc(u_ready, 1)

            def factors_out(r):
                dve.wait_ge(summed2, 2 * r + 2)
                s, q2, y2, t2 = m2[:], q[:, 0, :], rn[:, 0, :], t_[:, 0, :]
                v.tensor_scalar(q2, pc2, EPS_NORM * EPS_NORM, None, ALU.max).then_inc(read2, 1)
                v.drain()
                rsqrt_steps(v, y2, q2, t2)
                v.tensor_scalar(s, y2, ATANH_MAX, 1.0, ALU.mult, ALU.min)
                v.drain()
                wait_past(dve, spread2_ready, 2 * r * CHUNKS2)
                split_hi_lo(v, sp2[:, 0, :], sp2[:, 1, :], s).then_inc(factors2, 1)
            pipeline(dve, BANDS, [(3, factors_out), (3, products_out), (1, factors_u), (1, products_u)] +
                     ([(0, affine)] if first else []))


def residual_layer(net, x_rows, source, scale, bias, target, stats):
    nc, c = net.nc, net.c
    CHUNKS = TILE // BANK
    with ExitStack() as local:
        def sb(name, shape, dt=F32):
            return net.sb(local, name, shape, dt)
        xt, sqh, sqr, o_sb, x1 = (sb(k, [P, HALVES, TILE]) for k in ("xt", "sqh", "sqr", "o", "x1"))
        tt, r_sb = (sb(k, [P, 2, HALVES, TILE]) for k in ("tt", "r"))
        nh, nr, y, t_, m, n, th = (sb(k, [P, P]) for k in ("nh", "nr", "y", "t", "m", "n", "th"))
        parts = sb("parts", [P, 2, P])
        part = sb("part", [P, HALVES, CHUNKS * 6])
        sums = net.ps(local, "sums", [P, 2, BANK])[:, :, 0:P]
        spread = net.ps(local, "spread", [P, 2, BANK])

        def sem(name):
            return net.sem(local, name)
        x_loaded, stored = ([sem(f"{k}{h}") for h in range(2)] for k in ("x_loaded", "stored"))
        loaded = [[sem(f"loaded{parity}{h}") for h in range(2)] for parity in range(2)]
        rectified, squared, summed, read, norms, tanhs, factors, spread_ready, o_ready, x1_ready, measured = (
            sem(k) for k in ("rectified", "squared", "summed", "read", "norms", "tanhs", "factors", "spread_ready",
                             "o_ready", "x1_ready", "measured"))
        block = local.enter_context(nc.Block())

        @block.sync
        def _(sp):
            def load(r, parity):
                for h in range(HALVES):
                    wait_past(sp, squared, 2 * (r - 2) + h + 1)
                    sp.dma_start(tt[:, parity, h, :], source[r, h]).then_inc(loaded[parity][h], 16)

            def load_x(r, _):
                for h in range(HALVES):
                    wait_past(sp, x1_ready, 2 * (r - 1) + h + 1)
                    bands = x_rows[P * h:P * h + P, :].rearrange("p (t n) -> p t n", n=TILE)
                    sp.dma_start(xt[:, h, :], bands[:, r, :]).then_inc(x_loaded[h], 16)

            def store(r, _):
                for h in range(HALVES):
                    sp.wait_ge(x1_ready, 2 * r + h + 1)
                    sp.dma_start(target[r, h], x1[:, h, :]).then_inc(stored[h], 16)
            pipeline_by_two(sp, BANDS, [(0, load), (2, store), (1, load_x)])
            for h in range(HALVES):
                sp.wait_ge(stored[h], 16 * BANDS)

        @block.scalar
        def _(act):
            a = nc.scalar

            def squares(r, parity, h):
                act.wait_ge(loaded[parity][h], 8 * (r - parity) + 16)
                wait_past(act, o_ready, (2 * (r - 2) + h + 1) * CHUNKS)
                wait_past(act, squared, 2 * (r - 2) + h + 1)
                t, rectified_t = tt[:, parity, h, :], r_sb[:, parity, h, :]
                a.activation(rectified_t, t, ACT.Relu, bias=bias, scale=scale).then_inc(rectified, 1)
                wait_past(act, summed, 2 * (r - 1) + h + 1)
                a.activation(sqh[:, h, :], t, ACT.Square, bias=bias, scale=scale)
                act.wait_ge(rectified, 2 * r + h + 1)
                a.activation(sqr[:, h, :], rectified_t, ACT.Square).then_inc(squared, 1)

            def tangents(r, _):
                act.wait_ge(norms, r + 1)
                a.activation(th[:], n[:], ACT.Tanh).then_inc(tanhs, 1)
            pipeline_by_two(act, BANDS, [(0, lambda r, parity: squares(r, parity, 0)), (1, tangents),
                                         (0, lambda r, parity: squares(r, parity, 1))])

        @block.tensor
        def _(pe):
            mm = nc.tensor

            def sum_squares(r):
                wait_past(pe, read, r)
                for h in range(HALVES):
                    pe.wait_ge(squared, 2 * r + h + 1)
                    for kind, src in enumerate((sqh, sqr)):
                        for k in range(BLOCKS):
                            b = BLOCKS * h + k
                            q4 = QUAD * (b % 4)
                            last = mm.matmul(sums[q4:q4 + QUAD, kind, :], c["ones"][:, b // 4, :], src[:, h, P * k:P * k + P],
                                             start=(b < 4), stop=(b >= 2 * BLOCKS - 4), tile_position=(0, q4))
                    last.then_inc(summed, 1)

            def spread_factors(r):
                pe.wait_ge(factors, r + 1)
                for h in range(HALVES):
                    for k in range(CHUNKS):
                        wait_past(pe, o_ready, (2 * r + h) * CHUNKS + k - 1)
                        for j in range(4):
                            for z in range(2):
                                last = mm.matmul(spread[:, k % 2, P * j:P * j + P], c["sel"][:, BLOCKS * h + 4 * k + j, :],
                                                 parts[:, z, :].bitcast(F32R), start=(z == 0), stop=(z == 1))
                        last.then_inc(spread_ready, 1)
            pipeline(pe, BANDS, [(1, spread_factors), (0, sum_squares)])

        @block.gpsimd
        def _(pool):
            def add(r):
                for h in range(HALVES):
                    pool.wait_ge(o_ready, (2 * r + h + 1) * CHUNKS)
                    pool.wait_ge(x_loaded[h], 16 * r + 16)
                    wait_past(pool, stored[h], 16 * r)
                    wait_past(pool, measured, 2 * (r - 1) + h + 1)
                    nc.gpsimd.tensor_tensor(x1[:, h, :], o_sb[:, h, :], xt[:, h, :], ALU.add).then_inc(x1_ready, 1)
            pipeline(pool, BANDS, [(0, add)])

        @block.vector
        def _(dve):
            v = nc.vector
            def products(r, parity):
                for h in range(HALVES):
                    wait_past(dve, x1_ready, 2 * (r - 1) + h + 1)
                    for k in range(CHUNKS):
                        cols = slice(BANK * k, BANK * k + BANK)
                        dve.wait_ge(spread_ready, (2 * r + h) * CHUNKS + k + 1)
                        v.tensor_tensor(o_sb[:, h, cols], r_sb[:, parity, h, cols], spread[:, k % 2, :], ALU.mult).then_inc(o_ready, 1)

            def factor(r, _):
                dve.wait_ge(summed, 2 * r + 2)
                v.tensor_scalar(nh[:], sums[:, 0], EPS_NORM * EPS_NORM, None, ALU.max)
                v.tensor_scalar(nr[:], sums[:, 1], 1e-30, None, ALU.max).then_inc(read, 1)
                v.drain()
                rsqrt_steps(v, y[:], nh[:], t_[:])
                v.tensor_scalar(m[:], y[:], ATANH_MAX, 1.0, ALU.mult, ALU.min)
                v.drain()
                rsqrt_steps(v, y[:], nr[:], t_[:])
                v.tensor_tensor(nr[:], nr[:], y[:], ALU.mult)
                v.drain()
                v.tensor_tensor(nr[:], nr[:], m[:], ALU.mult)
                v.drain()
                v.tensor_scalar(n[:], nr[:], EPS_NORM, None, ALU.max).then_inc(norms, 1)
                v.drain()
                v.reciprocal(y[:], n[:])
                v.drain()
                v.tensor_tensor(m[:], m[:], y[:], ALU.mult)
                v.drain()
                dve.wait_ge(tanhs, r + 1)
                v.scalar_tensor_tensor(m[:], th[:], MAX_NORM, m[:], ALU.min, ALU.mult)
                v.drain()
                wait_past(dve, spread_ready, 2 * r * CHUNKS)
                split_hi_lo(v, parts[:, 0, :], parts[:, 1, :], m[:]).then_inc(factors, 1)

            def measure(r, _):
                for h in range(HALVES):
                    dve.wait_ge(x1_ready, 2 * r + h + 1)
                    for k in range(CHUNKS):
                        last = v.bn_stats(part[:, h, 6 * k:6 * k + 6], x1[:, h, BANK * k:BANK * k + BANK])
                    last.then_inc(measured, 1)
                    v.drain()
                    v.tensor_copy(stats[:, h, r, :], part[:, h, :])
            pipeline_by_two(dve, BANDS, [(2, measure), (1, factor), (1, products)])


MODES = 4
KP = CH * MODES
SUB = ROWS // 2


def spread_table(net, vectors, table):
    nc = net.nc
    with ExitStack() as local:
        wide = net.sb(local, "wide", [P, HALVES, P])
        rows = net.ps(local, "rows", [P, HALVES, P])
        ready, done = net.sem(local, "wide_ready"), net.sem(local, "rows_ready")
        block = local.enter_context(nc.Block())

        @block.vector
        def _(dve):
            nc.vector.tensor_copy(wide[:], vectors.unsqueeze(2).to_broadcast([P, HALVES, P])).then_inc(ready, 1)
            dve.wait_ge(done, 1)
            nc.vector.tensor_copy(table.rearrange("p (h n) -> p h n", h=HALVES), rows[:])

        @block.tensor
        def _(pe):
            pe.wait_ge(ready, 1)
            for h in range(HALVES):
                last = nc.tensor.matmul(rows[:, h, :], wide[:, h, :], net.c["ident"][:], start=True, stop=True)
            last.then_inc(done, 1)


def pole_kernels(net, g1, g2):
    nc, ins = net.nc, net.ins
    N = CH * KP
    with ExitStack() as local:
        wr, wi, den, re, im = (net.sb(local, k, [P, N]) for k in ("wr", "wi", "den", "re", "im"))
        dft = net.sb(local, "dft", [P, 3, P])
        grid, lam = net.sb(local, "grid", [P, 2, 3]), net.sb(local, "lam", [P, 2])
        freq = net.sb(local, "freq", [P, 1])
        acc = net.ps(local, "acc", [P, 2, 2, BANK])
        consts, poles, inverse, transformed, kept = (net.sem(local, k) for k in
                                                     ("consts", "poles", "inverse", "transformed", "kept"))
        block = local.enter_context(nc.Block())
        CHUNKS = N // BANK
        PER = BANK // KP

        @block.sync
        def _(sp):
            sp.dma_start(dft[:], ins["c_dft"]).then_inc(consts, 16)
            sp.dma_start(freq[:], ins["c_freq"]).then_inc(consts, 16)
            for n, name in enumerate(("x_grid", "t_grid")):
                sp.dma_start(grid[:, n, :], ins[name][:, 0:3].to_broadcast([P, 3])).then_inc(consts, 16)
            for n, name in enumerate(("wp1", "wp2")):
                wait_past(sp, inverse, n)
                sp.dma_start(wr[:], ins[name + "r"].to_broadcast([P, N])).then_inc(poles, 16)
                sp.dma_start(wi[:], ins[name + "i"].to_broadcast([P, N])).then_inc(poles, 16)

        @block.vector
        def _(dve):
            v = nc.vector
            dve.wait_ge(consts, 64)
            v.tensor_tensor(lam[:], grid[:, :, 2], grid[:, :, 0], ALU.subtract)
            v.drain()
            v.reciprocal(lam[:], lam[:])
            v.drain()
            v.tensor_scalar(lam[:], lam[:], freq[:, 0:1], 2.0 * np.pi, ALU.mult, ALU.mult)
            v.drain()
            for n in range(2):
                dve.wait_ge(poles, 32 * n + 32)
                wait_past(dve, transformed, n * CHUNKS)
                v.tensor_scalar(wi[:], wi[:], lam[:, n:n + 1], None, ALU.subtract)
                v.tensor_tensor(re[:], wr[:], wr[:], ALU.mult)
                v.drain()
                v.tensor_tensor(den[:], wi[:], wi[:], ALU.mult)
                v.drain()
                v.tensor_tensor(den[:], den[:], re[:], ALU.add)
                v.drain()
                v.reciprocal(den[:], den[:])
                v.drain()
                v.tensor_tensor(re[:], wr[:], den[:], ALU.mult)
                v.scalar_tensor_tensor(im[:], wi[:], -1.0, den[:], ALU.mult, ALU.mult).then_inc(inverse, 1)
                v.drain()

        @block.tensor
        def _(pe):
            m = nc.tensor
            for n in range(2):
                pe.wait_ge(inverse, n + 1)
                for k in range(CHUNKS):
                    wait_past(pe, kept, n * CHUNKS + k - 1)
                    cols = slice(BANK * k, BANK * k + BANK)
                    m.matmul(acc[:, k % 2, 0, :], dft[:, 0, :], re[:, cols], start=True, stop=False)
                    m.matmul(acc[:, k % 2, 0, :], dft[:, 1, :], im[:, cols], start=False, stop=True)
                    m.matmul(acc[:, k % 2, 1, :], dft[:, 0, :], im[:, cols], start=True, stop=False)
                    m.matmul(acc[:, k % 2, 1, :], dft[:, 2, :], re[:, cols], start=False, stop=True).then_inc(transformed, 1)

        @block.scalar
        def _(act):
            a = nc.scalar
            for n in range(2):
                for k in range(CHUNKS):
                    act.wait_ge(transformed, n * CHUNKS + k + 1)
                    i = slice(PER * k, PER * k + PER)
                    real, imag = (acc[:, k % 2, z, :].rearrange("p (i m) -> p i m", m=KP) for z in range(2))
                    if n == 0:
                        a.copy(g1[:, i, 0, :], real)
                        a.copy(g1[:, i, 1, :], imag).then_inc(kept, 1)
                    else:
                        a.mul(g2[:, i, 0, :], imag, -1.0)
                        a.copy(g2[:, i, 1, :], real)
                        a.copy(g2[:, i, 2, :], imag).then_inc(kept, 1)


def residues(net, source, scale_table, bias_table, g1, g2, coef):
    nc, ins = net.nc, net.ins
    with ExitStack() as local:
        rows = net.sb(local, "rows", [P, 2, IMAGES, COLS])
        xs = net.sb(local, "xs", [P, IMAGES, SUB])
        t_sb = net.sb(local, "t_sb", [P, 2, IMAGES, 2, KP])
        res = net.sb(local, "res", [P, CH, 2, MODES])
        prod = net.sb(local, "prod", [P, 4, 2, 2, 2, KP])
        acc = net.sb(local, "acc", [P, 4, 2, 2, 2, KP])
        mask = net.sb(local, "mask", [P, KP])
        t_ps = net.ps(local, "t_ps", [P, 2, 2, 2, KP])
        o_ps = net.ps(local, "o_ps", [P, 4, 2, 2, KP])
        consts, t_ready, t_kept, o_ready, weighted, added, sampled = (net.sem(local, k) for k in (
            "consts", "t_ready", "t_kept", "o_ready", "weighted", "added", "sampled"))
        cleared = net.sem(local, "cleared")
        loaded = [net.sem(local, f"loaded{j}") for j in range(2)]
        block = local.enter_context(nc.Block())
        PAIRS = CH // 2

        @block.sync
        def _(sp):
            sp.dma_start(res[:], ins["res"]).then_inc(consts, 16)
            sp.dma_start(mask[:], ins["c_mask"]).then_inc(consts, 16)

            def load(t):
                for j in range(2):
                    wait_past(sp, sampled, (2 * (t - 1) + j + 1))
                    for b in range(IMAGES):
                        src = source[:, b // GROUP, CH * (b % GROUP) + 2 * t + j, :]
                        src = src.rearrange("r (y z w) -> r y z w", z=2, w=COLS)[:, :, 0, :]
                        sp.dma_start(rows[:, j, b, :], src).then_inc(loaded[j], 16)
            pipeline(sp, PAIRS, [(0, load)])

        @block.vector
        def _(dve):
            v = nc.vector

            def sample(t, j):
                dve.wait_ge(loaded[j], 128 * t + 128)
                wait_past(dve, t_ready, 4 * (2 * t + j))
                for b in range(IMAGES):
                    col = b * CH + 2 * t + j
                    last = v.tensor_scalar(xs[:, b, :], rows[:, j, b, :].rearrange("p (x z) -> p x z", z=2)[:, :, 0],
                                           scale_table[:, bass.ds(col, 1)], bias_table[:, bass.ds(col, 1)], ALU.mult, ALU.add)
                last.then_inc(sampled, 1)

            def weight(t, j):
                i = 2 * t + j
                for b in range(4):
                    dve.wait_ge(o_ready, 4 * i + b + 1)
                    wait_past(dve, added, 4 * (i - 1) + b + 1)
                    for z in range(2):
                        last = v.tensor_tensor(prod[:, b, z].rearrange("p c z (k q) -> p (c z) k q", q=MODES),
                                               o_ps[:, b].rearrange("p c z (k q) -> p (c z) k q", q=MODES),
                                               res[:, i, z, :].unsqueeze(1).unsqueeze(1).to_broadcast([P, 4, CH, MODES]),
                                               ALU.mult)
                    last.then_inc(weighted, 1)
            dve.wait_ge(consts, 32)

            v.memset(acc[:], 0.0).then_inc(cleared, 1)
            pipeline(dve, PAIRS, [(0, lambda t: sample(t, 0)), (1, lambda t: weight(t, 1)),
                                  (0, lambda t: sample(t, 1)), (0, lambda t: weight(t, 0))])
            dve.wait_ge(added, 4 * CH)
            for b in range(4):
                re, im = coef[:, 2 * b:2 * b + 2, 0, :], coef[:, 2 * b:2 * b + 2, 1, :]
                v.tensor_tensor(re, acc[:, b, 0, :, 0, :], acc[:, b, 1, :, 1, :], ALU.subtract)
                v.tensor_tensor(im, acc[:, b, 0, :, 1, :], acc[:, b, 1, :, 0, :], ALU.add)
            v.drain()
            flat = coef.rearrange("p a z n -> p (a z) n")
            v.tensor_tensor(flat, flat, mask[:].unsqueeze(1).to_broadcast([P, 2 * IMAGES, KP]), ALU.mult)
            v.drain()

        @block.gpsimd
        def _(pool):
            pool.wait_ge(cleared, 1)

            def add(t):
                for j in range(2):
                    i = 2 * t + j
                    for b in range(4):
                        pool.wait_ge(weighted, 4 * i + b + 1)
                        wait_past(pool, added, 4 * (i - 1) + b + 1)
                        dst = acc[:, b].rearrange("p z c y n -> p (z c y n)")
                        nc.gpsimd.tensor_tensor(dst, dst, prod[:, b].rearrange("p z c y n -> p (z c y n)"),
                                                ALU.add).then_inc(added, 1)
            pipeline(pool, PAIRS, [(0, add)])

        @block.scalar
        def _(act):
            def keep(t):
                for j in range(2):
                    i = 2 * t + j
                    for b in range(4):
                        act.wait_ge(t_ready, 4 * i + b + 1)
                        wait_past(act, o_ready, 4 * (i - 2) + b + 1)
                        nc.scalar.copy(t_sb[:, j, 2 * b:2 * b + 2], t_ps[:, b % 2]).then_inc(t_kept, 1)
            pipeline(act, PAIRS, [(0, keep)])

        @block.tensor
        def _(pe):
            m = nc.tensor

            def first(t, j):
                i = 2 * t + j
                pe.wait_ge(sampled, i + 1)
                for b in range(4):
                    wait_past(pe, t_kept, 4 * i + b - 1)
                    for k in range(2):
                        last = m.matmul(t_ps[:, b % 2, k].rearrange("p z n -> p (z n)"), xs[:, 2 * b + k, :],
                                        g1[:, i].rearrange("p z n -> p (z n)"), start=True, stop=True)
                    last.then_inc(t_ready, 1)

            def second(t, j):
                i = 2 * t + j
                for b in range(4):
                    pe.wait_ge(t_kept, 4 * i + b + 1)
                    wait_past(pe, weighted, 4 * (i - 1) + b + 1)
                    for k in range(2):
                        dst = o_ps[:, b, k].rearrange("p z n -> p (z n)")
                        m.matmul(dst, t_sb[:, j, 2 * b + k, 0, :], g2[:, i, 1:3].rearrange("p z n -> p (z n)"),
                                 start=True, stop=False)
                        last = m.matmul(dst, t_sb[:, j, 2 * b + k, 1, :], g2[:, i, 0:2].rearrange("p z n -> p (z n)"),
                                        start=False, stop=True)
                    last.then_inc(o_ready, 1)

            pipeline(pe, PAIRS, [(0, lambda t: first(t, 0)), (1, lambda t: second(t, 1)),
                                 (0, lambda t: first(t, 1)), (0, lambda t: second(t, 0))])


TWO_PI_1 = 6.28125
TWO_PI_2 = float(np.float32(np.round((2 * np.pi - TWO_PI_1) * 2 ** 21) / 2 ** 21))
TWO_PI_3 = float(2 * np.pi - TWO_PI_1 - TWO_PI_2)
ROUND = 1.5 * 2 ** 23
PI_BELOW = 3.1415925


def evaluate_residues(net, source, coef, target, stats):
    nc, ins = net.nc, net.ins
    with ExitStack() as local:
        w = net.sb(local, "w", [P, 2, 2, CH])
        z = net.sb(local, "z", [P, 2, COLS])
        grow, ang, turns, sine, cosine = (net.sb(local, k, [P, 2, COLS]) for k in ("grow", "ang", "turns", "sin", "cos"))
        e1, e2 = net.sb(local, "e1", [P, 2, 3, COLS]), net.sb(local, "e2", [P, 2, 2, COLS])
        tmp = net.sb(local, "tmp", [P, 2, 2, COLS])
        xin, xout = net.sb(local, "xin", [P, 2, IMAGES, BANK]), net.sb(local, "xout", [P, 2, IMAGES, BANK])
        part = net.sb(local, "part", [P, IMAGES * 6])
        half_pi = net.sb(local, "half_pi", [P, 1])
        t_ps, o_ps = net.ps(local, "t_ps", [P, 2, BANK]), net.ps(local, "o_ps", [P, 2, BANK])
        consts, angles, sines, grown, waves, t_ready, t_kept, o_ready, summed, measured = (net.sem(local, k) for k in (
            "consts", "angles", "sines", "grown", "waves", "t_ready", "t_kept", "o_ready", "summed", "measured"))
        loaded = [net.sem(local, f"loaded{j}") for j in range(2)]
        stored = [net.sem(local, f"stored{j}") for j in range(2)]
        block = local.enter_context(nc.Block())
        PAIRS = CH // 2

        def rows_of(tensor, a, i):
            return tensor[:, a // GROUP, CH * (a % GROUP) + i, :].rearrange("r (z n) -> r z n", n=2 * COLS)

        @block.sync
        def _(sp):
            sp.dma_start(w[:], ins["poles"]).then_inc(consts, 16)
            sp.dma_start(z[:, 0, :], ins["x_grid"].to_broadcast([P, COLS])).then_inc(consts, 16)
            sp.dma_start(z[:, 1, :], ins["t_grid"].to_broadcast([P, COLS])).then_inc(consts, 16)

            def load(t):
                for j in range(2):
                    wait_past(sp, summed, IMAGES * (2 * (t - 1) + j + 1))
                    for a in range(IMAGES):
                        sp.dma_start(xin[:, j, a, :], rows_of(source, a, 2 * t + j)).then_inc(loaded[j], 16)

            def store(t):
                for j in range(2):
                    for a in range(IMAGES):
                        sp.wait_ge(summed, IMAGES * (2 * t + j) + a + 1)
                        sp.dma_start(rows_of(target, a, 2 * t + j), xout[:, j, a, :]).then_inc(stored[j], 16)
            pipeline(sp, PAIRS, [(0, load), (1, store)])
            for j in range(2):
                sp.wait_ge(stored[j], 16 * IMAGES * PAIRS)

        @block.scalar
        def _(act):
            s = nc.scalar
            act.wait_ge(consts, 48)

            def growth(t, j):
                i = 2 * t + j
                wait_past(act, waves, i)
                for n in range(2):
                    last = s.activation(grow[:, n, :], z[:, n, :], ACT.Exp, scale=w[:, n, 0, bass.ds(i, 1)])
                last.then_inc(grown, 1)

            def waves_of(t, j):
                i = 2 * t + j
                act.wait_ge(angles, i + 1)
                s.activation(sine[:], ang[:], ACT.Sin)
                s.activation(cosine[:], turns[:], ACT.Sin, bias=half_pi[:, 0:1], scale=-1.0).then_inc(sines, 1)

            def keep(t, j, images):
                for a in images:
                    n = IMAGES * (2 * t + j) + a
                    act.wait_ge(t_ready, n + 1)
                    wait_past(act, o_ready, n - 1)
                    s.copy(tmp[:, a % 2].rearrange("p z n -> p (z n)"), t_ps[:, a % 2, :]).then_inc(t_kept, 1)
            stages = []
            for j in range(2):
                stages += [(1, lambda t, j=j: keep(t, j, range(0, 2))), (0, lambda t, j=j: growth(t, j)),
                           (1, lambda t, j=j: keep(t, j, range(2, 5))), (0, lambda t, j=j: waves_of(t, j)),
                           (1, lambda t, j=j: keep(t, j, range(5, IMAGES)))]
            pipeline(act, PAIRS, stages)

        @block.vector
        def _(dve):
            v = nc.vector
            v.memset(half_pi[:], 0.5 * np.pi)
            v.drain()
            dve.wait_ge(consts, 48)

            def prepare(t, j):
                i = 2 * t + j
                wait_past(dve, sines, i)
                for n in range(2):
                    v.tensor_scalar(ang[:, n, :], z[:, n, :], w[:, n, 1, bass.ds(i, 1)], None, ALU.mult)
                v.drain()
                v.tensor_scalar(turns[:], ang[:], float(1 / (2 * np.pi)), ROUND, ALU.mult, ALU.add)
                v.drain()
                v.tensor_scalar(turns[:], turns[:], ROUND, None, ALU.subtract)
                for c in (TWO_PI_1, TWO_PI_2, TWO_PI_3):
                    v.drain()
                    v.scalar_tensor_tensor(ang[:], turns[:], -c, ang[:], ALU.mult, ALU.add)
                v.drain()
                v.tensor_scalar(ang[:], ang[:], PI_BELOW, -PI_BELOW, ALU.min, ALU.max)
                v.drain()
                v.scalar_tensor_tensor(turns[:], ang[:], -1.0, ang[:], ALU.mult, ALU.max).then_inc(angles, 1)

            def combine(t, j):
                i = 2 * t + j
                dve.wait_ge(sines, i + 1)
                dve.wait_ge(grown, i + 1)
                wait_past(dve, o_ready, IMAGES * (i - 1))
                v.tensor_tensor(e1[:, j, 1, :], grow[:, 0, :], cosine[:, 0, :], ALU.mult)
                v.tensor_tensor(e1[:, j, 2, :], grow[:, 0, :], sine[:, 0, :], ALU.mult)
                v.scalar_tensor_tensor(e1[:, j, 0, :], grow[:, 0, :], -1.0, sine[:, 0, :], ALU.mult, ALU.mult)
                v.tensor_tensor(e2[:, j, 0, :], grow[:, 1, :], cosine[:, 1, :], ALU.mult)
                v.scalar_tensor_tensor(e2[:, j, 1, :], grow[:, 1, :], -1.0, sine[:, 1, :], ALU.mult, ALU.mult).then_inc(waves, 1)

            def add(t, j):
                dve.wait_ge(loaded[j], 16 * IMAGES * (t + 1))
                wait_past(dve, stored[j], 16 * IMAGES * t)
                for a in range(IMAGES):
                    dve.wait_ge(o_ready, IMAGES * (2 * t + j) + a + 1)
                    v.scalar_tensor_tensor(xout[:, j, a, :], o_ps[:, a % 2, :], 1.0 / (SUB * SUB), xin[:, j, a, :],
                                           ALU.mult, ALU.add).then_inc(summed, 1)
                v.drain()
                for a in range(IMAGES):
                    v.bn_stats(part[:, 6 * a:6 * a + 6], xout[:, j, a, :])
                v.drain()
                v.tensor_copy(stats[:, 2 * t + j, :], part[:])
                v.drain()
            pipeline(dve, PAIRS, [(0, lambda t: prepare(t, 0)), (1, lambda t: add(t, 0)), (0, lambda t: combine(t, 0)),
                                  (0, lambda t: prepare(t, 1)), (1, lambda t: add(t, 1)), (0, lambda t: combine(t, 1))])

        @block.tensor
        def _(pe):
            m = nc.tensor

            def contract(t, j):
                i = 2 * t + j
                pe.wait_ge(waves, i + 1)

                def modes(a):
                    n = IMAGES * i + a
                    wait_past(pe, t_kept, n - 1)
                    m.matmul(t_ps[:, a % 2, :], coef[:, a, 0, :], e1[:, j, 1:3].rearrange("p z n -> p (z n)"),
                             start=True, stop=False)
                    m.matmul(t_ps[:, a % 2, :], coef[:, a, 1, :], e1[:, j, 0:2].rearrange("p z n -> p (z n)"),
                             start=False, stop=True).then_inc(t_ready, 1)

                def image(a):
                    n = IMAGES * i + a
                    pe.wait_ge(t_kept, n + 1)
                    wait_past(pe, summed, n - 1)
                    for s in range(2):
                        dst = o_ps[:, a % 2, COLS * s:COLS * s + COLS]
                        m.matmul(dst, tmp[:, a % 2, 0, s::2], e2[:, j, 0, :], start=True, stop=False)
                        last = m.matmul(dst, tmp[:, a % 2, 1, s::2], e2[:, j, 1, :], start=False, stop=True)
                    last.then_inc(o_ready, 1)
                modes(0)
                for a in range(IMAGES):
                    if a + 1 < IMAGES:
                        modes(a + 1)
                    image(a)
            pipeline(pe, PAIRS, [(1, lambda t: contract(t, 0)), (1, lambda t: contract(t, 1))])


def norm_vectors_by_image(net, stats, scale, bias):
    nc, c = net.nc, net.c
    N = CH * IMAGES
    GROUPS = CH // 2
    with ExitStack() as local:
        mean, var, d, e, g, y, t = (net.sb(local, k, [P, CH, IMAGES]) for k in ("mean", "var", "d", "e", "g", "y", "t"))
        ones = net.sb(local, "ones", [P, P])
        pick = net.sb(local, "pick", [P, P])
        pm = net.ps(local, "pm", [P, 2, BANK])
        s_mean, s_gm, s_e, s_gv = (net.sem(local, k) for k in ("mean", "gmean", "spread", "gvar"))
        block = local.enter_context(nc.Block())
        flat = lambda a: a[:].rearrange("p i a -> p (i a)")

        @block.tensor
        def _(pe):
            pe.wait_ge(s_mean, 1)
            nc.tensor.matmul(pm[:, 0, 0:N], ones[:], flat(mean), start=True, stop=True).then_inc(s_gm, 1)
            pe.wait_ge(s_e, 1)
            nc.tensor.matmul(pm[:, 1, 0:N], ones[:], flat(e), start=True, stop=True).then_inc(s_gv, 1)

        @block.vector
        def _(dve):
            v = nc.vector
            six = stats.rearrange("p i (a s) -> p i a s", s=6)

            def over_pairs(dst, src):
                s4 = src.rearrange("p (g two a) -> p g two a", two=2, a=IMAGES)
                d4 = dst[:].rearrange("p (g two) a -> p g two a", two=2)
                v.tensor_copy(flat(t), src)
                v.drain()
                t4 = t[:].rearrange("p (g two) a -> p g two a", two=2)
                for k in range(2):
                    v.tensor_tensor(d4[:, :, k, :], t4[:, :, 0, :], t4[:, :, 1, :], ALU.add)
                v.drain()
            v.memset(ones[:], 0.5 / P)
            v.tensor_tensor(mean[:], six[:, :, :, 1], six[:, :, :, 4], ALU.add)
            v.tensor_tensor(d[:], six[:, :, :, 1], six[:, :, :, 4], ALU.subtract)
            v.tensor_tensor(var[:], six[:, :, :, 2], six[:, :, :, 5], ALU.add)
            v.drain()
            v.tensor_scalar(mean[:], mean[:], 0.5, None, ALU.mult).then_inc(s_mean, 1)
            v.tensor_tensor(d[:], d[:], d[:], ALU.mult)
            v.drain()
            v.tensor_scalar(d[:], d[:], 0.25, None, ALU.mult)
            v.drain()
            v.scalar_tensor_tensor(var[:], var[:], 1.0 / BANK, d[:], ALU.mult, ALU.add)
            dve.wait_ge(s_gm, 1)
            over_pairs(g, pm[:, 0, 0:N])
            v.tensor_tensor(e[:], mean[:], g[:], ALU.subtract)
            v.drain()
            v.tensor_tensor(e[:], e[:], e[:], ALU.mult)
            v.drain()
            v.tensor_tensor(e[:], e[:], var[:], ALU.add).then_inc(s_e, 1)
            dve.wait_ge(s_gv, 1)
            over_pairs(d, pm[:, 1, 0:N])
            v.tensor_scalar(d[:], d[:], 1e-5, None, ALU.add)
            v.drain()
            rsqrt_steps(v, flat(y), flat(d), flat(t))
            v.scalar_tensor_tensor(g[:], g[:], -1.0, y[:], ALU.mult, ALU.mult)
            v.drain()
            for src, dst in ((y, scale), (g, bias)):
                for h in range(HALVES):
                    own = src[:, :, GROUP * h:GROUP * h + GROUP].rearrange("p i a -> p a i")
                    v.tensor_tensor(pick[:].rearrange("p (a i) -> p a i", a=GROUP), own,
                                    c["ident"][:].rearrange("p (a i) -> p a i", a=GROUP), ALU.mult)
                    v.drain()
                    v.reduce_sum(dst[:, h:h + 1], pick[:], axis=mybir.AxisListType.X)
                    v.drain()


def kan_constants(net, ctx):
    ins = net.ins
    k = {n: net.sb(ctx, n, list(ins[n].shape)) for n in ("kan_vec", "kan_basis", "kan_silu", "c_grid", "c_kan_ones",
                                                        "c_center")}
    k["sel8"] = net.sb(ctx, "sel8", [P, BLOCKS, P], F32R)
    k["pn_center"] = net.sb(ctx, "pn_center", [P, HALVES, P])
    k["pn_shift"] = net.sb(ctx, "pn_shift", [P, HALVES])
    k["grown"] = net.sb(ctx, "grown", [P, HALVES, P])
    k["end_b"] = net.sb(ctx, "end_b", [P, HALVES])
    return k


def prepare_kan(net, k, scale, bias):
    nc, ins = net.nc, net.ins
    with ExitStack() as local:
        staged = net.sb(local, "staged", [P, BLOCKS, P])
        shift = net.ps(local, "shift", [P, HALVES])
        loaded, shifted = (net.sem(local, s) for s in ("loaded", "shifted"))
        names = [n for n in k if n in ins]
        block = local.enter_context(nc.Block())

        @block.sync
        def _(sp):
            for n in names:
                sp.dma_start(k[n][:], ins[n]).then_inc(loaded, 16)
            sp.dma_start(staged[:], ins["c_sel8"]).then_inc(loaded, 16)
            sp.wait_ge(loaded, 16 * len(names) + 16)

        @block.tensor
        def _(pe):
            pe.wait_ge(loaded, 16 * len(names) + 16)
            nc.tensor.matmul(shift[:], k["c_center"][:, 0, :], bias, start=True, stop=True).then_inc(shifted, 1)

        @block.vector
        def _(dve):
            v = nc.vector
            vec = k["kan_vec"]
            dve.wait_ge(loaded, 16 * len(names) + 16)
            v.tensor_copy(k["sel8"][:], staged[:])
            v.tensor_scalar(k["end_b"][:], scale, 1.0, None, ALU.add)
            v.drain()
            for h in range(HALVES):
                v.tensor_scalar(k["pn_center"][:, h, :], k["c_center"][:, 0, :], scale[:, h:h + 1], None, ALU.mult)
                v.tensor_scalar(k["grown"][:, h, :], net.c["ident"][:], k["end_b"][:, h:h + 1], None, ALU.mult)
            v.drain()
            v.tensor_scalar(k["end_b"][:], bias, vec[:, 13:14], None, ALU.add)
            for n in range(4):
                v.tensor_scalar(vec[:, 2 + 3 * n:4 + 3 * n], vec[:, 2 + 3 * n:4 + 3 * n], 1.75, None, ALU.mult)
            v.tensor_scalar(k["kan_silu"][:], k["kan_silu"][:], 0.5, None, ALU.mult)
            dve.wait_ge(shifted, 1)
            v.tensor_copy(k["pn_shift"][:], shift[:])
            v.drain()


PN, K1, K2, K3, K4 = range(5)
KANS = (K1, K2, K3, K4)

UNITS = 32
SLOT = {K1: -24, K2: -16, K3: 0, K4: 24}
PREP = {"center0": (-59, -40, -32, -16, 10),
        "center1": (-57, -38, -30, -14, 12),
        "evac0": (-58, -39, -31, -15, 13),
        "evac1": (-55, -36, -28, -12, 15),
        "var0": (-56, -39, -29, -14, 13),
        "var1": (-55, -36, -28, -10, 14),
        "chain": (-51, -33, -24, -8, 18),
        "spread0": (-50, -33, -25, -7, 19),
        "spread1": (-49, -32, -24, -6, 20),
        "scale0": (-46, -30, -21, -3, 22),
        "scale1": (-45, -28, -20, -2, 23)}
SILU = {"tanh": {PN: -42, K4: 12}, "silu": {PN: -40, K4: 15}}
LOAD_X, LOAD_R, STORE, MEASURE = -64, 8, 35, 37
FEED_K1, FEED_U1, FEED_K2, FEED_U2, BACK_K1, BACK_K2 = -46, -44, -34, -29, -16, -7
TURN, HALF, TOTAL = -36, -5, 10
REPEAT = 3
EVACUATE = 2
ACT_UNITS = (2, 6)


class Order:

    def __init__(self, positions, tiles):
        self.period = len(positions)
        items = sorted(((UNITS * t + p, kind, t) for kind, p in positions.items() for t in range(tiles)))
        self.index = {(kind, t): n for n, (_, kind, t) in enumerate(items)}
        self.offset = {kind: self.index[kind, tiles // 2] - self.period * (tiles // 2) for kind in positions}

    def __call__(self, kind, t):
        return self.index[kind, t] if isinstance(t, int) else t * self.period + self.offset[kind]


def window_layer(net, k, source, bias, target, stats):
    nc, c = net.nc, net.c
    TILES = BANDS * HALVES
    CHUNKS = TILE // BANK
    RING = 4
    G = 2 * GROUP
    ON_DVE = [n for n in range(2 * CHUNKS) if n not in ACT_UNITS]
    prep_no = Order({kind: PREP["center0"][kind] for kind in (PN,) + KANS}, TILES)
    slot_no = Order(SLOT, TILES)
    silu_no = Order(SILU["silu"], TILES)
    with ExitStack() as local:
        def sb(name, shape, dt=F32):
            return net.sb(local, name, shape, dt)
        X, R, Z, W, D = (sb(n, [P, TILE]) for n in ("x", "x_to_x3", "z", "silu_z", "back_k2"))
        Y, U = sb("y", [P, 2, TILE]), sb("silu_y", [P, 2, TILE])
        kin, ku = sb("kin", [P, 2, TILE]), sb("ku", [P, 2, TILE])
        turned_y = sb("columns_first", [P, TILE])
        back = {K1: turned_y[:], K2: D[:]}
        sq = sb("sq", [P, TILE])
        srep = sb("srep", [P, CHUNKS, GROUP, BANK])
        ex = sb("ex", [P, RING, GROUP, BANK])
        y, t_ = sb("rstd", [P, P]), sb("t", [P, P])
        hilo = sb("hilo", [P, 2, P])
        part = sb("part", [P, CHUNKS * 6])
        one = sb("one", [P, 1])
        cen, spread, out = (net.ps(local, n, [P, 2, BANK]) for n in ("cen", "spread", "out"))
        var = net.ps(local, "var", [P, P])
        (centered, squared, var_ready, factors, spread_ready, scaled, normed, args, own_args, exps,
         used, evacuated, tanh_ready, u_ready, copied_y, copied_u, halved, summed, measured, x_loaded, r_loaded, stored) = (
            net.sem(local, n) for n in (
                "centered", "squared", "var_ready", "factors", "spread_ready", "scaled",
                "normed", "args", "own_args", "exps", "used", "evacuated", "tanh_ready", "u_ready", "copied_y", "copied_u",
                "halved", "summed", "measured", "x_loaded", "r_loaded", "stored"))
        kin_loaded = {kind: net.sem(local, f"kin_loaded{kind}") for kind in (K1, K2)}
        ku_loaded = {kind: net.sem(local, f"ku_loaded{kind}") for kind in (K1, K2)}
        back_loaded = {kind: net.sem(local, f"back_loaded{kind}") for kind in (K1, K2)}
        rep_loaded = [net.sem(local, f"rep_loaded{n}") for n in range(CHUNKS)]
        block = local.enter_context(nc.Block())

        def norm_in(kind, h):
            return {PN: X[:], K1: kin[:, 0], K2: kin[:, 1], K3: Y[:, h], K4: Z[:]}[kind]

        def norm_out(kind, h):
            return Y[:, h] if kind == PN else norm_in(kind, h)

        def silu_of(kind, h):
            return {K1: ku[:, 0], K2: ku[:, 1], K3: U[:, h], K4: W[:]}[kind]

        vec = k["kan_vec"]
        ln_g = {PN: vec[:, 0:1], **{n: vec[:, 3 * n - 1:3 * n] for n in KANS}}
        ln_b = {PN: vec[:, 1:2], **{n: vec[:, 3 * n:3 * n + 1] for n in KANS}}

        def out_b(kind, h):
            return k["end_b"][:, h:h + 1] if kind == K4 else vec[:, 3 * kind + 1:3 * kind + 2]

        def cols(n):
            return slice(BANK * n, BANK * n + BANK)

        def after(t, first=1):
            return not isinstance(t, int) or t >= first

        def band(t, h):
            return t // 2 if isinstance(t, int) else (t - h) // 2

        class Round:

            def __init__(self, number, parity):
                self.number, self.parity = number, parity

            def due(self, unit, position):
                if (unit - position) % UNITS:
                    return None, 0
                ahead = (unit - position) // UNITS
                t = self.number + ahead
                if isinstance(t, int) and not 0 <= t < TILES:
                    return None, 0
                return t, (self.parity + ahead) % 2

            def slot(self, unit):
                for kind in KANS:
                    t, h = self.due(unit - (unit - SLOT[kind]) % UNITS, SLOT[kind])
                    if (unit - SLOT[kind]) % UNITS < 2 * CHUNKS and t is not None:
                        return kind, (unit - SLOT[kind]) % UNITS, t, h
                return None, 0, None, 0

        def rounds(eng, round_):
            for n in range(-2, 4):
                round_(Round(n, n % 2))
            with eng.Fori(2, BANDS - 1) as r:
                for h in range(HALVES):
                    round_(Round(r * 2 + h, h))
            for n in range(TILES - 2, TILES + 2):
                round_(Round(n, n % 2))

        @block.sync
        def _(sp):
            def regroup(dst, src, sem, backwards=False):
                for i in range(2 * GROUP):
                    wide = (dst if backwards else src)[QUAD // 2 * i:QUAD // 2 * i + QUAD // 2]
                    wide = wide.rearrange("p (z n) -> p z n", z=BAND)
                    deep = (src if backwards else dst)[:, COLS * i:COLS * i + COLS]
                    sp.dma_start(wide if backwards else deep, deep if backwards else wide).then_inc(sem, 16)

            def load_x(t, h):
                tile_ = source[band(t, h), h]
                if after(t):
                    sp.wait_ge(scaled, CHUNKS * prep_no(PN, t - 1) + CHUNKS)
                sp.dma_start(X[:], tile_).then_inc(x_loaded, 16)

            def load_r(t, h):
                tile_ = source[band(t, h), h]
                wait_both(sp, stored, 16 * t, measured, t)
                sp.dma_start(R[:], tile_).then_inc(r_loaded, 16)

            def store(t, h):
                tile_ = target[band(t, h), h]
                sp.wait_ge(evacuated, CHUNKS * slot_no(K4, t) + CHUNKS)
                sp.dma_start(tile_, R[:]).then_inc(stored, 16)

            def feed_k1(t, h):
                sp.wait_ge(normed, prep_no(PN, t) + 1)
                regroup(kin[:, 0], Y[:, h], kin_loaded[K1])

            def feed_u1(t, h):
                wait_both(sp, back_loaded[K1], 128 * t, u_ready, silu_no(PN, t) + 1)
                regroup(ku[:, 0], U[:, h], ku_loaded[K1])

            def feed_k2(t, h):
                sp.wait_ge(copied_y, t + 1)
                regroup(kin[:, 1], turned_y[:], kin_loaded[K2])

            def feed_u2(t, h):
                wait_both(sp, copied_u, t + 1, back_loaded[K2], 128 * t)
                regroup(ku[:, 1], turned_y[:], ku_loaded[K2])

            def give_back(kind, t):
                complete = CHUNKS * slot_no(kind, t) + CHUNKS
                if kind == K2:
                    wait_both(sp, summed, t, evacuated, complete)
                else:
                    wait_both(sp, ku_loaded[K2], 128 * t + 128, evacuated, complete)
                regroup(back[kind], ku[:, kind - K1], back_loaded[kind], True)

            def repeat(kind, t, h, n):
                b = slot_no(kind, t)
                s = norm_out(kind, h)
                wait_both(sp, exps, 8 * b + (2 * n + 2 - 8), normed, prep_no(kind, t) + 1 if n == 0 else 0)
                for g in range(GROUP):
                    src = s[QUAD * g:QUAD * g + QUAD, cols(n)].unsqueeze(1).to_broadcast([QUAD, GROUP, BANK])
                    sp.dma_start(srep[:, n, g, :], src).then_inc(rep_loaded[n], 16)

            def round_(now):
                for u in range(UNITS):
                    for kind in KANS:
                        for n in range(CHUNKS):
                            t, h = now.due(u, SLOT[kind] - 2 * CHUNKS + 2 * n + REPEAT)
                            if t is not None:
                                repeat(kind, t, h, n)
                    for position, step in ((STORE, store), (LOAD_R, load_r), (LOAD_X, load_x), (FEED_K1, feed_k1), (FEED_U1, feed_u1),
                                           (FEED_K2, feed_k2), (FEED_U2, feed_u2)):
                        t, h = now.due(u, position)
                        if t is not None:
                            step(t, h)
                    for kind, position in ((K1, BACK_K1), (K2, BACK_K2)):
                        t, h = now.due(u, position)
                        if t is not None:
                            give_back(kind, t)
            rounds(sp, round_)
            sp.wait_ge(stored, 16 * TILES)

        @block.scalar
        def _(act):
            a = nc.scalar

            def evacuate_centred(kind, t, h, half):
                no = prep_no(kind, t)
                dst = norm_in(kind, h)
                shift = k["pn_shift"][:, h:h + 1] if kind == PN else 0.0
                if half == 0:
                    if kind in (K3, K4):
                        act.wait_ge(u_ready, silu_no(PN if kind == K3 else K4, t) + 1)
                    wait_past(act, var_ready, no)
                for n in (2 * half, 2 * half + 1):
                    act.wait_ge(centered, CHUNKS * no + n + 1)
                    a.activation(dst[:, cols(n)], cen[:, n % 2, :], ACT.Identity, bias=shift)
                    a.activation(sq[:, cols(n)], cen[:, n % 2, :], ACT.Square, bias=shift).then_inc(squared, 1)

            def tanh(kind, t, h):
                if kind == PN:
                    wait_past(act, summed, t - 1)
                    act.wait_ge(normed, prep_no(PN, t) + 1)
                    a.activation(U[:, h], Y[:, h], ACT.Tanh, scale=0.5).then_inc(tanh_ready, 1)
                else:
                    act.wait_ge(summed, t + 1)
                    a.activation(W[:], Z[:], ACT.Tanh, scale=0.5).then_inc(tanh_ready, 1)

            def exponential(kind, n, t, h):
                unit = 2 * CHUNKS * slot_no(kind, t) + n
                e = ex[:, n % RING].rearrange("p g n -> p (g n)")
                j = n % 2
                if n in ACT_UNITS:
                    b = slot_no(kind, t)
                    act.wait_ge(rep_loaded[n // 2], 64 * b + 64)
                    wait_past(act, used, 2 * CHUNKS * b + (n - RING + 1))
                    a.activation(e, srep[:, n // 2].rearrange("p g n -> p (g n)"), ACT.Square,
                                 bias=k["c_grid"][:, j, 2:3]).then_inc(own_args, 1)
                    act.wait_ge(own_args, len(ACT_UNITS) * b + (ACT_UNITS.index(n) + 1))
                    a.activation(e, e, ACT.Exp, scale=-1.0).then_inc(exps, 1)
                else:
                    act.wait_ge(args, len(ON_DVE) * slot_no(kind, t) + (ON_DVE.index(n) + 1))
                    a.activation(e, e, ACT.Exp, bias=k["c_grid"][:, j, 1:2], scale=-1.0).then_inc(exps, 1)

            def evacuate(kind, t, h, n):
                b = slot_no(kind, t)
                dst = R[:] if kind == K4 else silu_of(kind, h)
                act.wait_ge(used, 2 * CHUNKS * b + (2 * n + 2))
                a.activation(dst[:, cols(n)], out[:, n % 2, :], ACT.Identity, bias=out_b(kind, h)).then_inc(evacuated, 1)

            def round_(now):
                for u in range(UNITS):
                    for kind in SILU["tanh"]:
                        t, h = now.due(u, SILU["tanh"][kind])
                        if t is not None:
                            tanh(kind, t, h)
                    for kind in (PN,) + KANS:
                        for half in range(2):
                            t, h = now.due(u, PREP[f"evac{half}"][kind])
                            if t is not None:
                                evacuate_centred(kind, t, h, half)
                    kind, n, t, h = now.slot(u)
                    if t is not None:
                        exponential(kind, n, t, h)
                    for kind in KANS:
                        for n in range(CHUNKS):
                            t, h = now.due(u, SLOT[kind] + 2 * n + 1 + EVACUATE)
                            if t is not None:
                                evacuate(kind, t, h, n)
            rounds(act, round_)

        @block.vector
        def _(dve):
            v = nc.vector
            def chain(kind, t, h):
                no = prep_no(kind, t)
                wait_past(dve, spread_ready, CHUNKS * no)
                dve.wait_ge(var_ready, no + 1)
                v.tensor_scalar(var[:], var[:], 1.0 * G / P if kind in (K1, K2) else 0.5 * G / P, EPS_LN, ALU.mult, ALU.add)
                v.drain()
                rsqrt_steps(v, y[:], var[:], t_[:])
                split_hi_lo(v, hilo[:, 0, :], hilo[:, 1, :], y[:]).then_inc(factors, 1)

            def scale(kind, t, h, half):
                no = prep_no(kind, t)
                src, dst = norm_in(kind, h), norm_out(kind, h)
                for n in (2 * half, 2 * half + 1):
                    dve.wait_ge(spread_ready, CHUNKS * no + n + 1)
                    v.scalar_tensor_tensor(dst[:, cols(n)], src[:, cols(n)], ln_g[kind], spread[:, n % 2, :],
                                           ALU.mult, ALU.mult).then_inc(scaled, 1)
                if half:
                    dve.wait_ge(scaled, CHUNKS * no + CHUNKS)
                    v.tensor_scalar(dst, dst, ln_b[kind], None, ALU.add).then_inc(normed, 1)

            def silu(kind, t, h):
                dve.wait_ge(tanh_ready, silu_no(kind, t) + 1)
                x_, u_ = (Y[:, h], U[:, h]) if kind == PN else (Z[:], W[:])
                v.scalar_tensor_tensor(u_, u_, 1.0, x_, ALU.add, ALU.mult).then_inc(u_ready, 1)

            def measure(t, h):
                dve.wait_ge(evacuated, CHUNKS * slot_no(K4, t) + CHUNKS)
                for n in range(CHUNKS):
                    last = v.bn_stats(part[:, 6 * n:6 * n + 6], R[:, cols(n)])
                last.then_inc(measured, 1)
                v.drain()
                v.tensor_copy(stats[:, h, band(t, h), :], part[:])
                v.drain()

            def distances(kind, n, t, h):
                b = slot_no(kind, t)
                dve.wait_ge(rep_loaded[n // 2], 64 * b + 64)
                wait_past(dve, used, 2 * CHUNKS * b + (n - RING + 1))
                s = srep[:, n // 2].rearrange("p g n -> p (g n)")
                v.scalar_tensor_tensor(ex[:, n % RING].rearrange("p g n -> p (g n)"), s, k["c_grid"][:, n % 2, 0:1], s,
                                       ALU.add, ALU.mult).then_inc(args, 1)

            def round_(now):
                for u in range(UNITS):
                    for kind in SILU["silu"]:
                        t, h = now.due(u, SILU["silu"][kind])
                        if t is not None:
                            silu(kind, t, h)
                    for kind in (PN,) + KANS:
                        t, h = now.due(u, PREP["chain"][kind])
                        if t is not None:
                            chain(kind, t, h)
                        for half in range(2):
                            t, h = now.due(u, PREP[f"scale{half}"][kind])
                            if t is not None:
                                scale(kind, t, h, half)
                    t, h = now.due(u, MEASURE)
                    if t is not None:
                        measure(t, h)
                    kind, n, t, h = now.slot(u)
                    if t is not None and n in ON_DVE:
                        distances(kind, n, t, h)
            rounds(dve, round_)

        @block.tensor
        def _(pe):
            m = nc.tensor

            def center(kind, t, h, half):
                no = prep_no(kind, t)
                src = norm_in(kind, h)
                if half == 0:
                    if kind == PN:
                        pe.wait_ge(x_loaded, 16 * t + 16)
                    elif kind in (K1, K2):
                        pe.wait_ge(kin_loaded[kind], 128 * t + 128)
                    elif kind == K4:
                        pe.wait_ge(summed, t + 1)
                weights = k["pn_center"][:, h, :] if kind == PN else k["c_center"][:, 1 if kind in (K1, K2) else 0, :]
                for n in (2 * half, 2 * half + 1):
                    wait_past(pe, squared, CHUNKS * no + (n - 1))
                    m.matmul(cen[:, n % 2, :], weights, src[:, cols(n)], start=True, stop=True).then_inc(centered, 1)

            def variance(kind, t, h, half):
                no = prep_no(kind, t)
                if half == 0:
                    wait_past(pe, factors, no)
                pe.wait_ge(squared, CHUNKS * no + 2 * half + 2)
                for i in range(GROUP):
                    for quarter in (2 * half, 2 * half + 1):
                        block_ = P * (GROUP * quarter + i)
                        last = m.matmul(var[QUAD * quarter:QUAD * quarter + QUAD, :],
                                        k["c_kan_ones"][:, 0 if kind in (K1, K2) else 1, i, :], sq[:, block_:block_ + P],
                                        start=(i == 0), stop=(i == GROUP - 1), tile_position=(0, QUAD * quarter))
                if half:
                    last.then_inc(var_ready, 1)

            def spread_out(kind, t, h, half):
                no = prep_no(kind, t)
                pe.wait_ge(factors, no + 1)
                for n in (2 * half, 2 * half + 1):
                    wait_past(pe, scaled, CHUNKS * no + (n - 1))
                    for i in range(GROUP):
                        for z in range(2):
                            last = m.matmul(spread[:, n % 2, P * i:P * i + P], k["sel8"][:, GROUP * n + i, :],
                                            hilo[:, z, :].bitcast(F32R), start=(z == 0), stop=(z == 1))
                    last.then_inc(spread_ready, 1)

            def products(kind, n, t, h):
                b = slot_no(kind, t)
                bank = out[:, n // 2 % 2, :]
                if n == 0:
                    if kind in (K1, K2):
                        pe.wait_ge(ku_loaded[kind], 128 * t + 128)
                    else:
                        pe.wait_ge(u_ready, silu_no(PN if kind == K3 else K4, t) + 1)
                    if kind == K4:
                        pe.wait_ge(r_loaded, 16 * t + 16)
                if n % 2 == 0:
                    wait_past(pe, evacuated, CHUNKS * b + (n // 2 - 1))
                    m.matmul(bank, k["kan_silu"][:, kind - 1, :], silu_of(kind, h)[:, cols(n // 2)], start=True, stop=False)
                    if kind == K4:
                        m.matmul(bank, k["grown"][:, h, :], R[:, cols(n // 2)], start=False, stop=False)
                pe.wait_ge(exps, 2 * CHUNKS * b + (n + 1))
                for g in range(GROUP):
                    last = m.matmul(out[QUAD * g:QUAD * g + QUAD, n // 2 % 2, :], k["kan_basis"][:, kind - 1, n % 2, :],
                                    ex[:, n % RING, g, :], start=False, stop=(n % 2 == 1), tile_position=(0, QUAD * g))
                last.then_inc(used, 1)

            def round_(now):
                for u in range(UNITS):
                    for kind in (PN,) + KANS:
                        for half in range(2):
                            t, h = now.due(u, PREP[f"center{half}"][kind])
                            if t is not None:
                                center(kind, t, h, half)
                        for half in range(2):
                            t, h = now.due(u, PREP[f"var{half}"][kind])
                            if t is not None:
                                variance(kind, t, h, half)
                        for half in range(2):
                            t, h = now.due(u, PREP[f"spread{half}"][kind])
                            if t is not None:
                                spread_out(kind, t, h, half)
                    kind, n, t, h = now.slot(u)
                    if t is not None:
                        products(kind, n, t, h)
            rounds(pe, round_)

        @block.gpsimd
        def _(pool):
            g = nc.gpsimd

            def turn(t, h):
                rows_first = lambda tile_: tile_.rearrange("p (rw x) -> p x rw", x=BAND)
                columns_first = turned_y[:].rearrange("p (x rw) -> p x rw", x=BAND)
                ones = one[:].unsqueeze(1).to_broadcast([P, BAND, BAND * QUAD])
                pool.wait_ge(normed, prep_no(PN, t) + 1)
                wait_past(pool, halved, t)
                g.tensor_tensor(columns_first, rows_first(Y[:, h]), ones, ALU.mult).then_inc(copied_y, 1)
                pool.wait_ge(u_ready, silu_no(PN, t) + 1)
                pool.wait_ge(kin_loaded[K2], 128 * t + 128)
                g.tensor_tensor(columns_first, rows_first(U[:, h]), ones, ALU.mult).then_inc(copied_u, 1)

            d = D[:].rearrange("p (x rw) -> p rw x", x=BAND)

            def by_columns(tile_):
                return tile_.rearrange("p (rw x) -> p rw x", x=BAND)

            def half(t, h):
                pool.wait_ge(back_loaded[K1], 128 * t + 128)
                pool.wait_ge(back_loaded[K2], 128 * t + 128)
                g.tensor_tensor(d, d, by_columns(back[K1]), ALU.add).then_inc(halved, 1)

            def total(t, h):
                if after(t):
                    pool.wait_ge(exps, 8 * slot_no(K4, t - 1) + 8)
                pool.wait_ge(evacuated, CHUNKS * slot_no(K3, t) + CHUNKS)
                pool.wait_ge(halved, t + 1)
                g.tensor_tensor(by_columns(Z[:]), by_columns(U[:, h]), d, ALU.add).then_inc(summed, 1)

            def round_(now):
                for u in range(UNITS):
                    for position, step in ((TOTAL, total), (TURN, turn), (HALF, half)):
                        t, h = now.due(u, position)
                        if t is not None:
                            step(t, h)
            g.memset(one[:], 1.0)
            g.drain()
            rounds(pool, round_)


PATTERN = {(1, 1): (128, 1), (1, 0): (64, 2), (1, -1): (32, 4), (0, 1): (16, 8)}


def pattern_layer(net, source, scale, bias, out):
    nc, c = net.nc, net.c
    WEIGHT = 0.5 / 255
    ON_PE, ON_DVE = [(1, 1), (1, 0)], [(1, -1), (0, 1)]
    DIRS = ON_PE + ON_DVE
    TILES = BANDS * HALVES
    CHUNKS = TILE // BANK
    with ExitStack() as local:
        xt = net.sb(local, "xt", [P, HALVES, HALO, COLS])
        z = net.sb(local, "z", [P, HALVES, HALO, PAD])
        d = net.sb(local, "d", [P, HALVES, len(DIRS), BAND + 1, PAD])
        ot = net.sb(local, "ot", [P, HALVES, BAND, COLS])
        weights = net.sb(local, "weights", [P, 2 * len(ON_PE), P])
        acc = net.ps(local, "acc", [P, HALVES, CHUNKS, BANK])
        padded, weighted, z_ready, diff_dve, diff_pool, tanh_ready, acc_ready, x_used, added, out_ready = (
            net.sem(local, n) for n in ("padded", "weighted", "z_ready", "diff_dve", "diff_pool", "tanh_ready", "acc_ready",
                                        "x_used", "added", "out_ready"))
        loaded = [net.sem(local, f"loaded{h}") for h in range(HALVES)]
        stored = [net.sem(local, f"stored{h}") for h in range(HALVES)]
        block = local.enter_context(nc.Block())
        bands = out.rearrange("b c r w -> (b c) (r w)").rearrange("p (t n) -> p t n", n=TILE)

        def region(dr, dc):
            return slice(1 - dr, BAND + 1), slice(0 if dc > 0 else 1, PAD if dc < 0 else PAD - 1)

        def difference(engine, h, direction):
            (dr, dc), n = direction, DIRS.index(direction)
            rows, columns = region(dr, dc)
            there = z[:, h, rows.start + dr:rows.stop + dr, columns.start + dc:columns.stop + dc]
            return engine.tensor_tensor(d[:, h, n, rows, columns], there, z[:, h, rows, columns], ALU.subtract)

        def term(h, direction, opposite, rows):
            (dr, dc), n = direction, DIRS.index(direction)
            back = (dr, dc) if opposite else (0, 0)
            return d[:, h, n, rows.start + 1 - back[0]:rows.stop + 1 - back[0], 1 - back[1]:1 - back[1] + COLS]

        def factor(direction, opposite):
            return (-WEIGHT if opposite else WEIGHT) * PATTERN[direction][int(opposite)]

        @block.sync
        def _(sp):
            def load(r):
                for h in range(HALVES):
                    wait_past(sp, x_used, 2 * (r - 1) + h + 1)
                    for rows, src in ((slice(1, BAND + 1), source[r, h]),
                                      (slice(0, 1), source[(r + BANDS - 1) % BANDS, h, :, TILE - COLS:]),
                                      (slice(HALO - 1, HALO), source[(r + 1) % BANDS, h, :, 0:COLS])):
                        sp.dma_start(xt[:, h, rows, :].rearrange("p r w -> p (r w)"), src).then_inc(loaded[h], 16)

            def store(r):
                for h in range(HALVES):
                    sp.wait_ge(out_ready, 2 * r + h + 1)
                    sp.dma_start(bands[P * h:P * h + P, r, :], ot[:, h].rearrange("p r w -> p (r w)")).then_inc(stored[h], 16)
            pipeline(sp, BANDS, [(0, load), (1, store)])
            for h in range(HALVES):
                sp.wait_ge(stored[h], 16 * BANDS)

        @block.scalar
        def _(act):
            a = nc.scalar
            act.wait_ge(padded, 1)

            def normalise(r, h):
                i = 2 * r + h
                first, last = (isinstance(r, int) and r == e for e in (0, BANDS - 1))
                act.wait_ge(loaded[h], 48 * r + 48)
                wait_past(act, diff_dve, i - 1)
                wait_past(act, diff_pool, i - 1)
                inner = slice(1 if first else 0, HALO - 1 if last else HALO)
                n = a.activation(z[:, h, inner, 1:COLS + 1], xt[:, h, inner, :], ACT.Identity, bias=bias[:, h:h + 1],
                                 scale=scale[:, h:h + 1])
                if last:
                    n = a.activation(z[:, h, HALO - 1, 1:COLS + 1], xt[:, h, HALO - 1, :], ACT.Copy, scale=0.0)
                n.then_inc(z_ready, 1)

            def tanh(r, h):
                i = 2 * r + h
                for n, (dr, dc) in enumerate(DIRS):
                    if n == 0:
                        act.wait_ge(diff_dve, i + 1)
                    if n == 2:
                        act.wait_ge(diff_pool, i + 1)
                    rows, columns = region(dr, dc)
                    t = d[:, h, n, rows, columns]
                    a.activation(t, t, ACT.Tanh, scale=5.0).then_inc(tanh_ready, 1)
            normalise(0, 0)
            normalise(0, 1)
            tanh(0, 0)
            with act.Fori(1, BANDS - 1) as r:
                normalise(r, 0)
                tanh(r - 1, 1)
                normalise(r, 1)
                tanh(r, 0)
            normalise(BANDS - 1, 0)
            tanh(BANDS - 2, 1)
            normalise(BANDS - 1, 1)
            tanh(BANDS - 1, 0)
            tanh(BANDS - 1, 1)

        @block.gpsimd
        def _(pool):
            g = nc.gpsimd

            def differences(r):
                for h in range(HALVES):
                    i = 2 * r + h
                    wait_past(pool, out_ready, i - 1)
                    pool.wait_ge(z_ready, i + 1)
                    difference(g, h, ON_DVE[0])
                    difference(g, h, ON_DVE[1]).then_inc(diff_pool, 1)
            g.memset(z[:], 0.0).then_inc(padded, 1)
            pipeline(pool, BANDS, [(0, differences)])

        @block.vector
        def _(dve):
            v = nc.vector
            for n, (direction, opposite) in enumerate((p, o) for p in ON_PE for o in (False, True)):
                last = v.tensor_scalar(weights[:, n, :], c["ident"][:], factor(direction, opposite), None, ALU.mult)
            last.then_inc(weighted, 1)

            def differences(r, h):
                i = 2 * r + h
                wait_past(dve, acc_ready, CHUNKS * (i - 1))
                dve.wait_ge(z_ready, i + 1)
                difference(v, h, ON_PE[0])
                difference(v, h, ON_PE[1]).then_inc(diff_dve, 1)

            def add(r, h):
                i = 2 * r + h
                wait_past(dve, stored[h], 16 * r)
                into, before = ot[:, h], xt[:, h, 1:BAND + 1, :]
                for n, (direction, opposite) in enumerate((p, o) for p in ON_DVE for o in (False, True)):
                    dve.wait_ge(tanh_ready, len(DIRS) * i + len(ON_PE) + n // 2 + 1)
                    if n == 1:
                        dve.wait_ge(x_used, i + 1)
                    if n > 1:
                        dve.wait_ge(added, 3 * i + n - 1)
                    v.scalar_tensor_tensor(into, term(h, direction, opposite, slice(0, BAND)), factor(direction, opposite),
                                           before, ALU.mult, ALU.add).then_inc(added if n else x_used, 1)
                    before = into
                dve.wait_ge(acc_ready, CHUNKS * i + CHUNKS)
                dve.wait_ge(added, 3 * i + 3)
                sums = acc[:, h].rearrange("p k (r w) -> p (k r) w", w=COLS)
                v.scalar_tensor_tensor(into, into, 0.5, sums, ALU.add, ALU.add).then_inc(out_ready, 1)
            differences(0, 0)
            differences(0, 1)
            add(0, 0)
            with dve.Fori(1, BANDS) as r:
                differences(r, 0)
                add(r - 1, 1)
                differences(r, 1)
                add(r, 0)
            add(BANDS - 1, 1)

        @block.tensor
        def _(pe):
            m = nc.tensor
            pe.wait_ge(weighted, 1)

            def sums(r):
                for h in range(HALVES):
                    i = 2 * r + h
                    wait_past(pe, out_ready, i - 1)
                    for n, direction in enumerate(ON_PE):
                        pe.wait_ge(tanh_ready, len(DIRS) * i + n + 1)
                        for k in range(CHUNKS):
                            for o in (0, 1):
                                last = m.matmul(acc[:, h, k, :], weights[:, 2 * n + o, :],
                                                term(h, direction, bool(o), slice(2 * k, 2 * k + 2)),
                                                start=(n + o == 0), stop=(n + o == 2))
                            if n:
                                last.then_inc(acc_ready, 1)
            pipeline(pe, BANDS, [(0, sums)])


def build_program(nc, ins, out):
    with ExitStack() as ctx:
        net = Net(nc, ctx, ins)
        load_constants(net, ctx, ["c_ident"])
        x_rows = ins["x"].rearrange("b c r w -> (b c) (r w)")
        t1, t2, x1, x2, x3 = (net.scratch(k) for k in ("t1", "t2", "x1", "x2", "x3"))
        SW = BANDS * TILE // BANK * 6
        stats = net.sb(ctx, "stats", [P, HALVES, SW])
        by_band = stats[:].rearrange("p h (r n) -> p h r n", r=BANDS)
        merged = stats[:].rearrange("p h n -> p (h n)").rearrange("p (o n) -> p o n", o=1)
        scale, bias = net.sb(ctx, "scale", [P, HALVES]), net.sb(ctx, "bias", [P, HALVES])
        with ExitStack() as local:
            load_constants(net, local, ["c_ones", "c_sel", "bn"])
            bn = net.c["bn"]
            input_stats(net, x_rows, stats[:])
            norm_vectors(net, stats[:], "pair", 1e-5, scale[:], bias[:])
            conv_layer(net, x_rows, scale, bias, ins["w1"], ins["b1"], t1, by_band, True)
            norm_vectors(net, merged, "channel", 1e-5, scale[:, 0:1], bias[:, 0:1], bn[:, 0:1], bn[:, 1:2])
            conv_layer(net, t1, scale[:, 0:1], bias[:, 0:1], ins["w2"], ins["b2"], t2, by_band, False)
            norm_vectors(net, merged, "channel", 1e-5, scale[:, 0:1], bias[:, 0:1], bn[:, 2:3], bn[:, 3:4])
            residual_layer(net, x_rows, t2, scale[:, 0:1], bias[:, 0:1], x1, by_band)
        norm_vectors(net, stats[:], "pair", 1e-5, scale[:], bias[:])
        with ExitStack() as local:
            coef = net.sb(local, "coef", [P, IMAGES, 2, KP])
            with ExitStack() as inner:
                tables = net.sb(inner, "tables", [P, 2, HALVES * P])
                g1 = net.sb(inner, "g1", [P, CH, 2, KP])
                g2 = net.sb(inner, "g2", [P, CH, 3, KP])
                spread_table(net, scale[:], tables[:, 0, :])
                spread_table(net, bias[:], tables[:, 1, :])
                pole_kernels(net, g1, g2)
                residues(net, x1, tables[:, 0, :], tables[:, 1, :], g1, g2, coef[:])
            image_stats = stats[:].rearrange("p h n -> p (h n)").rearrange("p (i n) -> p i n", i=CH)
            evaluate_residues(net, x1, coef, x2, image_stats)
            norm_vectors_by_image(net, image_stats, scale, bias)
        with ExitStack() as local:
            k = kan_constants(net, local)
            prepare_kan(net, k, scale[:], bias[:])
            window_layer(net, k, x2, bias, x3, by_band)
        norm_vectors(net, stats[:], "pair", 1e-5, scale[:], bias[:])
        pattern_layer(net, x3, scale, bias, out)


def shape_constants():
    p = np.arange(P)
    f = lambda a: np.ascontiguousarray(a, dtype=np.float32)
    sel = np.zeros((P, HALVES * BLOCKS, P), np.float32)
    edge = np.ones((P, BANDS), np.float32)
    for b in range(HALVES * BLOCKS):
        for g in range(GROUP):
            row = QUAD * (b % 4) + GROUP * (b // 4) + g
            sel[row, b, QUAD * g:QUAD * g + QUAD] = 1.0
            if b < COLS // P:
                edge[row, 0] = 0.0
            if HALO * COLS // P - COLS // P <= b < HALO * COLS // P:
                edge[row, BANDS - 1] = 0.0
    sel8 = np.zeros((P, BLOCKS, P), np.float32)
    for k in range(P):
        sel8[k, k // 8, 16 * (k % 8):16 * (k % 8) + 16] = 1.0
    same = lambda n: p[:, None] // n == p[None] // n
    near = (p % GROUP)[:, None] + GROUP * np.arange(2)[None] - 3.5
    turn = 2 * np.pi * ((p[:, None] * p[None]) % SUB) / SUB
    return {
        "c_ident": np.eye(P, dtype=np.float32),
        "c_ones": f(np.arange(QUAD)[None, None] == GROUP * np.arange(8)[None, :, None] + (p // QUAD)[:, None, None]),
        "c_edge": edge,
        "c_pair": f(0.5 * (p[:, None] // 2 == p[None] // 2)),
        "c_channel": f((p[:, None] % CH == p[None] % CH) / GROUP),
        "c_sel": sel,
        "c_sel8": sel8,
        "c_kan_ones": f(np.stack([[np.stack([(np.arange(QUAD) // 8 == i) & (q // n == np.arange(QUAD) % 8 * 16 // n)
                                         for i in range(GROUP)]) for n in (16, 32)] for q in p])),
        "c_center": f(np.stack([np.eye(P) - same(n) / n for n in (32, 16)], axis=1)),
        "c_grid": f(np.stack([-2 * near, -near ** 2, -near], axis=2)),
        "c_dft": np.stack([np.cos(turn), np.sin(turn), -np.sin(turn)], axis=1).astype(np.float32),
        "c_freq": np.fft.fftfreq(SUB).astype(np.float32)[:, None],
        "c_mask": f(p[:, None] // MODES == p[None] // MODES),
    }


def conv_weights(w):
    out = np.zeros((4, CH, 2, 3, CH), w.dtype)
    for o in range(2):
        for dy in range(3):
            out[o + dy, :, o] = w[:, :, dy, :].transpose(1, 2, 0)
    return np.ascontiguousarray(out.reshape(P, 2, 3, CH))


def kan_arrays(a):
    place = np.arange(16).reshape(8, 2).T.ravel()
    vec, basis, silu = [np.tile(a["L2_conv_pn_" + n], GROUP) for n in "gb"], [], []
    for n in range(1, 5):
        get = lambda name: a[f"L2_conv_k{n}_{name}"]
        order = place if n < 3 else np.arange(CH)
        F = len(order)
        vec += [np.tile(get(name)[order], P // F) for name in ("ln_g", "ln_b", "bb")]
        ws = get("ws").reshape(F, F, 2, GROUP)[order][:, order]
        b = np.zeros((QUAD // F, F, GROUP, 2, QUAD // F, F), ws.dtype)
        u = np.zeros((P // F, F, P // F, F), ws.dtype)
        for d in range(QUAD // F):
            b[d, :, :, :, d, :] = ws.transpose(1, 3, 2, 0)
        for d in range(P // F):
            u[d, :, d, :] = get("wb")[order][:, order].T
        basis.append(b.reshape(P, 2, QUAD))
        silu.append(u.reshape(P, P))
    return {"kan_vec": np.stack(vec, axis=1), "kan_basis": np.stack(basis, axis=1), "kan_silu": np.stack(silu, axis=1)}


def lay_out(inputs):
    a = {k: np.asarray(v) for k, v in inputs.items()}
    per_channel = lambda v: np.ascontiguousarray(np.tile(v, GROUP)[:, None])
    d = {"x": np.ascontiguousarray(a["x"])}
    d["w1"], d["w2"] = conv_weights(a["L0_conv_w1"]), conv_weights(a["L0_conv_w2"])
    d["b1"], d["b2"] = per_channel(a["L0_conv_b1"]), per_channel(a["L0_conv_b2"])
    d["bn"] = np.concatenate([per_channel(a["L0_conv_" + k]) for k in ("g1", "beta1", "g2", "beta2")], axis=1)
    for n in ("wp1", "wp2"):
        for z in "ri":
            d[n + z] = np.ascontiguousarray(a[f"L1_conv_{n}{z}"].reshape(1, CH * KP))
    d["poles"] = np.ascontiguousarray(np.stack([np.stack([a[f"L1_conv_{n}{z}"].transpose(0, 2, 1).reshape(KP, CH)
                                                          for z in "ri"], axis=1) for n in ("wp1", "wp2")], axis=1))
    d["res"] = np.ascontiguousarray(np.stack([a[f"L1_conv_wr{z}"].transpose(1, 2, 0, 3).reshape(KP, CH, MODES)
                                              for z in "ri"], axis=2))
    d["x_grid"], d["t_grid"] = a["L1_conv_x_grid"], a["L1_conv_t_grid"]
    d.update(kan_arrays(a))
    d.update(shape_constants())
    return d


def kernel(**inputs):
    import concourse.bacc as bacc
    from concourse.bass_utils import run_bass_kernel_spmd

    arrays = lay_out(inputs)
    nc = bacc.Bacc("TRN2", target_bir_lowering=False, num_devices=1)
    ins = {n: nc.dram_tensor("in_" + n, v.shape, mybir.dt.from_np(v.dtype), kind="ExternalInput").ap()
           for n, v in arrays.items()}
    out = nc.dram_tensor("out", (IMAGES, CH, ROWS, COLS), F32, kind="ExternalOutput").ap()
    build_program(nc, ins, out)
    r = run_bass_kernel_spmd(nc, [{"in_" + n: v for n, v in arrays.items()}], core_ids=[0])
    return r.results[0]["out"]
```

```python
from contextlib import ExitStack

import numpy as np

import concourse.bass as bass
from concourse import mybir

F32 = mybir.dt.float32
F32R = mybir.dt.float32r
I32 = mybir.dt.int32
ALU = mybir.AluOpType
ACT = mybir.ActivationFunctionType

P = 128
QUAD = 32
IMAGES, CH, ROWS, COLS = 8, 32, 256, 256
GROUP = P // CH
HALVES = IMAGES // GROUP
BAND = 8
BANDS = ROWS // BAND
TILE = BAND * COLS
BANK = 512
BLOCKS = TILE // P
HALO = BAND + 2
PAD = COLS + 2

MAX_NORM = 1.0 - 0.0001
ATANH_MAX = float(np.arctanh(np.float64(MAX_NORM)))
EPS_NORM = 1e-5
EPS_LN = 1e-5
CLIP = 1.0 - 1e-5


def pipeline(eng, count, stages):
    deep = max(lag for lag, _ in stages)
    for t in range(deep + 1):
        for lag, step in stages:
            if t >= lag:
                step(t - lag)
    with eng.Fori(deep + 1, count) as t:
        for lag, step in stages:
            step(t - lag)
    for t in range(count, count + deep):
        for lag, step in stages:
            if t - lag < count:
                step(t - lag)


def pipeline_by_two(eng, count, stages):
    deep = max(lag for lag, _ in stages)
    first = deep + 2 - deep % 2

    def round_(number, parity):
        for lag, step in stages:
            if not isinstance(number, int) or 0 <= number - lag < count:
                step(number - lag, (parity - lag) % 2)
    for number in range(first):
        round_(number, number % 2)
    with eng.Fori(first // 2, count // 2) as t:
        for parity in range(2):
            round_(t * 2 + parity, parity)
    for number in range(count, count + deep):
        round_(number, number % 2)


def wait_past(eng, sem, value):
    if not isinstance(value, int) or value > 0:
        eng.wait_ge(sem, value)


def wait_both(eng, sem_a, value_a, sem_b, value_b):
    value_a, value_b = (v if isinstance(v, int) else eng.to_reg(v) for v in (value_a, value_b))
    wait_past(eng, sem_a, value_a)
    wait_past(eng, sem_b, value_b)


def rsqrt_steps(dve, y, q, t):
    dve.tensor_scalar(y.bitcast(I32), q.bitcast(I32), -0.5, 1597463007.0, ALU.mult, ALU.add)
    for _ in range(3):
        dve.drain()
        dve.tensor_tensor(t, y, y, ALU.mult)
        dve.drain()
        dve.scalar_tensor_tensor(t, t, -0.5, q, ALU.mult, ALU.mult)
        dve.drain()
        dve.scalar_tensor_tensor(y, t, 1.5, y, ALU.add, ALU.mult)
    dve.drain()


def split_hi_lo(dve, hi, lo, s):
    dve.tensor_copy(hi.bitcast(F32R), s)
    dve.drain()
    return dve.tensor_tensor(lo.bitcast(F32R), s, hi, ALU.subtract)


class Net:

    def __init__(self, nc, ctx, ins):
        self.nc, self.ctx, self.ins = nc, ctx, ins
        self.count, self.sems, self.c = 0, {}, {}

    def sb(self, ctx, name, shape, dt=F32):
        self.count += 1
        return ctx.enter_context(self.nc.sbuf_tensor(f"{name}_{self.count}", shape, dt))

    def ps(self, ctx, name, shape):
        self.count += 1
        return ctx.enter_context(self.nc.psum_tensor(f"{name}_{self.count}", shape, F32))

    def sem(self, ctx, name):
        self.count += 1
        if ctx not in self.sems:
            self.sems[ctx] = []
            ctx.callback(self.clear, ctx)
        self.sems[ctx].append(self.nc.alloc_semaphore(f"{name}_{self.count}"))
        return self.sems[ctx][-1]

    def clear(self, ctx):
        self.nc.clear_and_free_semaphores(self.sems.pop(ctx))
        self.nc.all_engine_barrier()

    def scratch(self, name):
        return self.nc.dram_tensor(name, [BANDS, HALVES, P, TILE], F32).ap()


def load_constants(net, ctx, names):
    nc, ins = net.nc, net.ins
    selections = [n for n in names if n.startswith("c_sel")]
    own = {n: net.sb(ctx, n, list(ins[n].shape), F32R if n in selections else F32) for n in names}
    net.c.update({n.removeprefix("c_"): tile for n, tile in own.items()})
    with ExitStack() as local:
        staged = {n: net.sb(local, "staged", list(ins[n].shape)) for n in selections}
        loaded = net.sem(local, "loaded")
        block = local.enter_context(nc.Block())

        @block.sync
        def _(sp):
            for n in names:
                sp.dma_start(staged.get(n, own[n])[:], ins[n]).then_inc(loaded, 16)

        @block.vector
        def _(dve):
            dve.wait_ge(loaded, 16 * len(names))
            for n in selections:
                nc.vector.tensor_copy(own[n][:], staged[n][:])
            nc.vector.drain()


def norm_vectors(net, stats, average, eps, scale, bias, gamma=None, beta=None):
    nc = net.nc
    n = stats.shape[1]
    with ExitStack() as local:
        mv = net.sb(local, "mean_var", [P, n, 2])
        mean = net.sb(local, "mean", [P, n])
        spread = net.sb(local, "spread", [P, n])
        y = net.sb(local, "rstd", [P, n])
        t = net.sb(local, "t", [P, n])
        pm = net.ps(local, "pm", [P, 2, BANK])
        matrix = net.sb(local, "average", [P, P])
        loaded, own, gmean, sp_ready, gvar = (net.sem(local, k) for k in ("loaded", "own", "gmean", "spread", "gvar"))
        block = local.enter_context(nc.Block())

        @block.sync
        def _(sp):
            sp.dma_start(matrix[:], net.ins["c_" + average]).then_inc(loaded, 16)

        @block.tensor
        def _(pe):
            pe.wait_ge(loaded, 16)
            pe.wait_ge(own, 1)
            nc.tensor.matmul(pm[:, 0, 0:n], matrix[:], mv[:, :, 0], start=True, stop=True).then_inc(gmean, 1)
            pe.wait_ge(sp_ready, 1)
            nc.tensor.matmul(pm[:, 1, 0:n], matrix[:], spread[:], start=True, stop=True).then_inc(gvar, 1)

        @block.vector
        def _(dve):
            v = nc.vector
            for h in range(n):
                v.bn_aggr(mv[:, h, :], stats[:, h])
            v.drain()
            v.tensor_copy(t[:], mv[:, :, 0]).then_inc(own, 1)
            dve.wait_ge(gmean, 1)
            v.tensor_copy(mean[:], pm[:, 0, 0:n])
            v.drain()
            v.tensor_tensor(t[:], mv[:, :, 0], mean[:], ALU.subtract)
            v.drain()
            v.tensor_tensor(t[:], t[:], t[:], ALU.mult)
            v.drain()
            v.tensor_tensor(spread[:], t[:], mv[:, :, 1], ALU.add).then_inc(sp_ready, 1)
            dve.wait_ge(gvar, 1)
            v.tensor_scalar(spread[:], pm[:, 1, 0:n], eps, None, ALU.add)
            v.drain()
            rsqrt_steps(v, y[:], spread[:], t[:])
            if gamma is None:
                v.tensor_copy(scale, y[:])
            else:
                v.tensor_scalar(scale, y[:], gamma, None, ALU.mult)
            v.drain()
            v.tensor_tensor(t[:], mean[:], scale, ALU.mult)
            v.drain()
            if beta is None:
                v.tensor_scalar(bias, t[:], -1.0, None, ALU.mult)
            else:
                v.tensor_scalar(bias, t[:], -1.0, beta, ALU.mult, ALU.add)
            v.drain()


def input_stats(net, x_rows, stats):
    nc = net.nc
    span = 2
    with ExitStack() as local:
        xt = net.sb(local, "xt", [P, HALVES, span * TILE])
        part = net.sb(local, "part", [P, HALVES, span * TILE // BANK * 6])
        loaded = [net.sem(local, f"loaded{h}") for h in range(HALVES)]
        used = [net.sem(local, f"used{h}") for h in range(HALVES)]
        block = local.enter_context(nc.Block())
        wide = x_rows.rearrange("p (t n) -> p t n", n=span * TILE)
        into = stats.rearrange("p h (t n) -> p h t n", n=span * TILE // BANK * 6)

        @block.sync
        def _(sp):
            def load(t):
                for h in range(HALVES):
                    wait_past(sp, used[h], t)
                    sp.dma_start(xt[:, h, :], wide[P * h:P * h + P, t, :]).then_inc(loaded[h], 16)
            pipeline(sp, BANDS // span, [(0, load)])

        @block.vector
        def _(dve):
            v = nc.vector

            def measure(t):
                for h in range(HALVES):
                    dve.wait_ge(loaded[h], 16 * t + 16)
                    for k in range(span * TILE // BANK):
                        last = v.bn_stats(part[:, h, 6 * k:6 * k + 6], xt[:, h, BANK * k:BANK * k + BANK])
                    last.then_inc(used[h], 1)
                    v.drain()
                    v.tensor_copy(into[:, h, t, :], part[:, h, :])
            pipeline(dve, BANDS // span, [(0, measure)])


def conv_layer(net, source, scale, bias, weights, conv_bias, target, stats, first):
    nc, c = net.nc, net.c
    HT = HALO * COLS
    with ExitStack() as local:
        def sb(name, shape, dt=F32):
            return net.sb(local, name, shape, dt)
        xt = sb("xt", [P, HALVES, HALO, COLS])
        xn = sb("xn", [P, HALVES, HT])
        sq = sb("sq", [P, HALVES, HT])
        u = sb("u", [P, HALVES, HALO, PAD])
        uc = sb("uc", [P, HALVES, GROUP, BAND // 2, PAD])
        v_sb = sb("v", [P, 2, HALVES, TILE])
        sqv = sb("sqv", [P, HALVES, TILE])
        w_sb = sb("w", [P, 2, 3, CH])
        cb = sb("cb", [P, 1])
        edge = sb("edge", [P, BANDS])
        part = sb("part", [P, HALVES, TILE // BANK * 6])
        n2, q, rn, t_, nc_, l1, l2, sl, pl, xx = (sb(k, [P, COLS]) for k in
                                                  ("n2", "q", "rn", "t", "nclip", "l1", "l2", "sl", "pl", "xx"))
        sp1 = sb("sp1", [P, 2, COLS])
        q2, y2, t2, m2 = (sb(k, [P, COLS]) for k in ("q2", "y2", "t2", "m2"))
        sp2 = sb("sp2", [P, 2, COLS])
        pc1 = net.ps(local, "pc1", [P, BANK])[:, 0:COLS]
        pc2 = net.ps(local, "pc2", [P, BANK])[:, 0:COLS]
        spread1 = net.ps(local, "spread1", [P, 2, BANK])
        spread2 = net.ps(local, "spread2", [P, 2, BANK])
        conv = net.ps(local, "conv", [P, 2, BANK])

        def sem(name):
            return net.sem(local, name)
        loaded = [sem(f"loaded{h}") for h in range(2)]
        uc_loaded = [sem(f"uc_loaded{h}") for h in range(2)]
        stored = [[sem(f"stored{parity}{h}") for h in range(2)] for parity in range(2)]
        ready = sem("params")
        zeroed = sem("zeroed")
        (normed, squared, summed1, normsq, logs, factors1, spread1_ready, u_ready, conv_ready, evacuated, summed2,
         factors2, spread2_ready, out_ready, measured, read1, read2) = (sem(k) for k in (
             "normed", "squared", "summed1", "normsq", "logs", "factors1", "spread1_ready", "u_ready", "conv_ready",
             "evacuated", "summed2", "factors2", "spread2_ready", "out_ready", "measured", "read1", "read2"))
        block = local.enter_context(nc.Block())
        CHUNKS1 = HT // BANK
        CHUNKS2 = TILE // BANK

        @block.sync
        def _(sp):
            sp.dma_start(w_sb[:], weights).then_inc(ready, 16)
            sp.dma_start(cb[:], conv_bias).then_inc(ready, 16)
            sp.dma_start(edge[:], net.ins["c_edge"]).then_inc(ready, 16)

            def load(r, _):
                for h in range(HALVES):
                    wait_past(sp, squared, 2 * (r - 1) + h + 1)
                    if first:
                        rows = source[P * h:P * h + P, :].rearrange("p (r w) -> p r w", w=COLS)
                        bands = source[P * h:P * h + P, :].rearrange("p (t n) -> p t n", n=TILE)
                        main = bands[:, r, :]
                        above = rows[:, (r * BAND + ROWS - 1) % ROWS, :]
                        below = rows[:, (r * BAND + BAND) % ROWS, :]
                    else:
                        main = source[r, h]
                        above = source[(r + BANDS - 1) % BANDS, h, :, (BAND - 1) * COLS:]
                        below = source[(r + 1) % BANDS, h, :, 0:COLS]
                    sp.dma_start(xt[:, h, 1:BAND + 1, :].rearrange("p r w -> p (r w)"), main).then_inc(loaded[h], 16)
                    sp.dma_start(xt[:, h, 0, :], above).then_inc(loaded[h], 16)
                    sp.dma_start(xt[:, h, BAND + 1, :], below).then_inc(loaded[h], 16)

            def regroup(r, h):
                wait_both(sp, u_ready, (2 * r + h + 1) * CHUNKS1, conv_ready, (2 * (r - 1) + h + 1) * 4)
                for b in range(GROUP):
                    for k in range(4):
                        sp.dma_start(uc[QUAD * k:QUAD * k + QUAD, h, b, :, :],
                                     u[QUAD * b:QUAD * b + QUAD, h, k:k + BAND - 1:2, :]).then_inc(uc_loaded[h], 16)

            def store(r, parity, h):
                sp.wait_ge(out_ready, (2 * r + h + 1) * CHUNKS2)
                sp.dma_start(target[r, h], v_sb[:, parity, h, :]).then_inc(stored[parity][h], 16)
            pipeline_by_two(sp, BANDS, [(0, load), (3, lambda r, parity: store(r, parity, 0)), (1, lambda r, _: regroup(r, 0)),
                                        (1, lambda r, _: regroup(r, 1)), (3, lambda r, parity: store(r, parity, 1))])
            for parity in range(2):
                for h in range(HALVES):
                    sp.wait_ge(stored[parity][h], 16 * BANDS // 2)

        @block.scalar
        def _(act):
            a = nc.scalar
            act.wait_ge(ready, 48)

            def squares(r, _):
                for h in range(HALVES):
                    wait_past(act, summed1, 2 * (r - 1) + h + 1)
                    act.wait_ge(loaded[h], 48 * r + 48)
                    wait_past(act, u_ready, (2 * (r - 1) + h + 1) * CHUNKS1)
                    src = xt[:, h].rearrange("p r w -> p (r w)")
                    scale_h, bias_h = (vec[:, h:h + 1] if first else vec for vec in (scale, bias))
                    a.activation(xn[:, h, :], src, ACT.Identity if first else ACT.Relu, bias=bias_h, scale=scale_h).then_inc(normed, 1)
                    a.activation(sq[:, h, :], src, ACT.Square, bias=bias_h, scale=scale_h).then_inc(squared, 1)

            def logarithms(r, _):
                act.wait_ge(normsq, r + 1)
                a.activation(l1[:], nc_[:], ACT.Ln, bias=1.0, scale=1.0)
                a.activation(l2[:], nc_[:], ACT.Ln, bias=1.0, scale=-1.0).then_inc(logs, 1)

            def evacuate(r, parity, h, groups):
                if groups[0] == 0:
                    wait_past(act, stored[parity][h], 8 * (r - parity))
                    wait_past(act, measured, 2 * (r - 2) + h + 1)
                    wait_past(act, summed2, 2 * (r - 1) + h + 1)
                for k in groups:
                    p, o = k // 2, k % 2
                    act.wait_ge(conv_ready, (2 * r + h) * 4 + k + 1)
                    src = conv[:, k % 2, :].rearrange("p (i w) -> p i w", i=2)
                    rows = slice(4 * p + o, 4 * p + o + 3, 2)
                    v_rows, sq_rows = (tile_.rearrange("p (r w) -> p r w", w=COLS)[:, rows, :]
                                       for tile_ in (v_sb[:, parity, h, :], sqv[:, h, :]))
                    a.activation(v_rows, src, ACT.Identity, bias=cb[:, 0:1])
                    a.activation(sq_rows, src, ACT.Square, bias=cb[:, 0:1]).then_inc(evacuated, 1)
            pipeline_by_two(act, BANDS, [(2, lambda r, parity: evacuate(r, parity, 0, range(4)))] + ([(1, logarithms)] if first else []) +
                            [(2, lambda r, parity: evacuate(r, parity, 1, (0, 1, 2))), (0, squares),
                             (2, lambda r, parity: evacuate(r, parity, 1, (3,)))])

        @block.tensor
        def _(pe):
            m = nc.tensor
            pe.wait_ge(ready, 48)

            def sum_squares(r):
                wait_past(pe, read1, r)
                for h in range(HALVES):
                    pe.wait_ge(squared, 2 * r + h + 1)
                    for k in range(HALO):
                        b = HALO * h + k
                        q4 = QUAD * (b % 4)
                        last = m.matmul(pc1[q4:q4 + QUAD, :], c["ones"][:, b // 4, :], sq[:, h, COLS * k:COLS * k + COLS],
                                        start=(b < 4), stop=(b >= HALVES * HALO - 4), tile_position=(0, q4))
                    last.then_inc(summed1, 1)

            def spread_out(r, h):
                pe.wait_ge(factors2, r + 1)
                for k in range(CHUNKS2):
                    n = (2 * r + h) * CHUNKS2 + k
                    wait_past(pe, out_ready, n - 1)
                    for j in range(BANK // COLS):
                        for z in range(2):
                            last = m.matmul(spread2[:, k % 2, COLS * j:COLS * j + COLS], c["sel"][:, BAND * h + 2 * k + j, :],
                                            sp2[:, z, :].bitcast(F32R), start=(z == 0), stop=(z == 1))
                    last.then_inc(spread2_ready, 1)

            def convolve(r, h, groups):
                pe.wait_ge(uc_loaded[h], (r + 1) * 256)
                for k in groups:
                    p, o = k // 2, k % 2
                    wait_past(pe, evacuated, (2 * r + h) * 4 + k - 1)
                    for d in range(3):
                        for b in range(GROUP):
                            last = m.matmul(conv[QUAD * b:QUAD * b + QUAD, k % 2, :], w_sb[:, o, d, :],
                                            uc[:, h, b, 2 * p:2 * p + 2, d:d + COLS], start=(d == 0), stop=(d == 2),
                                            tile_position=(0, QUAD * b))
                    last.then_inc(conv_ready, 1)

            def spread_u(r):
                pe.wait_ge(factors1, r + 1)
                for h in range(HALVES):
                    for k in range(CHUNKS1):
                        n = (2 * r + h) * CHUNKS1 + k
                        wait_past(pe, u_ready, n - 1)
                        for j in range(BANK // COLS):
                            for z in range(2):
                                last = m.matmul(spread1[:, (h * CHUNKS1 + k) % 2, COLS * j:COLS * j + COLS],
                                                c["sel"][:, HALO * h + 2 * k + j, :],
                                                sp1[:, z, :].bitcast(F32R), start=(z == 0), stop=(z == 1))
                        last.then_inc(spread1_ready, 1)

            def sum_out(r):
                wait_past(pe, read2, r)
                for h in range(HALVES):
                    pe.wait_ge(evacuated, (2 * r + h + 1) * 4)
                    for k in range(BAND):
                        b = BAND * h + k
                        q4 = QUAD * (b % 4)
                        last = m.matmul(pc2[q4:q4 + QUAD, :], c["ones"][:, b // 4, :], sqv[:, h, COLS * k:COLS * k + COLS],
                                        start=(b < 4), stop=(b >= HALVES * BAND - 4), tile_position=(0, q4))
                    last.then_inc(summed2, 1)
            pipeline(pe, BANDS, [(2, lambda r: convolve(r, 0, range(4))), (2, lambda r: convolve(r, 1, (0, 1))),
                                 (3, lambda r: spread_out(r, 0)), (2, lambda r: convolve(r, 1, (2,))), (1, spread_u),
                                 (3, lambda r: spread_out(r, 1)), (2, lambda r: convolve(r, 1, (3,))), (0, sum_squares),
                                 (2, sum_out)])

        @block.vector
        def _(dve):
            v = nc.vector
            v.memset(u[:, :, :, 0:1], 0.0)
            v.memset(u[:, :, :, PAD - 1:PAD], 0.0)
            v.drain()
            dve.wait_ge(ready, 48)

            def norms_u(r, _):
                dve.wait_ge(summed1, 2 * r + 2)
                v.tensor_copy(n2[:], pc1).then_inc(read1, 1)
                v.drain()
                v.tensor_scalar(q[:], n2[:], EPS_NORM * EPS_NORM, None, ALU.max)
                v.drain()
                rsqrt_steps(v, rn[:], q[:], t_[:])
                if first:
                    v.tensor_tensor(nc_[:], q[:], rn[:], ALU.mult)
                    v.drain()
                    v.tensor_scalar(nc_[:], nc_[:], CLIP, None, ALU.min).then_inc(normsq, 1)
                    v.tensor_scalar(xx[:], q[:], 0.05, None, ALU.min)
                    v.drain()
                    v.tensor_scalar(pl[:], xx[:], 1.0 / 11, None, ALU.mult)
                    for k in (9, 7, 5, 3):
                        v.drain()
                        v.scalar_tensor_tensor(pl[:], pl[:], 1.0 / k, xx[:], ALU.add, ALU.mult)
                else:
                    v.tensor_scalar(sl[:], rn[:], ATANH_MAX, 1.0, ALU.mult, ALU.min).then_inc(normsq, 1)
                v.drain()

            def factors_u(r, _):
                if first:
                    dve.wait_ge(logs, r + 1)
                    v.tensor_tensor(sl[:], l1[:], l2[:], ALU.subtract)
                    v.drain()
                    v.scalar_tensor_tensor(sl[:], sl[:], 0.5, rn[:], ALU.mult, ALU.mult)
                    v.tensor_scalar(t_[:], q[:], 0.04, None, ALU.is_lt)
                    v.drain()
                    v.scalar_tensor_tensor(pl[:], pl[:], 1.0, sl[:], ALU.add, ALU.subtract)
                    v.drain()
                    v.tensor_tensor(pl[:], pl[:], t_[:], ALU.mult)
                    v.drain()
                    v.tensor_tensor(sl[:], sl[:], pl[:], ALU.add)
                    v.drain()
                v.tensor_scalar(sl[:], sl[:], edge[:, bass.ds(r, 1)], None, ALU.mult)
                v.drain()
                wait_past(dve, spread1_ready, 2 * r * CHUNKS1)
                split_hi_lo(v, sp1[:, 0, :], sp1[:, 1, :], sl[:]).then_inc(factors1, 1)

            def products_out(r, parity, h):
                for k in range(CHUNKS2):
                    dve.wait_ge(spread2_ready, (2 * r + h) * CHUNKS2 + k + 1)
                    cols = slice(BANK * k, BANK * k + BANK)
                    v.tensor_tensor(v_sb[:, parity, h, cols], v_sb[:, parity, h, cols], spread2[:, k % 2, :],
                                    ALU.mult).then_inc(out_ready, 1)
                v.drain()
                for k in range(CHUNKS2):
                    last = v.bn_stats(part[:, h, 6 * k:6 * k + 6], v_sb[:, parity, h, BANK * k:BANK * k + BANK])
                last.then_inc(measured, 1)
                v.drain()
                v.tensor_copy(stats[:, h, r, :], part[:, h, :])

            def products_u(r, _):
                for h in range(HALVES):
                    wait_past(dve, uc_loaded[h], 256 * r)
                    dve.wait_ge(normed, 2 * r + h + 1)
                    for k in range(CHUNKS1):
                        dve.wait_ge(spread1_ready, (2 * r + h) * CHUNKS1 + k + 1)
                        v.tensor_tensor(u[:, h, 2 * k:2 * k + 2, 1:COLS + 1],
                                        xn[:, h, BANK * k:BANK * k + BANK].rearrange("p (r w) -> p r w", w=COLS),
                                        spread1[:, (h * CHUNKS1 + k) % 2, :].rearrange("p (r w) -> p r w", w=COLS),
                                        ALU.mult).then_inc(u_ready, 1)

            def factors_out(r, _):
                dve.wait_ge(summed2, 2 * r + 2)
                v.tensor_scalar(q2[:], pc2, EPS_NORM * EPS_NORM, None, ALU.max).then_inc(read2, 1)
                v.drain()
                rsqrt_steps(v, y2[:], q2[:], t2[:])
                v.tensor_scalar(m2[:], y2[:], ATANH_MAX, 1.0, ALU.mult, ALU.min)
                v.drain()
                wait_past(dve, spread2_ready, 2 * r * CHUNKS2)
                split_hi_lo(v, sp2[:, 0, :], sp2[:, 1, :], m2[:]).then_inc(factors2, 1)
            pipeline_by_two(dve, BANDS, [(1, norms_u), (3, factors_out), (1, factors_u), (3, lambda r, parity: products_out(r, parity, 0)),
                                  (1, products_u), (3, lambda r, parity: products_out(r, parity, 1))])


def residual_layer(net, x_rows, source, scale, bias, target, stats):
    nc, c = net.nc, net.c
    CHUNKS = TILE // BANK
    with ExitStack() as local:
        def sb(name, shape, dt=F32):
            return net.sb(local, name, shape, dt)
        xt, sqh, sqr, o_sb, x1 = (sb(k, [P, HALVES, TILE]) for k in ("xt", "sqh", "sqr", "o", "x1"))
        tt, r_sb = (sb(k, [P, 2, HALVES, TILE]) for k in ("tt", "r"))
        squares_of, y, t_ = (sb(k, [P, 2, P]) for k in ("squares_of", "y", "t"))
        m, n, th = (sb(k, [P, P]) for k in ("m", "n", "th"))
        parts = sb("parts", [P, 2, P])
        part = sb("part", [P, HALVES, CHUNKS * 6])
        sums = net.ps(local, "sums", [P, 2, BANK])[:, :, 0:P]
        spread = net.ps(local, "spread", [P, 2, BANK])

        def sem(name):
            return net.sem(local, name)
        x_loaded, stored = ([sem(f"{k}{h}") for h in range(2)] for k in ("x_loaded", "stored"))
        loaded = [[sem(f"loaded{parity}{h}") for h in range(2)] for parity in range(2)]
        rectified, squared, summed, read, norms, tanhs, factors, spread_ready, o_ready, x1_ready, measured = (
            sem(k) for k in ("rectified", "squared", "summed", "read", "norms", "tanhs", "factors", "spread_ready",
                             "o_ready", "x1_ready", "measured"))
        block = local.enter_context(nc.Block())

        @block.sync
        def _(sp):
            def load(r, parity):
                for h in range(HALVES):
                    wait_past(sp, squared, 2 * (r - 2) + h + 1)
                    sp.dma_start(tt[:, parity, h, :], source[r, h]).then_inc(loaded[parity][h], 16)

            def load_x(r, _):
                for h in range(HALVES):
                    wait_past(sp, x1_ready, 2 * (r - 1) + h + 1)
                    bands = x_rows[P * h:P * h + P, :].rearrange("p (t n) -> p t n", n=TILE)
                    sp.dma_start(xt[:, h, :], bands[:, r, :]).then_inc(x_loaded[h], 16)

            def store(r, _):
                for h in range(HALVES):
                    sp.wait_ge(x1_ready, 2 * r + h + 1)
                    sp.dma_start(target[r, h], x1[:, h, :]).then_inc(stored[h], 16)
            pipeline_by_two(sp, BANDS, [(0, load), (2, store), (1, load_x)])
            for h in range(HALVES):
                sp.wait_ge(stored[h], 16 * BANDS)

        @block.scalar
        def _(act):
            a = nc.scalar

            def squares(r, parity, h):
                act.wait_ge(loaded[parity][h], 8 * (r - parity) + 16)
                wait_past(act, o_ready, (2 * (r - 2) + h + 1) * CHUNKS)
                wait_past(act, squared, 2 * (r - 2) + h + 1)
                t, rectified_t = tt[:, parity, h, :], r_sb[:, parity, h, :]
                a.activation(rectified_t, t, ACT.Relu, bias=bias, scale=scale).then_inc(rectified, 1)
                wait_past(act, summed, 2 * (r - 1) + h + 1)
                a.activation(sqh[:, h, :], t, ACT.Square, bias=bias, scale=scale)
                act.wait_ge(rectified, 2 * r + h + 1)
                a.activation(sqr[:, h, :], rectified_t, ACT.Square).then_inc(squared, 1)

            def tangents(r, _):
                act.wait_ge(norms, r + 1)
                a.activation(th[:], n[:], ACT.Tanh).then_inc(tanhs, 1)
            pipeline_by_two(act, BANDS, [(0, lambda r, parity: squares(r, parity, 0)),
                                         (0, lambda r, parity: squares(r, parity, 1)), (1, tangents)])

        @block.tensor
        def _(pe):
            mm = nc.tensor

            def sum_squares(r, h):
                if h == 0:
                    wait_past(pe, read, r)
                pe.wait_ge(squared, 2 * r + h + 1)
                for kind, src in enumerate((sqh, sqr)):
                    for k in range(BLOCKS):
                        b = BLOCKS * h + k
                        q4 = QUAD * (b % 4)
                        last = mm.matmul(sums[q4:q4 + QUAD, kind, :], c["ones"][:, b // 4, :], src[:, h, P * k:P * k + P],
                                         start=(b < 4), stop=(b >= 2 * BLOCKS - 4), tile_position=(0, q4))
                last.then_inc(summed, 1)

            def spread_factors(r, h):
                pe.wait_ge(factors, r + 1)
                for k in range(CHUNKS):
                    wait_past(pe, o_ready, (2 * r + h) * CHUNKS + k - 1)
                    for j in range(4):
                        for z in range(2):
                            last = mm.matmul(spread[:, k % 2, P * j:P * j + P], c["sel"][:, BLOCKS * h + 4 * k + j, :],
                                             parts[:, z, :].bitcast(F32R), start=(z == 0), stop=(z == 1))
                    last.then_inc(spread_ready, 1)
            pipeline(pe, BANDS, [(0, lambda r: sum_squares(r, 0)), (0, lambda r: sum_squares(r, 1)),
                                 (1, lambda r: spread_factors(r, 0)), (1, lambda r: spread_factors(r, 1))])

        @block.gpsimd
        def _(pool):
            def add(r):
                for h in range(HALVES):
                    pool.wait_ge(o_ready, (2 * r + h + 1) * CHUNKS)
                    pool.wait_ge(x_loaded[h], 16 * r + 16)
                    wait_past(pool, stored[h], 16 * r)
                    wait_past(pool, measured, 2 * (r - 1) + h + 1)
                    nc.gpsimd.tensor_tensor(x1[:, h, :], o_sb[:, h, :], xt[:, h, :], ALU.add).then_inc(x1_ready, 1)
            pipeline(pool, BANDS, [(0, add)])

        @block.vector
        def _(dve):
            v = nc.vector
            def product(r, parity, h, k):
                if k == 0:
                    wait_past(dve, x1_ready, 2 * (r - 1) + h + 1)
                cols = slice(BANK * k, BANK * k + BANK)
                dve.wait_ge(spread_ready, (2 * r + h) * CHUNKS + k + 1)
                v.tensor_tensor(o_sb[:, h, cols], r_sb[:, parity, h, cols], spread[:, k % 2, :], ALU.mult).then_inc(o_ready, 1)

            def factor(r, _):
                dve.wait_ge(summed, 2 * r + 2)
                v.tensor_scalar(squares_of[:, 0], sums[:, 0], EPS_NORM * EPS_NORM, None, ALU.max)
                v.tensor_scalar(squares_of[:, 1], sums[:, 1], 1e-30, None, ALU.max).then_inc(read, 1)
                v.drain()
                rsqrt_steps(v, y[:], squares_of[:], t_[:])
                v.tensor_scalar(m[:], y[:, 0], ATANH_MAX, 1.0, ALU.mult, ALU.min)
                v.tensor_tensor(n[:], squares_of[:, 1], y[:, 1], ALU.mult)
                v.drain()
                v.tensor_tensor(n[:], n[:], m[:], ALU.mult)
                v.drain()
                v.tensor_scalar(n[:], n[:], EPS_NORM, None, ALU.max).then_inc(norms, 1)
                v.drain()
                v.reciprocal(t_[:, 0], n[:])
                v.drain()
                v.tensor_tensor(m[:], m[:], t_[:, 0], ALU.mult)
                v.drain()
                dve.wait_ge(tanhs, r + 1)
                v.scalar_tensor_tensor(m[:], th[:], MAX_NORM, m[:], ALU.min, ALU.mult)
                v.drain()
                wait_past(dve, spread_ready, 2 * r * CHUNKS)
                split_hi_lo(v, parts[:, 0, :], parts[:, 1, :], m[:]).then_inc(factors, 1)

            def measure(r, h, k):
                if k == 0:
                    dve.wait_ge(x1_ready, 2 * r + h + 1)
                last = v.bn_stats(part[:, h, 6 * k:6 * k + 6], x1[:, h, BANK * k:BANK * k + BANK])
                if k == CHUNKS - 1:
                    last.then_inc(measured, 1)
                    v.drain()
                    v.tensor_copy(stats[:, h, r, :], part[:, h, :])
                    v.drain()

            stages = [(1, factor)]
            for h in range(HALVES):
                for k in range(CHUNKS):
                    stages.append((1, lambda r, parity, h=h, k=k: product(r, parity, h, k)))
                    stages.append((2, lambda r, parity, h=h, k=k: measure(r, h, k)))
            pipeline_by_two(dve, BANDS, stages)


MODES = 4
KP = CH * MODES
SUB = ROWS // 2


def spread_table(net, vectors, table):
    nc = net.nc
    with ExitStack() as local:
        wide = net.sb(local, "wide", [P, HALVES, P])
        rows = net.ps(local, "rows", [P, HALVES, P])
        ready, done = net.sem(local, "wide_ready"), net.sem(local, "rows_ready")
        block = local.enter_context(nc.Block())

        @block.vector
        def _(dve):
            nc.vector.tensor_copy(wide[:], vectors.unsqueeze(2).to_broadcast([P, HALVES, P])).then_inc(ready, 1)
            dve.wait_ge(done, 1)
            nc.vector.tensor_copy(table.rearrange("p (h n) -> p h n", h=HALVES), rows[:])

        @block.tensor
        def _(pe):
            pe.wait_ge(ready, 1)
            for h in range(HALVES):
                last = nc.tensor.matmul(rows[:, h, :], wide[:, h, :], net.c["ident"][:], start=True, stop=True)
            last.then_inc(done, 1)


def pole_kernels(net, g1, g2):
    nc, ins = net.nc, net.ins
    N = CH * KP
    with ExitStack() as local:
        wr, wi = (net.sb(local, k, [P, 2, N]) for k in ("wr", "wi"))
        den, re, im = (net.sb(local, k, [P, 2, BANK]) for k in ("den", "re", "im"))
        dft = net.sb(local, "dft", [P, 3, P])
        grid, lam = net.sb(local, "grid", [P, 2, 3]), net.sb(local, "lam", [P, 2])
        freq = net.sb(local, "freq", [P, 1])
        acc = net.ps(local, "acc", [P, 2, 2, BANK])
        consts, inverse, transformed, kept = (net.sem(local, k) for k in ("consts", "inverse", "transformed", "kept"))
        poles = [net.sem(local, f"poles{n}") for n in range(2)]
        block = local.enter_context(nc.Block())
        CHUNKS = N // BANK
        PER = BANK // KP

        @block.sync
        def _(sp):
            sp.dma_start(dft[:], ins["c_dft"]).then_inc(consts, 16)
            sp.dma_start(freq[:], ins["c_freq"]).then_inc(consts, 16)
            for n, name in enumerate(("x_grid", "t_grid")):
                sp.dma_start(grid[:, n, :], ins[name][:, 0:3].to_broadcast([P, 3])).then_inc(consts, 16)
            for n, name in enumerate(("wp1", "wp2")):
                sp.dma_start(wr[:, n, :], ins[name + "r"].to_broadcast([P, N])).then_inc(poles[n], 16)
                sp.dma_start(wi[:, n, :], ins[name + "i"].to_broadcast([P, N])).then_inc(poles[n], 16)

        @block.vector
        def _(dve):
            v = nc.vector
            dve.wait_ge(consts, 64)
            v.tensor_tensor(lam[:], grid[:, :, 2], grid[:, :, 0], ALU.subtract)
            v.drain()
            v.reciprocal(lam[:], lam[:])
            v.drain()
            v.tensor_scalar(lam[:], lam[:], freq[:, 0:1], 2.0 * np.pi, ALU.mult, ALU.mult)
            v.drain()
            for n in range(2):
                dve.wait_ge(poles[n], 32)
                for k in range(CHUNKS):
                    wr_k, wi_k = (tile_[:, n, BANK * k:BANK * k + BANK] for tile_ in (wr, wi))
                    den_k, re_k, im_k = (tile_[:, k % 2, :] for tile_ in (den, re, im))
                    wait_past(dve, transformed, n * CHUNKS + k - 1)
                    v.tensor_scalar(wi_k, wi_k, lam[:, n:n + 1], None, ALU.subtract)
                    v.tensor_tensor(re_k, wr_k, wr_k, ALU.mult)
                    v.drain()
                    v.tensor_tensor(den_k, wi_k, wi_k, ALU.mult)
                    v.drain()
                    v.tensor_tensor(den_k, den_k, re_k, ALU.add)
                    v.drain()
                    v.reciprocal(den_k, den_k)
                    v.drain()
                    v.tensor_tensor(re_k, wr_k, den_k, ALU.mult)
                    v.scalar_tensor_tensor(im_k, wi_k, -1.0, den_k, ALU.mult, ALU.mult).then_inc(inverse, 1)
            v.drain()

        @block.tensor
        def _(pe):
            m = nc.tensor
            for n in range(2):
                for k in range(CHUNKS):
                    pe.wait_ge(inverse, n * CHUNKS + k + 1)
                    wait_past(pe, kept, n * CHUNKS + k - 1)
                    m.matmul(acc[:, k % 2, 0, :], dft[:, 0, :], re[:, k % 2, :], start=True, stop=False)
                    m.matmul(acc[:, k % 2, 0, :], dft[:, 1, :], im[:, k % 2, :], start=False, stop=True)
                    m.matmul(acc[:, k % 2, 1, :], dft[:, 0, :], im[:, k % 2, :], start=True, stop=False)
                    m.matmul(acc[:, k % 2, 1, :], dft[:, 2, :], re[:, k % 2, :], start=False, stop=True).then_inc(transformed, 1)

        @block.scalar
        def _(act):
            a = nc.scalar
            for n in range(2):
                for k in range(CHUNKS):
                    act.wait_ge(transformed, n * CHUNKS + k + 1)
                    i = slice(PER * k, PER * k + PER)
                    real, imag = (acc[:, k % 2, z, :].rearrange("p (i m) -> p i m", m=KP) for z in range(2))
                    if n == 0:
                        a.copy(g1[:, i, 0, :], real)
                        a.copy(g1[:, i, 1, :], imag).then_inc(kept, 1)
                    else:
                        a.mul(g2[:, i, 0, :], imag, -1.0)
                        a.copy(g2[:, i, 1, :], real)
                        a.copy(g2[:, i, 2, :], imag).then_inc(kept, 1)


def residues(net, source, scale_table, bias_table, g1, g2, coef):
    nc, ins = net.nc, net.ins
    with ExitStack() as local:
        rows = net.sb(local, "rows", [P, 2, IMAGES, COLS])
        xs = net.sb(local, "xs", [P, IMAGES, SUB])
        t_sb = net.sb(local, "t_sb", [P, 2, IMAGES, 2, KP])
        res = net.sb(local, "res", [P, CH, 2, MODES])
        prod = net.sb(local, "prod", [P, 4, 2, 2, 2, KP])
        acc = net.sb(local, "acc", [P, 4, 2, 2, 2, KP])
        mask = net.sb(local, "mask", [P, KP])
        t_ps = net.ps(local, "t_ps", [P, 2, 2, 2, KP])
        o_ps = net.ps(local, "o_ps", [P, 4, 2, 2, KP])
        consts, t_ready, t_kept, o_ready, weighted, added, sampled = (net.sem(local, k) for k in (
            "consts", "t_ready", "t_kept", "o_ready", "weighted", "added", "sampled"))
        cleared = net.sem(local, "cleared")
        loaded = [net.sem(local, f"loaded{j}") for j in range(2)]
        block = local.enter_context(nc.Block())
        PAIRS = CH // 2

        @block.sync
        def _(sp):
            sp.dma_start(res[:], ins["res"]).then_inc(consts, 16)
            sp.dma_start(mask[:], ins["c_mask"]).then_inc(consts, 16)

            def load(t):
                for j in range(2):
                    wait_past(sp, sampled, (2 * (t - 1) + j + 1))
                    for b in range(IMAGES):
                        src = source[:, b // GROUP, CH * (b % GROUP) + 2 * t + j, :]
                        src = src.rearrange("r (y z w) -> r y z w", z=2, w=COLS)[:, :, 0, :]
                        sp.dma_start(rows[:, j, b, :], src).then_inc(loaded[j], 16)
            pipeline(sp, PAIRS, [(0, load)])

        @block.vector
        def _(dve):
            v = nc.vector

            def sample(t, j):
                dve.wait_ge(loaded[j], 128 * t + 128)
                wait_past(dve, t_ready, 4 * (2 * t + j))
                for b in range(IMAGES):
                    col = b * CH + 2 * t + j
                    last = v.tensor_scalar(xs[:, b, :], rows[:, j, b, :].rearrange("p (x z) -> p x z", z=2)[:, :, 0],
                                           scale_table[:, bass.ds(col, 1)], bias_table[:, bass.ds(col, 1)], ALU.mult, ALU.add)
                last.then_inc(sampled, 1)

            def weight(t, j, pairs):
                i = 2 * t + j
                for b in pairs:
                    dve.wait_ge(o_ready, 4 * i + b + 1)
                    wait_past(dve, added, 4 * (i - 1) + b + 1)
                    for z in range(2):
                        last = v.tensor_tensor(prod[:, b, z].rearrange("p c z (k q) -> p (c z) k q", q=MODES),
                                               o_ps[:, b].rearrange("p c z (k q) -> p (c z) k q", q=MODES),
                                               res[:, i, z, :].unsqueeze(1).unsqueeze(1).to_broadcast([P, 4, CH, MODES]),
                                               ALU.mult)
                    last.then_inc(weighted, 1)
            dve.wait_ge(consts, 32)

            v.memset(acc[:], 0.0).then_inc(cleared, 1)
            pipeline(dve, PAIRS, [(2, lambda t: weight(t, 1, (0, 1))), (1, lambda t: sample(t, 1)), (2, lambda t: weight(t, 1, (2, 3))),
                                  (1, lambda t: weight(t, 0, (0, 1))), (0, lambda t: sample(t, 0)), (1, lambda t: weight(t, 0, (2, 3)))])
            dve.wait_ge(added, 4 * CH)
            for b in range(4):
                re, im = coef[:, 2 * b:2 * b + 2, 0, :], coef[:, 2 * b:2 * b + 2, 1, :]
                v.tensor_tensor(re, acc[:, b, 0, :, 0, :], acc[:, b, 1, :, 1, :], ALU.subtract)
                v.tensor_tensor(im, acc[:, b, 0, :, 1, :], acc[:, b, 1, :, 0, :], ALU.add)
            v.drain()
            flat = coef.rearrange("p a z n -> p (a z) n")
            v.tensor_tensor(flat, flat, mask[:].unsqueeze(1).to_broadcast([P, 2 * IMAGES, KP]), ALU.mult)
            v.drain()

        @block.gpsimd
        def _(pool):
            pool.wait_ge(cleared, 1)

            def add(t):
                for j in range(2):
                    i = 2 * t + j
                    for b in range(4):
                        pool.wait_ge(weighted, 4 * i + b + 1)
                        wait_past(pool, added, 4 * (i - 1) + b + 1)
                        dst = acc[:, b].rearrange("p z c y n -> p (z c y n)")
                        nc.gpsimd.tensor_tensor(dst, dst, prod[:, b].rearrange("p z c y n -> p (z c y n)"),
                                                ALU.add).then_inc(added, 1)
            pipeline(pool, PAIRS, [(0, add)])

        @block.scalar
        def _(act):
            def keep(t):
                for j in range(2):
                    i = 2 * t + j
                    for b in range(4):
                        act.wait_ge(t_ready, 4 * i + b + 1)
                        wait_past(act, o_ready, 4 * (i - 2) + b + 1)
                        nc.scalar.copy(t_sb[:, j, 2 * b:2 * b + 2], t_ps[:, b % 2]).then_inc(t_kept, 1)
            pipeline(act, PAIRS, [(0, keep)])

        @block.tensor
        def _(pe):
            m = nc.tensor

            def first(t, j):
                i = 2 * t + j
                pe.wait_ge(sampled, i + 1)
                for b in range(4):
                    wait_past(pe, t_kept, 4 * i + b - 1)
                    for k in range(2):
                        last = m.matmul(t_ps[:, b % 2, k].rearrange("p z n -> p (z n)"), xs[:, 2 * b + k, :],
                                        g1[:, i].rearrange("p z n -> p (z n)"), start=True, stop=True)
                    last.then_inc(t_ready, 1)

            def second(t, j):
                i = 2 * t + j
                for b in range(4):
                    pe.wait_ge(t_kept, 4 * i + b + 1)
                    wait_past(pe, weighted, 4 * (i - 1) + b + 1)
                    for k in range(2):
                        dst = o_ps[:, b, k].rearrange("p z n -> p (z n)")
                        m.matmul(dst, t_sb[:, j, 2 * b + k, 0, :], g2[:, i, 1:3].rearrange("p z n -> p (z n)"),
                                 start=True, stop=False)
                        last = m.matmul(dst, t_sb[:, j, 2 * b + k, 1, :], g2[:, i, 0:2].rearrange("p z n -> p (z n)"),
                                        start=False, stop=True)
                    last.then_inc(o_ready, 1)

            pipeline(pe, PAIRS, [(0, lambda t: first(t, 0)), (1, lambda t: second(t, 1)),
                                 (0, lambda t: first(t, 1)), (0, lambda t: second(t, 0))])


TWO_PI_1 = 6.28125
TWO_PI_2 = float(np.float32(np.round((2 * np.pi - TWO_PI_1) * 2 ** 21) / 2 ** 21))
TWO_PI_3 = float(2 * np.pi - TWO_PI_1 - TWO_PI_2)
ROUND = 1.5 * 2 ** 23
PI_BELOW = 3.1415925


def evaluate_residues(net, source, coef, target, stats):
    nc, ins = net.nc, net.ins
    with ExitStack() as local:
        w = net.sb(local, "w", [P, 2, 2, CH])
        z = net.sb(local, "z", [P, 2, COLS])
        grow, ang, turns, sine, cosine = (net.sb(local, k, [P, 2, COLS]) for k in ("grow", "ang", "turns", "sin", "cos"))
        e1, e2 = net.sb(local, "e1", [P, 2, 3, COLS]), net.sb(local, "e2", [P, 2, 2, COLS])
        tmp = net.sb(local, "tmp", [P, 2, 2, COLS])
        xin, xout = net.sb(local, "xin", [P, 2, IMAGES, BANK]), net.sb(local, "xout", [P, 2, IMAGES, BANK])
        part = net.sb(local, "part", [P, IMAGES * 6])
        half_pi = net.sb(local, "half_pi", [P, 1])
        t_ps, o_ps = net.ps(local, "t_ps", [P, 2, BANK]), net.ps(local, "o_ps", [P, 2, BANK])
        consts, angles, sines, grown, waves, t_ready, t_kept, o_ready, summed, measured = (net.sem(local, k) for k in (
            "consts", "angles", "sines", "grown", "waves", "t_ready", "t_kept", "o_ready", "summed", "measured"))
        loaded = [net.sem(local, f"loaded{j}") for j in range(2)]
        stored = [net.sem(local, f"stored{j}") for j in range(2)]
        block = local.enter_context(nc.Block())
        PAIRS = CH // 2
        PREPARED, COMBINED = 1, 6

        def rows_of(tensor, a, i):
            return tensor[:, a // GROUP, CH * (a % GROUP) + i, :].rearrange("r (z n) -> r z n", n=2 * COLS)

        @block.sync
        def _(sp):
            sp.dma_start(w[:], ins["poles"]).then_inc(consts, 16)
            sp.dma_start(z[:, 0, :], ins["x_grid"].to_broadcast([P, COLS])).then_inc(consts, 16)
            sp.dma_start(z[:, 1, :], ins["t_grid"].to_broadcast([P, COLS])).then_inc(consts, 16)

            def load(t, j):
                wait_past(sp, summed, IMAGES * (2 * (t - 1) + j + 1))
                for a in range(IMAGES):
                    sp.dma_start(xin[:, j, a, :], rows_of(source, a, 2 * t + j)).then_inc(loaded[j], 16)

            def store(t, j):
                for a in range(IMAGES):
                    sp.wait_ge(summed, IMAGES * (2 * t + j) + a + 1)
                    sp.dma_start(rows_of(target, a, 2 * t + j), xout[:, j, a, :]).then_inc(stored[j], 16)
            pipeline(sp, PAIRS, [(1, lambda t: store(t, 0)), (0, lambda t: load(t, 0)),
                                 (1, lambda t: store(t, 1)), (0, lambda t: load(t, 1))])
            for j in range(2):
                sp.wait_ge(stored[j], 16 * IMAGES * PAIRS)

        @block.scalar
        def _(act):
            s = nc.scalar
            act.wait_ge(consts, 48)

            def growth(t, j):
                i = 2 * t + j
                wait_past(act, waves, i)
                for n in range(2):
                    last = s.activation(grow[:, n, :], z[:, n, :], ACT.Exp, scale=w[:, n, 0, bass.ds(i, 1)])
                last.then_inc(grown, 1)

            def waves_of(t, j):
                i = 2 * t + j
                act.wait_ge(angles, i + 1)
                s.activation(sine[:], ang[:], ACT.Sin)
                s.activation(cosine[:], turns[:], ACT.Sin, bias=half_pi[:, 0:1], scale=-1.0).then_inc(sines, 1)

            def keep(t, j, images):
                for a in images:
                    n = IMAGES * (2 * t + j) + a
                    act.wait_ge(t_ready, n + 1)
                    wait_past(act, o_ready, n - 1)
                    s.copy(tmp[:, a % 2].rearrange("p z n -> p (z n)"), t_ps[:, a % 2, :]).then_inc(t_kept, 1)
            stages = []
            for j in range(2):
                lag, other = 1 - j, 1 - j
                stages += [(1, lambda t, j=j: keep(t, j, range(0, 2))), (lag, lambda t, j=other: growth(t, j)),
                           (1, lambda t, j=j: keep(t, j, range(2, 5))), (lag, lambda t, j=other: waves_of(t, j)),
                           (1, lambda t, j=j: keep(t, j, range(5, IMAGES)))]
            pipeline(act, PAIRS, stages)

        @block.vector
        def _(dve):
            v = nc.vector
            v.memset(half_pi[:], 0.5 * np.pi)
            v.drain()
            dve.wait_ge(consts, 48)

            def prepare(t, j):
                i = 2 * t + j
                wait_past(dve, sines, i)
                for n in range(2):
                    v.tensor_scalar(ang[:, n, :], z[:, n, :], w[:, n, 1, bass.ds(i, 1)], None, ALU.mult)
                v.drain()
                v.tensor_scalar(turns[:], ang[:], float(1 / (2 * np.pi)), ROUND, ALU.mult, ALU.add)
                v.drain()
                v.tensor_scalar(turns[:], turns[:], ROUND, None, ALU.subtract)
                for c in (TWO_PI_1, TWO_PI_2, TWO_PI_3):
                    v.drain()
                    v.scalar_tensor_tensor(ang[:], turns[:], -c, ang[:], ALU.mult, ALU.add)
                v.drain()
                v.tensor_scalar(ang[:], ang[:], PI_BELOW, -PI_BELOW, ALU.min, ALU.max)
                v.drain()
                v.scalar_tensor_tensor(turns[:], ang[:], -1.0, ang[:], ALU.mult, ALU.max).then_inc(angles, 1)

            def combine(t, j):
                i = 2 * t + j
                dve.wait_ge(sines, i + 1)
                dve.wait_ge(grown, i + 1)
                wait_past(dve, o_ready, IMAGES * (i - 1))
                v.tensor_tensor(e1[:, j, 1, :], grow[:, 0, :], cosine[:, 0, :], ALU.mult)
                v.tensor_tensor(e1[:, j, 2, :], grow[:, 0, :], sine[:, 0, :], ALU.mult)
                v.scalar_tensor_tensor(e1[:, j, 0, :], grow[:, 0, :], -1.0, sine[:, 0, :], ALU.mult, ALU.mult)
                v.tensor_tensor(e2[:, j, 0, :], grow[:, 1, :], cosine[:, 1, :], ALU.mult)
                v.scalar_tensor_tensor(e2[:, j, 1, :], grow[:, 1, :], -1.0, sine[:, 1, :], ALU.mult, ALU.mult).then_inc(waves, 1)

            def add(t, j, images):
                if images[0] == 0:
                    dve.wait_ge(loaded[j], 16 * IMAGES * (t + 1))
                    wait_past(dve, stored[j], 16 * IMAGES * t)
                for a in images:
                    dve.wait_ge(o_ready, IMAGES * (2 * t + j) + a + 1)
                    v.scalar_tensor_tensor(xout[:, j, a, :], o_ps[:, a % 2, :], 1.0 / (SUB * SUB), xin[:, j, a, :],
                                           ALU.mult, ALU.add).then_inc(summed, 1)
                    v.drain()
                    v.bn_stats(part[:, 6 * a:6 * a + 6], xout[:, j, a, :])
                if images[-1] == IMAGES - 1:
                    v.drain()
                    v.tensor_copy(stats[:, 2 * t + j, :], part[:])
                    v.drain()
            stages = []
            for j in range(2):
                lag, other = 1 - j, 1 - j
                stages += [(1, lambda t, j=j: add(t, j, range(0, PREPARED))), (lag, lambda t, j=other: prepare(t, j)),
                           (1, lambda t, j=j: add(t, j, range(PREPARED, COMBINED))), (lag, lambda t, j=other: combine(t, j)),
                           (1, lambda t, j=j: add(t, j, range(COMBINED, IMAGES)))]
            pipeline(dve, PAIRS, stages)

        @block.tensor
        def _(pe):
            m = nc.tensor

            def contract(t, j):
                i = 2 * t + j
                pe.wait_ge(waves, i + 1)

                def modes(a):
                    n = IMAGES * i + a
                    wait_past(pe, t_kept, n - 1)
                    m.matmul(t_ps[:, a % 2, :], coef[:, a, 0, :], e1[:, j, 1:3].rearrange("p z n -> p (z n)"),
                             start=True, stop=False)
                    m.matmul(t_ps[:, a % 2, :], coef[:, a, 1, :], e1[:, j, 0:2].rearrange("p z n -> p (z n)"),
                             start=False, stop=True).then_inc(t_ready, 1)

                def image(a):
                    n = IMAGES * i + a
                    pe.wait_ge(t_kept, n + 1)
                    wait_past(pe, summed, n - 1)
                    for s in range(2):
                        dst = o_ps[:, a % 2, COLS * s:COLS * s + COLS]
                        m.matmul(dst, tmp[:, a % 2, 0, s::2], e2[:, j, 0, :], start=True, stop=False)
                        last = m.matmul(dst, tmp[:, a % 2, 1, s::2], e2[:, j, 1, :], start=False, stop=True)
                    last.then_inc(o_ready, 1)
                modes(0)
                for a in range(IMAGES):
                    if a + 1 < IMAGES:
                        modes(a + 1)
                    image(a)
            pipeline(pe, PAIRS, [(1, lambda t: contract(t, 0)), (1, lambda t: contract(t, 1))])


def norm_vectors_by_image(net, stats, scale, bias):
    nc, c = net.nc, net.c
    N = CH * IMAGES
    GROUPS = CH // 2
    with ExitStack() as local:
        mean, var, d, e, g, y, t = (net.sb(local, k, [P, CH, IMAGES]) for k in ("mean", "var", "d", "e", "g", "y", "t"))
        ones = net.sb(local, "ones", [P, P])
        pick = net.sb(local, "pick", [P, P])
        pm = net.ps(local, "pm", [P, 2, BANK])
        s_mean, s_gm, s_e, s_gv = (net.sem(local, k) for k in ("mean", "gmean", "spread", "gvar"))
        block = local.enter_context(nc.Block())
        flat = lambda a: a[:].rearrange("p i a -> p (i a)")

        @block.tensor
        def _(pe):
            pe.wait_ge(s_mean, 1)
            nc.tensor.matmul(pm[:, 0, 0:N], ones[:], flat(mean), start=True, stop=True).then_inc(s_gm, 1)
            pe.wait_ge(s_e, 1)
            nc.tensor.matmul(pm[:, 1, 0:N], ones[:], flat(e), start=True, stop=True).then_inc(s_gv, 1)

        @block.vector
        def _(dve):
            v = nc.vector
            six = stats.rearrange("p i (a s) -> p i a s", s=6)

            def over_pairs(dst, src):
                s4 = src.rearrange("p (g two a) -> p g two a", two=2, a=IMAGES)
                d4 = dst[:].rearrange("p (g two) a -> p g two a", two=2)
                v.tensor_copy(flat(t), src)
                v.drain()
                t4 = t[:].rearrange("p (g two) a -> p g two a", two=2)
                for k in range(2):
                    v.tensor_tensor(d4[:, :, k, :], t4[:, :, 0, :], t4[:, :, 1, :], ALU.add)
                v.drain()
            v.memset(ones[:], 0.5 / P)
            v.tensor_tensor(mean[:], six[:, :, :, 1], six[:, :, :, 4], ALU.add)
            v.tensor_tensor(d[:], six[:, :, :, 1], six[:, :, :, 4], ALU.subtract)
            v.tensor_tensor(var[:], six[:, :, :, 2], six[:, :, :, 5], ALU.add)
            v.drain()
            v.tensor_scalar(mean[:], mean[:], 0.5, None, ALU.mult).then_inc(s_mean, 1)
            v.tensor_tensor(d[:], d[:], d[:], ALU.mult)
            v.drain()
            v.tensor_scalar(d[:], d[:], 0.25, None, ALU.mult)
            v.drain()
            v.scalar_tensor_tensor(var[:], var[:], 1.0 / BANK, d[:], ALU.mult, ALU.add)
            dve.wait_ge(s_gm, 1)
            over_pairs(g, pm[:, 0, 0:N])
            v.tensor_tensor(e[:], mean[:], g[:], ALU.subtract)
            v.drain()
            v.tensor_tensor(e[:], e[:], e[:], ALU.mult)
            v.drain()
            v.tensor_tensor(e[:], e[:], var[:], ALU.add).then_inc(s_e, 1)
            dve.wait_ge(s_gv, 1)
            over_pairs(d, pm[:, 1, 0:N])
            v.tensor_scalar(d[:], d[:], 1e-5, None, ALU.add)
            v.drain()
            rsqrt_steps(v, flat(y), flat(d), flat(t))
            v.scalar_tensor_tensor(g[:], g[:], -1.0, y[:], ALU.mult, ALU.mult)
            v.drain()
            for src, dst in ((y, scale), (g, bias)):
                for h in range(HALVES):
                    own = src[:, :, GROUP * h:GROUP * h + GROUP].rearrange("p i a -> p a i")
                    v.tensor_tensor(pick[:].rearrange("p (a i) -> p a i", a=GROUP), own,
                                    c["ident"][:].rearrange("p (a i) -> p a i", a=GROUP), ALU.mult)
                    v.drain()
                    v.reduce_sum(dst[:, h:h + 1], pick[:], axis=mybir.AxisListType.X)
                    v.drain()


def kan_constants(net, ctx):
    ins = net.ins
    k = {n: net.sb(ctx, n, list(ins[n].shape)) for n in ("kan_vec", "kan_basis", "kan_silu", "c_grid", "c_kan_ones",
                                                        "c_center")}
    k["sel8"] = net.sb(ctx, "sel8", [P, BLOCKS, P], F32R)
    k["pn_center"] = net.sb(ctx, "pn_center", [P, HALVES, P])
    k["pn_shift"] = net.sb(ctx, "pn_shift", [P, HALVES])
    k["grown"] = net.sb(ctx, "grown", [P, HALVES, P])
    k["end_b"] = net.sb(ctx, "end_b", [P, HALVES])
    return k


def prepare_kan(net, k, scale, bias):
    nc, ins = net.nc, net.ins
    with ExitStack() as local:
        staged = net.sb(local, "staged", [P, BLOCKS, P])
        shift = net.ps(local, "shift", [P, HALVES])
        loaded, shifted = (net.sem(local, s) for s in ("loaded", "shifted"))
        names = [n for n in k if n in ins]
        block = local.enter_context(nc.Block())

        @block.sync
        def _(sp):
            for n in names:
                sp.dma_start(k[n][:], ins[n]).then_inc(loaded, 16)
            sp.dma_start(staged[:], ins["c_sel8"]).then_inc(loaded, 16)
            sp.wait_ge(loaded, 16 * len(names) + 16)

        @block.tensor
        def _(pe):
            pe.wait_ge(loaded, 16 * len(names) + 16)
            nc.tensor.matmul(shift[:], k["c_center"][:, 0, :], bias, start=True, stop=True).then_inc(shifted, 1)

        @block.vector
        def _(dve):
            v = nc.vector
            vec = k["kan_vec"]
            dve.wait_ge(loaded, 16 * len(names) + 16)
            v.tensor_copy(k["sel8"][:], staged[:])
            v.tensor_scalar(k["end_b"][:], scale, 1.0, None, ALU.add)
            v.drain()
            for h in range(HALVES):
                v.tensor_scalar(k["pn_center"][:, h, :], k["c_center"][:, 0, :], scale[:, h:h + 1], None, ALU.mult)
                v.tensor_scalar(k["grown"][:, h, :], net.c["ident"][:], k["end_b"][:, h:h + 1], None, ALU.mult)
            v.drain()
            v.tensor_scalar(k["end_b"][:], bias, vec[:, 13:14], None, ALU.add)
            for n in range(4):
                v.tensor_scalar(vec[:, 2 + 3 * n:4 + 3 * n], vec[:, 2 + 3 * n:4 + 3 * n], 1.75, None, ALU.mult)
            v.tensor_scalar(k["kan_silu"][:], k["kan_silu"][:], 0.5, None, ALU.mult)
            dve.wait_ge(shifted, 1)
            v.tensor_copy(k["pn_shift"][:], shift[:])
            v.drain()


PN, K1, K2, K3, K4 = range(5)
KANS = (K1, K2, K3, K4)

UNITS = 32
SLOT = {K1: -24, K2: -16, K3: 0, K4: 24}
PREP = {"center0": (-60, -42, -35, -17, 10),
        "center1": (-58, -38, -30, -14, 13),
        "evac0": (-59, -41, -32, -14, 13),
        "evac1": (-56, -37, -28, -13, 15),
        "square0": (-56, -37, -31, -14, 14),
        "square1": (-54, -35, -28, -13, 16),
        "var0": (-56, -39, -30, -14, 14),
        "var1": (-54, -36, -28, -10, 15),
        "chain": (-50, -32, -25, -7, 18),
        "spread0": (-50, -31, -24, -8, 19),
        "spread1": (-48, -29, -23, -7, 20),
        "scale0": (-47, -28, -21, -5, 21),
        "scale1": (-46, -26, -20, -4, 22),
        "shift0": (-47, -30, -21, -3, 21),
        "shift1": (-45, -26, -18, 0, 24)}
SILU = {"tanh": {PN: -44, K4: 11}, "silu": {PN: -40, K4: 14}}
LOAD_X, LOAD_R, STORE, MEASURE = -64, 8, 34, 37
FEED_K1, FEED_U1, FEED_K2, FEED_U2, BACK_K1, BACK_K2 = -46, -44, -38, -22, -16, -11
TURN, TURN_U, HALF, TOTAL = -36, -30, -5, 10
REPEAT = 3
EVACUATE = 1
ACT_UNITS = (2, 6)


class Order:

    def __init__(self, positions, tiles):
        self.period = len(positions)
        items = sorted(((UNITS * t + p, kind, t) for kind, p in positions.items() for t in range(tiles)))
        self.index = {(kind, t): n for n, (_, kind, t) in enumerate(items)}
        self.offset = {kind: self.index[kind, tiles // 2] - self.period * (tiles // 2) for kind in positions}

    def __call__(self, kind, t):
        return self.index[kind, t] if isinstance(t, int) else t * self.period + self.offset[kind]


def window_layer(net, k, source, bias, target, stats):
    nc, c = net.nc, net.c
    TILES = BANDS * HALVES
    CHUNKS = TILE // BANK
    RING = 4
    G = 2 * GROUP
    ON_DVE = [n for n in range(2 * CHUNKS) if n not in ACT_UNITS]
    prep_no = Order({kind: PREP["center0"][kind] for kind in (PN,) + KANS}, TILES)
    slot_no = Order(SLOT, TILES)
    silu_no = Order(SILU["silu"], TILES)
    with ExitStack() as local:
        def sb(name, shape, dt=F32):
            return net.sb(local, name, shape, dt)
        X, R, Z, W, D = (sb(n, [P, TILE]) for n in ("x", "x_to_x3", "z", "silu_z", "back_k2"))
        Y, U = sb("y", [P, 2, TILE]), sb("silu_y", [P, 2, TILE])
        kin, ku = sb("kin", [P, 2, TILE]), sb("ku", [P, 2, TILE])
        turned_y = sb("columns_first", [P, TILE])
        back = {K1: turned_y[:], K2: D[:]}
        sq = sb("sq", [P, TILE])
        srep = sb("srep", [P, CHUNKS, GROUP, BANK])
        ex = sb("ex", [P, RING, GROUP, BANK])
        y, t_ = sb("rstd", [P, P]), sb("t", [P, P])
        hilo = sb("hilo", [P, 2, P])
        part = sb("part", [P, CHUNKS * 6])
        one = sb("one", [P, 1])
        cen, spread, out = (net.ps(local, n, [P, 2, BANK]) for n in ("cen", "spread", "out"))
        var = net.ps(local, "var", [P, P])
        (centered, moved, squared, var_ready, factors, spread_ready, scaled, normed, args, own_args, exps,
         used, evacuated, tanh_ready, u_ready, copied_y, copied_u, halved, summed, measured, x_loaded, r_loaded, stored) = (
            net.sem(local, n) for n in (
                "centered", "moved", "squared", "var_ready", "factors", "spread_ready", "scaled",
                "normed", "args", "own_args", "exps", "used", "evacuated", "tanh_ready", "u_ready", "copied_y", "copied_u",
                "halved", "summed", "measured", "x_loaded", "r_loaded", "stored"))
        kin_loaded = {kind: net.sem(local, f"kin_loaded{kind}") for kind in (K1, K2)}
        ku_loaded = {kind: net.sem(local, f"ku_loaded{kind}") for kind in (K1, K2)}
        back_loaded = {kind: net.sem(local, f"back_loaded{kind}") for kind in (K1, K2)}
        rep_loaded = [net.sem(local, f"rep_loaded{n}") for n in range(CHUNKS)]
        block = local.enter_context(nc.Block())

        def norm_in(kind, h):
            return {PN: X[:], K1: kin[:, 0], K2: kin[:, 1], K3: Y[:, h], K4: Z[:]}[kind]

        def norm_out(kind, h):
            return Y[:, h] if kind == PN else norm_in(kind, h)

        def silu_of(kind, h):
            return {K1: ku[:, 0], K2: ku[:, 1], K3: U[:, h], K4: W[:]}[kind]

        vec = k["kan_vec"]
        ln_g = {PN: vec[:, 0:1], **{n: vec[:, 3 * n - 1:3 * n] for n in KANS}}
        ln_b = {PN: vec[:, 1:2], **{n: vec[:, 3 * n:3 * n + 1] for n in KANS}}

        def out_b(kind, h):
            return k["end_b"][:, h:h + 1] if kind == K4 else vec[:, 3 * kind + 1:3 * kind + 2]

        def cols(n):
            return slice(BANK * n, BANK * n + BANK)

        def after(t, first=1):
            return not isinstance(t, int) or t >= first

        def band(t, h):
            return t // 2 if isinstance(t, int) else (t - h) // 2

        class Round:

            def __init__(self, number, parity):
                self.number, self.parity = number, parity

            def due(self, unit, position):
                if (unit - position) % UNITS:
                    return None, 0
                ahead = (unit - position) // UNITS
                t = self.number + ahead
                if isinstance(t, int) and not 0 <= t < TILES:
                    return None, 0
                return t, (self.parity + ahead) % 2

            def slot(self, unit):
                for kind in KANS:
                    t, h = self.due(unit - (unit - SLOT[kind]) % UNITS, SLOT[kind])
                    if (unit - SLOT[kind]) % UNITS < 2 * CHUNKS and t is not None:
                        return kind, (unit - SLOT[kind]) % UNITS, t, h
                return None, 0, None, 0

        def rounds(eng, round_):
            for n in range(-2, 4):
                round_(Round(n, n % 2))
            with eng.Fori(2, BANDS - 1) as r:
                for h in range(HALVES):
                    round_(Round(r * 2 + h, h))
            for n in range(TILES - 2, TILES + 2):
                round_(Round(n, n % 2))

        @block.sync
        def _(sp):
            def regroup(dst, src, sem, backwards=False):
                for i in range(2 * GROUP):
                    wide = (dst if backwards else src)[QUAD // 2 * i:QUAD // 2 * i + QUAD // 2]
                    wide = wide.rearrange("p (z n) -> p z n", z=BAND)
                    deep = (src if backwards else dst)[:, COLS * i:COLS * i + COLS]
                    sp.dma_start(wide if backwards else deep, deep if backwards else wide).then_inc(sem, 16)

            def load_x(t, h):
                tile_ = source[band(t, h), h]
                if after(t):
                    sp.wait_ge(scaled, CHUNKS * prep_no(PN, t - 1) + CHUNKS)
                sp.dma_start(X[:], tile_).then_inc(x_loaded, 16)

            def load_r(t, h):
                tile_ = source[band(t, h), h]
                wait_both(sp, stored, 16 * t, measured, t)
                sp.dma_start(R[:], tile_).then_inc(r_loaded, 16)

            def store(t, h):
                tile_ = target[band(t, h), h]
                sp.wait_ge(evacuated, CHUNKS * slot_no(K4, t) + CHUNKS)
                sp.dma_start(tile_, R[:]).then_inc(stored, 16)

            def feed_k1(t, h):
                sp.wait_ge(normed, 2 * prep_no(PN, t) + 2)
                regroup(kin[:, 0], Y[:, h], kin_loaded[K1])

            def feed_u1(t, h):
                wait_both(sp, back_loaded[K1], 128 * t, u_ready, silu_no(PN, t) + 1)
                regroup(ku[:, 0], U[:, h], ku_loaded[K1])

            def feed_k2(t, h):
                sp.wait_ge(copied_y, t + 1)
                regroup(kin[:, 1], turned_y[:], kin_loaded[K2])

            def feed_u2(t, h):
                wait_both(sp, copied_u, t + 1, back_loaded[K2], 128 * t)
                regroup(ku[:, 1], turned_y[:], ku_loaded[K2])

            def give_back(kind, t):
                complete = CHUNKS * slot_no(kind, t) + CHUNKS
                if kind == K2:
                    wait_both(sp, summed, t, evacuated, complete)
                else:
                    wait_both(sp, ku_loaded[K2], 128 * t + 128, evacuated, complete)
                regroup(back[kind], ku[:, kind - K1], back_loaded[kind], True)

            def repeat(kind, t, h, n):
                b = slot_no(kind, t)
                s = norm_out(kind, h)
                wait_both(sp, exps, 8 * b + (2 * n + 2 - 8), normed, 2 * prep_no(kind, t) + 2 if n == 0 else 0)
                for g in range(GROUP):
                    src = s[QUAD * g:QUAD * g + QUAD, cols(n)].unsqueeze(1).to_broadcast([QUAD, GROUP, BANK])
                    sp.dma_start(srep[:, n, g, :], src).then_inc(rep_loaded[n], 16)

            def round_(now):
                for u in range(UNITS):
                    for kind in KANS:
                        for n in range(CHUNKS):
                            t, h = now.due(u, SLOT[kind] - 2 * CHUNKS + 2 * n + REPEAT)
                            if t is not None:
                                repeat(kind, t, h, n)
                    for position, step in ((STORE, store), (LOAD_R, load_r), (LOAD_X, load_x), (FEED_K1, feed_k1), (FEED_U1, feed_u1),
                                           (FEED_K2, feed_k2), (FEED_U2, feed_u2)):
                        t, h = now.due(u, position)
                        if t is not None:
                            step(t, h)
                    for kind, position in ((K1, BACK_K1), (K2, BACK_K2)):
                        t, h = now.due(u, position)
                        if t is not None:
                            give_back(kind, t)
            rounds(sp, round_)
            sp.wait_ge(stored, 16 * TILES)

        @block.scalar
        def _(act):
            a = nc.scalar

            def evacuate_centred(kind, t, h, half):
                no = prep_no(kind, t)
                dst = norm_in(kind, h)
                shift = k["pn_shift"][:, h:h + 1] if kind == PN else 0.0
                if half == 0:
                    if kind in (K3, K4):
                        act.wait_ge(u_ready, silu_no(PN if kind == K3 else K4, t) + 1)
                for n in (2 * half, 2 * half + 1):
                    act.wait_ge(centered, CHUNKS * no + n + 1)
                    a.activation(dst[:, cols(n)], cen[:, n % 2, :], ACT.Identity, bias=shift).then_inc(moved, 1)

            def tanh(kind, t, h):
                if kind == PN:
                    wait_past(act, summed, t - 1)
                    act.wait_ge(normed, 2 * prep_no(PN, t) + 2)
                    a.activation(U[:, h], Y[:, h], ACT.Tanh, scale=0.5).then_inc(tanh_ready, 1)
                else:
                    act.wait_ge(summed, t + 1)
                    a.activation(W[:], Z[:], ACT.Tanh, scale=0.5).then_inc(tanh_ready, 1)

            def exponential(kind, n, t, h):
                unit = 2 * CHUNKS * slot_no(kind, t) + n
                e = ex[:, n % RING].rearrange("p g n -> p (g n)")
                j = n % 2
                if n in ACT_UNITS:
                    b = slot_no(kind, t)
                    act.wait_ge(rep_loaded[n // 2], 64 * b + 64)
                    wait_past(act, used, 2 * CHUNKS * b + (n - RING + 1))
                    a.activation(e, srep[:, n // 2].rearrange("p g n -> p (g n)"), ACT.Square,
                                 bias=k["c_grid"][:, j, 2:3]).then_inc(own_args, 1)
                    act.wait_ge(own_args, len(ACT_UNITS) * b + (ACT_UNITS.index(n) + 1))
                    a.activation(e, e, ACT.Exp, scale=-1.0).then_inc(exps, 1)
                else:
                    act.wait_ge(args, len(ON_DVE) * slot_no(kind, t) + (ON_DVE.index(n) + 1))
                    a.activation(e, e, ACT.Exp, bias=k["c_grid"][:, j, 1:2], scale=-1.0).then_inc(exps, 1)

            def evacuate(kind, t, h, n):
                b = slot_no(kind, t)
                dst = R[:] if kind == K4 else silu_of(kind, h)
                act.wait_ge(used, 2 * CHUNKS * b + (2 * n + 2))
                a.activation(dst[:, cols(n)], out[:, n % 2, :], ACT.Identity, bias=out_b(kind, h)).then_inc(evacuated, 1)

            def round_(now):
                for u in range(UNITS):
                    for kind in SILU["tanh"]:
                        t, h = now.due(u, SILU["tanh"][kind])
                        if t is not None:
                            tanh(kind, t, h)
                    for kind in (PN,) + KANS:
                        for half in range(2):
                            t, h = now.due(u, PREP[f"evac{half}"][kind])
                            if t is not None:
                                evacuate_centred(kind, t, h, half)
                    kind, n, t, h = now.slot(u)
                    if t is not None:
                        exponential(kind, n, t, h)
                    for kind in KANS:
                        for n in range(CHUNKS):
                            t, h = now.due(u, SLOT[kind] + 2 * n + 1 + EVACUATE)
                            if t is not None:
                                evacuate(kind, t, h, n)
            rounds(act, round_)

        @block.vector
        def _(dve):
            v = nc.vector
            def chain(kind, t, h):
                no = prep_no(kind, t)
                wait_past(dve, spread_ready, CHUNKS * no)
                dve.wait_ge(var_ready, no + 1)
                v.tensor_scalar(var[:], var[:], 1.0 * G / P if kind in (K1, K2) else 0.5 * G / P, EPS_LN, ALU.mult, ALU.add)
                v.drain()
                rsqrt_steps(v, y[:], var[:], t_[:])
                split_hi_lo(v, hilo[:, 0, :], hilo[:, 1, :], y[:]).then_inc(factors, 1)

            def scale(kind, t, h, half):
                no = prep_no(kind, t)
                src, dst = norm_in(kind, h), norm_out(kind, h)
                for n in (2 * half, 2 * half + 1):
                    dve.wait_ge(spread_ready, CHUNKS * no + n + 1)
                    v.scalar_tensor_tensor(dst[:, cols(n)], src[:, cols(n)], ln_g[kind], spread[:, n % 2, :],
                                           ALU.mult, ALU.mult).then_inc(scaled, 1)

            def silu(kind, t, h):
                dve.wait_ge(tanh_ready, silu_no(kind, t) + 1)
                x_, u_ = (Y[:, h], U[:, h]) if kind == PN else (Z[:], W[:])
                v.scalar_tensor_tensor(u_, u_, 1.0, x_, ALU.add, ALU.mult).then_inc(u_ready, 1)

            def measure(t, h):
                dve.wait_ge(evacuated, CHUNKS * slot_no(K4, t) + CHUNKS)
                for n in range(CHUNKS):
                    last = v.bn_stats(part[:, 6 * n:6 * n + 6], R[:, cols(n)])
                last.then_inc(measured, 1)
                v.drain()
                v.tensor_copy(stats[:, h, band(t, h), :], part[:])
                v.drain()

            def distances(kind, n, t, h):
                b = slot_no(kind, t)
                dve.wait_ge(rep_loaded[n // 2], 64 * b + 64)
                wait_past(dve, used, 2 * CHUNKS * b + (n - RING + 1))
                s = srep[:, n // 2].rearrange("p g n -> p (g n)")
                v.scalar_tensor_tensor(ex[:, n % RING].rearrange("p g n -> p (g n)"), s, k["c_grid"][:, n % 2, 0:1], s,
                                       ALU.add, ALU.mult).then_inc(args, 1)

            def round_(now):
                for u in range(UNITS):
                    for kind in SILU["silu"]:
                        t, h = now.due(u, SILU["silu"][kind])
                        if t is not None:
                            silu(kind, t, h)
                    for kind in (PN,) + KANS:
                        t, h = now.due(u, PREP["chain"][kind])
                        if t is not None:
                            chain(kind, t, h)
                        for half in range(2):
                            t, h = now.due(u, PREP[f"scale{half}"][kind])
                            if t is not None:
                                scale(kind, t, h, half)
                    t, h = now.due(u, MEASURE)
                    if t is not None:
                        measure(t, h)
                    kind, n, t, h = now.slot(u)
                    if t is not None and n in ON_DVE:
                        distances(kind, n, t, h)
            rounds(dve, round_)

        @block.tensor
        def _(pe):
            m = nc.tensor

            def center(kind, t, h, half):
                no = prep_no(kind, t)
                src = norm_in(kind, h)
                if half == 0:
                    if kind == PN:
                        pe.wait_ge(x_loaded, 16 * t + 16)
                    elif kind in (K1, K2):
                        pe.wait_ge(kin_loaded[kind], 128 * t + 128)
                    elif kind == K4:
                        pe.wait_ge(summed, t + 1)
                weights = k["pn_center"][:, h, :] if kind == PN else k["c_center"][:, 1 if kind in (K1, K2) else 0, :]
                for n in (2 * half, 2 * half + 1):
                    wait_past(pe, moved, CHUNKS * no + (n - 1))
                    m.matmul(cen[:, n % 2, :], weights, src[:, cols(n)], start=True, stop=True).then_inc(centered, 1)

            def variance(kind, t, h, half):
                no = prep_no(kind, t)
                if half == 0:
                    wait_past(pe, factors, no)
                pe.wait_ge(squared, 2 * no + half + 1)
                for i in range(GROUP):
                    for quarter in (2 * half, 2 * half + 1):
                        block_ = P * (GROUP * quarter + i)
                        last = m.matmul(var[QUAD * quarter:QUAD * quarter + QUAD, :],
                                        k["c_kan_ones"][:, 0 if kind in (K1, K2) else 1, i, :], sq[:, block_:block_ + P],
                                        start=(i == 0), stop=(i == GROUP - 1), tile_position=(0, QUAD * quarter))
                if half:
                    last.then_inc(var_ready, 1)

            def spread_out(kind, t, h, half):
                no = prep_no(kind, t)
                pe.wait_ge(factors, no + 1)
                for n in (2 * half, 2 * half + 1):
                    wait_past(pe, scaled, CHUNKS * no + (n - 1))
                    for i in range(GROUP):
                        for z in range(2):
                            last = m.matmul(spread[:, n % 2, P * i:P * i + P], k["sel8"][:, GROUP * n + i, :],
                                            hilo[:, z, :].bitcast(F32R), start=(z == 0), stop=(z == 1))
                    last.then_inc(spread_ready, 1)

            def products(kind, n, t, h):
                b = slot_no(kind, t)
                bank = out[:, n // 2 % 2, :]
                if n == 0:
                    if kind in (K1, K2):
                        pe.wait_ge(ku_loaded[kind], 128 * t + 128)
                    else:
                        pe.wait_ge(u_ready, silu_no(PN if kind == K3 else K4, t) + 1)
                    if kind == K4:
                        pe.wait_ge(r_loaded, 16 * t + 16)
                if n % 2 == 0:
                    wait_past(pe, evacuated, CHUNKS * b + (n // 2 - 1))
                    m.matmul(bank, k["kan_silu"][:, kind - 1, :], silu_of(kind, h)[:, cols(n // 2)], start=True, stop=False)
                    if kind == K4:
                        m.matmul(bank, k["grown"][:, h, :], R[:, cols(n // 2)], start=False, stop=False)
                pe.wait_ge(exps, 2 * CHUNKS * b + (n + 1))
                for g in range(GROUP):
                    last = m.matmul(out[QUAD * g:QUAD * g + QUAD, n // 2 % 2, :], k["kan_basis"][:, kind - 1, n % 2, :],
                                    ex[:, n % RING, g, :], start=False, stop=(n % 2 == 1), tile_position=(0, QUAD * g))
                last.then_inc(used, 1)

            def round_(now):
                for u in range(UNITS):
                    for kind in (PN,) + KANS:
                        for half in range(2):
                            t, h = now.due(u, PREP[f"center{half}"][kind])
                            if t is not None:
                                center(kind, t, h, half)
                        for half in range(2):
                            t, h = now.due(u, PREP[f"var{half}"][kind])
                            if t is not None:
                                variance(kind, t, h, half)
                        for half in range(2):
                            t, h = now.due(u, PREP[f"spread{half}"][kind])
                            if t is not None:
                                spread_out(kind, t, h, half)
                    kind, n, t, h = now.slot(u)
                    if t is not None:
                        products(kind, n, t, h)
            rounds(pe, round_)

        @block.gpsimd
        def _(pool):
            g = nc.gpsimd

            columns_first = turned_y[:].rearrange("p (x rw) -> p x rw", x=BAND)
            ones = one[:].unsqueeze(1).to_broadcast([P, BAND, BAND * QUAD])

            def rows_first(tile_):
                return tile_.rearrange("p (rw x) -> p x rw", x=BAND)

            def turn_y(t, h):
                pool.wait_ge(normed, 2 * prep_no(PN, t) + 2)
                wait_past(pool, halved, t)
                g.tensor_tensor(columns_first, rows_first(Y[:, h]), ones, ALU.mult).then_inc(copied_y, 1)

            def turn_u(t, h):
                pool.wait_ge(u_ready, silu_no(PN, t) + 1)
                pool.wait_ge(kin_loaded[K2], 128 * t + 128)
                g.tensor_tensor(columns_first, rows_first(U[:, h]), ones, ALU.mult).then_inc(copied_u, 1)

            d = D[:].rearrange("p (x rw) -> p rw x", x=BAND)

            def by_columns(tile_):
                return tile_.rearrange("p (rw x) -> p rw x", x=BAND)

            def half(t, h):
                pool.wait_ge(back_loaded[K1], 128 * t + 128)
                pool.wait_ge(back_loaded[K2], 128 * t + 128)
                g.tensor_tensor(d, d, by_columns(back[K1]), ALU.add).then_inc(halved, 1)

            def total(t, h):
                if after(t):
                    pool.wait_ge(exps, 8 * slot_no(K4, t - 1) + 8)
                pool.wait_ge(evacuated, CHUNKS * slot_no(K3, t) + CHUNKS)
                pool.wait_ge(halved, t + 1)
                g.tensor_tensor(by_columns(Z[:]), by_columns(U[:, h]), d, ALU.add).then_inc(summed, 1)

            def halves(half):
                return slice(2 * BANK * half, 2 * BANK * half + 2 * BANK)

            def square(kind, t, h, half):
                no = prep_no(kind, t)
                src = norm_in(kind, h)[:, halves(half)]
                wait_past(pool, var_ready, no)
                pool.wait_ge(moved, CHUNKS * no + 2 * half + 2)
                g.tensor_tensor(sq[:, halves(half)], src, src, ALU.mult).then_inc(squared, 1)

            def shift(kind, t, h, half):
                no = prep_no(kind, t)
                dst = norm_out(kind, h)[:, halves(half)]
                pool.wait_ge(scaled, CHUNKS * no + 2 * half + 2)
                g.tensor_tensor(dst, dst, ln_b[kind].to_broadcast([P, 2 * BANK]), ALU.add).then_inc(normed, 1)

            def round_(now):
                for u in range(UNITS):
                    for kind in (PN,) + KANS:
                        for part_ in range(2):
                            t, h = now.due(u, PREP[f"shift{part_}"][kind])
                            if t is not None:
                                shift(kind, t, h, part_)
                        for part_ in range(2):
                            t, h = now.due(u, PREP[f"square{part_}"][kind])
                            if t is not None:
                                square(kind, t, h, part_)
                    for position, step in ((TOTAL, total), (TURN, turn_y), (TURN_U, turn_u), (HALF, half)):
                        t, h = now.due(u, position)
                        if t is not None:
                            step(t, h)
            g.memset(one[:], 1.0)
            g.drain()
            rounds(pool, round_)


PATTERN = {(1, 1): (128, 1), (1, 0): (64, 2), (1, -1): (32, 4), (0, 1): (16, 8)}


def pattern_layer(net, source, scale, bias, out):
    nc, c = net.nc, net.c
    WEIGHT = 0.5 / 255
    ON_PE, ON_DVE = [(1, 1), (1, 0)], [(1, -1), (0, 1)]
    DIRS = ON_PE + ON_DVE
    TILES = BANDS * HALVES
    CHUNKS = TILE // BANK
    with ExitStack() as local:
        xt = net.sb(local, "xt", [P, 2, HALVES, HALO, COLS])
        z = net.sb(local, "z", [P, HALVES, HALO, PAD])
        d = net.sb(local, "d", [P, HALVES, len(DIRS), BAND + 1, PAD])
        ot = net.sb(local, "ot", [P, HALVES, BAND, COLS])
        weights = net.sb(local, "weights", [P, 2 * len(ON_PE), P])
        acc = net.ps(local, "acc", [P, HALVES, CHUNKS, BANK])
        padded, weighted, z_ready, diff_dve, diff_pool, tanh_ready, acc_ready, x_used, added, out_ready = (
            net.sem(local, n) for n in ("padded", "weighted", "z_ready", "diff_dve", "diff_pool", "tanh_ready", "acc_ready",
                                        "x_used", "added", "out_ready"))
        loaded = [[net.sem(local, f"loaded{parity}{h}") for h in range(HALVES)] for parity in range(2)]
        stored = [net.sem(local, f"stored{h}") for h in range(HALVES)]
        block = local.enter_context(nc.Block())
        bands = out.rearrange("b c r w -> (b c) (r w)").rearrange("p (t n) -> p t n", n=TILE)

        def region(dr, dc):
            return slice(1 - dr, BAND + 1), slice(0 if dc > 0 else 1, PAD if dc < 0 else PAD - 1)

        def difference(engine, h, direction):
            (dr, dc), n = direction, DIRS.index(direction)
            rows, columns = region(dr, dc)
            there = z[:, h, rows.start + dr:rows.stop + dr, columns.start + dc:columns.stop + dc]
            return engine.tensor_tensor(d[:, h, n, rows, columns], there, z[:, h, rows, columns], ALU.subtract)

        def term(h, direction, opposite, rows):
            (dr, dc), n = direction, DIRS.index(direction)
            back = (dr, dc) if opposite else (0, 0)
            return d[:, h, n, rows.start + 1 - back[0]:rows.stop + 1 - back[0], 1 - back[1]:1 - back[1] + COLS]

        def factor(direction, opposite):
            return (-WEIGHT if opposite else WEIGHT) * PATTERN[direction][int(opposite)]

        @block.sync
        def _(sp):
            def load(r, parity):
                for h in range(HALVES):
                    wait_past(sp, x_used, 2 * (r - 2) + h + 1)
                    for rows, src in ((slice(1, BAND + 1), source[r, h]),
                                      (slice(0, 1), source[(r + BANDS - 1) % BANDS, h, :, TILE - COLS:]),
                                      (slice(HALO - 1, HALO), source[(r + 1) % BANDS, h, :, 0:COLS])):
                        sp.dma_start(xt[:, parity, h, rows, :].rearrange("p r w -> p (r w)"), src).then_inc(loaded[parity][h], 16)

            def store(r, _):
                for h in range(HALVES):
                    sp.wait_ge(out_ready, 2 * r + h + 1)
                    sp.dma_start(bands[P * h:P * h + P, r, :], ot[:, h].rearrange("p r w -> p (r w)")).then_inc(stored[h], 16)
            pipeline_by_two(sp, BANDS, [(0, load), (1, store)])
            for h in range(HALVES):
                sp.wait_ge(stored[h], 16 * BANDS)

        @block.scalar
        def _(act):
            a = nc.scalar
            act.wait_ge(padded, 1)

            def normalise(r, parity, h):
                i = 2 * r + h
                first, last = (isinstance(r, int) and r == e for e in (0, BANDS - 1))
                act.wait_ge(loaded[parity][h], 24 * (r - parity) + 48)
                wait_past(act, diff_dve, i - 1)
                wait_past(act, diff_pool, 2 * (i - 1))
                inner = slice(1 if first else 0, HALO - 1 if last else HALO)
                n = a.activation(z[:, h, inner, 1:COLS + 1], xt[:, parity, h, inner, :], ACT.Identity, bias=bias[:, h:h + 1],
                                 scale=scale[:, h:h + 1])
                if last:
                    n = a.activation(z[:, h, HALO - 1, 1:COLS + 1], xt[:, parity, h, HALO - 1, :], ACT.Copy, scale=0.0)
                n.then_inc(z_ready, 1)

            def tanh(r, h):
                i = 2 * r + h
                for n, (dr, dc) in enumerate(DIRS):
                    if n == 0:
                        act.wait_ge(diff_dve, i + 1)
                    if n in (1, 2):
                        act.wait_ge(diff_pool, 2 * i + n)
                    rows, columns = region(dr, dc)
                    t = d[:, h, n, rows, columns]
                    a.activation(t, t, ACT.Tanh, scale=5.0).then_inc(tanh_ready, 1)
            def band(r, parity):
                normalise(r, parity, 0)
                tanh(r - 1, 1)
                normalise(r, parity, 1)
                tanh(r, 0)
            normalise(0, 0, 0)
            normalise(0, 0, 1)
            tanh(0, 0)
            with act.Fori(0, BANDS // 2 - 1) as pair:
                band(pair * 2 + 1, 1)
                band(pair * 2 + 2, 0)
            band(BANDS - 1, 1)
            tanh(BANDS - 1, 1)

        @block.gpsimd
        def _(pool):
            g = nc.gpsimd

            def differences(r):
                for h in range(HALVES):
                    i = 2 * r + h
                    wait_past(pool, out_ready, i - 1)
                    pool.wait_ge(z_ready, i + 1)
                    difference(g, h, ON_PE[1]).then_inc(diff_pool, 1)
                    difference(g, h, ON_DVE[0])
                    difference(g, h, ON_DVE[1]).then_inc(diff_pool, 1)
            g.memset(z[:], 0.0).then_inc(padded, 1)
            pipeline(pool, BANDS, [(0, differences)])

        @block.vector
        def _(dve):
            v = nc.vector
            for n, (direction, opposite) in enumerate((p, o) for p in ON_PE for o in (False, True)):
                last = v.tensor_scalar(weights[:, n, :], c["ident"][:], factor(direction, opposite), None, ALU.mult)
            last.then_inc(weighted, 1)

            def differences(r, h):
                i = 2 * r + h
                wait_past(dve, acc_ready, CHUNKS * (i - 1))
                dve.wait_ge(z_ready, i + 1)
                difference(v, h, ON_PE[0]).then_inc(diff_dve, 1)

            def add(r, parity, h):
                i = 2 * r + h
                wait_past(dve, stored[h], 16 * r)
                into, before = ot[:, h], xt[:, parity, h, 1:BAND + 1, :]
                for n, (direction, opposite) in enumerate((p, o) for p in ON_DVE for o in (False, True)):
                    dve.wait_ge(tanh_ready, len(DIRS) * i + len(ON_PE) + n // 2 + 1)
                    if n == 1:
                        dve.wait_ge(x_used, i + 1)
                    if n > 1:
                        dve.wait_ge(added, 3 * i + n - 1)
                    v.scalar_tensor_tensor(into, term(h, direction, opposite, slice(0, BAND)), factor(direction, opposite),
                                           before, ALU.mult, ALU.add).then_inc(added if n else x_used, 1)
                    before = into
                dve.wait_ge(acc_ready, CHUNKS * i + CHUNKS)
                dve.wait_ge(added, 3 * i + 3)
                sums = acc[:, h].rearrange("p k (r w) -> p (k r) w", w=COLS)
                v.scalar_tensor_tensor(into, into, 0.5, sums, ALU.add, ALU.add).then_inc(out_ready, 1)
            def band(r, parity):
                differences(r, 0)
                add(r - 1, 1 - parity, 1)
                differences(r, 1)
                add(r, parity, 0)
            differences(0, 0)
            differences(0, 1)
            add(0, 0, 0)
            with dve.Fori(0, BANDS // 2 - 1) as pair:
                band(pair * 2 + 1, 1)
                band(pair * 2 + 2, 0)
            band(BANDS - 1, 1)
            add(BANDS - 1, 1, 1)

        @block.tensor
        def _(pe):
            m = nc.tensor
            pe.wait_ge(weighted, 1)

            def sums(r):
                for h in range(HALVES):
                    i = 2 * r + h
                    wait_past(pe, out_ready, i - 1)
                    for n, direction in enumerate(ON_PE):
                        pe.wait_ge(tanh_ready, len(DIRS) * i + n + 1)
                        for k in range(CHUNKS):
                            for o in (0, 1):
                                last = m.matmul(acc[:, h, k, :], weights[:, 2 * n + o, :],
                                                term(h, direction, bool(o), slice(2 * k, 2 * k + 2)),
                                                start=(n + o == 0), stop=(n + o == 2))
                            if n:
                                last.then_inc(acc_ready, 1)
            pipeline(pe, BANDS, [(0, sums)])


def build_program(nc, ins, out):
    with ExitStack() as ctx:
        net = Net(nc, ctx, ins)
        load_constants(net, ctx, ["c_ident"])
        x_rows = ins["x"].rearrange("b c r w -> (b c) (r w)")
        t1, t2, x1, x2, x3 = (net.scratch(k) for k in ("t1", "t2", "x1", "x2", "x3"))
        SW = BANDS * TILE // BANK * 6
        stats = net.sb(ctx, "stats", [P, HALVES, SW])
        by_band = stats[:].rearrange("p h (r n) -> p h r n", r=BANDS)
        merged = stats[:].rearrange("p h n -> p (h n)").rearrange("p (o n) -> p o n", o=1)
        scale, bias = net.sb(ctx, "scale", [P, HALVES]), net.sb(ctx, "bias", [P, HALVES])
        with ExitStack() as local:
            load_constants(net, local, ["c_ones", "c_sel", "bn"])
            bn = net.c["bn"]
            input_stats(net, x_rows, stats[:])
            norm_vectors(net, stats[:], "pair", 1e-5, scale[:], bias[:])
            conv_layer(net, x_rows, scale, bias, ins["w1"], ins["b1"], t1, by_band, True)
            norm_vectors(net, merged, "channel", 1e-5, scale[:, 0:1], bias[:, 0:1], bn[:, 0:1], bn[:, 1:2])
            conv_layer(net, t1, scale[:, 0:1], bias[:, 0:1], ins["w2"], ins["b2"], t2, by_band, False)
            norm_vectors(net, merged, "channel", 1e-5, scale[:, 0:1], bias[:, 0:1], bn[:, 2:3], bn[:, 3:4])
            residual_layer(net, x_rows, t2, scale[:, 0:1], bias[:, 0:1], x1, by_band)
        norm_vectors(net, stats[:], "pair", 1e-5, scale[:], bias[:])
        with ExitStack() as local:
            coef = net.sb(local, "coef", [P, IMAGES, 2, KP])
            with ExitStack() as inner:
                tables = net.sb(inner, "tables", [P, 2, HALVES * P])
                g1 = net.sb(inner, "g1", [P, CH, 2, KP])
                g2 = net.sb(inner, "g2", [P, CH, 3, KP])
                spread_table(net, scale[:], tables[:, 0, :])
                spread_table(net, bias[:], tables[:, 1, :])
                pole_kernels(net, g1, g2)
                residues(net, x1, tables[:, 0, :], tables[:, 1, :], g1, g2, coef[:])
            image_stats = stats[:].rearrange("p h n -> p (h n)").rearrange("p (i n) -> p i n", i=CH)
            evaluate_residues(net, x1, coef, x2, image_stats)
            norm_vectors_by_image(net, image_stats, scale, bias)
        with ExitStack() as local:
            k = kan_constants(net, local)
            prepare_kan(net, k, scale[:], bias[:])
            window_layer(net, k, x2, bias, x3, by_band)
        norm_vectors(net, stats[:], "pair", 1e-5, scale[:], bias[:])
        pattern_layer(net, x3, scale, bias, out)


def shape_constants():
    p = np.arange(P)
    f = lambda a: np.ascontiguousarray(a, dtype=np.float32)
    sel = np.zeros((P, HALVES * BLOCKS, P), np.float32)
    edge = np.ones((P, BANDS), np.float32)
    for b in range(HALVES * BLOCKS):
        for g in range(GROUP):
            row = QUAD * (b % 4) + GROUP * (b // 4) + g
            sel[row, b, QUAD * g:QUAD * g + QUAD] = 1.0
            if b < HALVES * HALO and b % HALO == 0:
                edge[row, 0] = 0.0
            if b < HALVES * HALO and b % HALO == HALO - 1:
                edge[row, BANDS - 1] = 0.0
    sel8 = np.zeros((P, BLOCKS, P), np.float32)
    for k in range(P):
        sel8[k, k // 8, 16 * (k % 8):16 * (k % 8) + 16] = 1.0
    same = lambda n: p[:, None] // n == p[None] // n
    near = (p % GROUP)[:, None] + GROUP * np.arange(2)[None] - 3.5
    turn = 2 * np.pi * ((p[:, None] * p[None]) % SUB) / SUB
    return {
        "c_ident": np.eye(P, dtype=np.float32),
        "c_ones": f(np.arange(QUAD)[None, None] == GROUP * np.arange(8)[None, :, None] + (p // QUAD)[:, None, None]),
        "c_edge": edge,
        "c_pair": f(0.5 * (p[:, None] // 2 == p[None] // 2)),
        "c_channel": f((p[:, None] % CH == p[None] % CH) / GROUP),
        "c_sel": sel,
        "c_sel8": sel8,
        "c_kan_ones": f(np.stack([[np.stack([(np.arange(QUAD) // 8 == i) & (q // n == np.arange(QUAD) % 8 * 16 // n)
                                         for i in range(GROUP)]) for n in (16, 32)] for q in p])),
        "c_center": f(np.stack([np.eye(P) - same(n) / n for n in (32, 16)], axis=1)),
        "c_grid": f(np.stack([-2 * near, -near ** 2, -near], axis=2)),
        "c_dft": np.stack([np.cos(turn), np.sin(turn), -np.sin(turn)], axis=1).astype(np.float32),
        "c_freq": np.fft.fftfreq(SUB).astype(np.float32)[:, None],
        "c_mask": f(p[:, None] // MODES == p[None] // MODES),
    }


def conv_weights(w):
    out = np.zeros((4, CH, 2, 3, CH), w.dtype)
    for o in range(2):
        for dy in range(3):
            out[o + dy, :, o] = w[:, :, dy, :].transpose(1, 2, 0)
    return np.ascontiguousarray(out.reshape(P, 2, 3, CH))


def kan_arrays(a):
    place = np.arange(16).reshape(8, 2).T.ravel()
    vec, basis, silu = [np.tile(a["L2_conv_pn_" + n], GROUP) for n in "gb"], [], []
    for n in range(1, 5):
        get = lambda name: a[f"L2_conv_k{n}_{name}"]
        order = place if n < 3 else np.arange(CH)
        F = len(order)
        vec += [np.tile(get(name)[order], P // F) for name in ("ln_g", "ln_b", "bb")]
        ws = get("ws").reshape(F, F, 2, GROUP)[order][:, order]
        b = np.zeros((QUAD // F, F, GROUP, 2, QUAD // F, F), ws.dtype)
        u = np.zeros((P // F, F, P // F, F), ws.dtype)
        for d in range(QUAD // F):
            b[d, :, :, :, d, :] = ws.transpose(1, 3, 2, 0)
        for d in range(P // F):
            u[d, :, d, :] = get("wb")[order][:, order].T
        basis.append(b.reshape(P, 2, QUAD))
        silu.append(u.reshape(P, P))
    return {"kan_vec": np.stack(vec, axis=1), "kan_basis": np.stack(basis, axis=1), "kan_silu": np.stack(silu, axis=1)}


def lay_out(inputs):
    a = {k: np.asarray(v) for k, v in inputs.items()}
    per_channel = lambda v: np.ascontiguousarray(np.tile(v, GROUP)[:, None])
    d = {"x": np.ascontiguousarray(a["x"])}
    d["w1"], d["w2"] = conv_weights(a["L0_conv_w1"]), conv_weights(a["L0_conv_w2"])
    d["b1"], d["b2"] = per_channel(a["L0_conv_b1"]), per_channel(a["L0_conv_b2"])
    d["bn"] = np.concatenate([per_channel(a["L0_conv_" + k]) for k in ("g1", "beta1", "g2", "beta2")], axis=1)
    for n in ("wp1", "wp2"):
        for z in "ri":
            d[n + z] = np.ascontiguousarray(a[f"L1_conv_{n}{z}"].reshape(1, CH * KP))
    d["poles"] = np.ascontiguousarray(np.stack([np.stack([a[f"L1_conv_{n}{z}"].transpose(0, 2, 1).reshape(KP, CH)
                                                          for z in "ri"], axis=1) for n in ("wp1", "wp2")], axis=1))
    d["res"] = np.ascontiguousarray(np.stack([a[f"L1_conv_wr{z}"].transpose(1, 2, 0, 3).reshape(KP, CH, MODES)
                                              for z in "ri"], axis=2))
    d["x_grid"], d["t_grid"] = a["L1_conv_x_grid"], a["L1_conv_t_grid"]
    d.update(kan_arrays(a))
    d.update(shape_constants())
    return d


def kernel(**inputs):
    import concourse.bacc as bacc
    from concourse.bass_utils import run_bass_kernel_spmd

    arrays = lay_out(inputs)
    nc = bacc.Bacc("TRN2", target_bir_lowering=False, num_devices=1)
    ins = {n: nc.dram_tensor("in_" + n, v.shape, mybir.dt.from_np(v.dtype), kind="ExternalInput").ap()
           for n, v in arrays.items()}
    out = nc.dram_tensor("out", (IMAGES, CH, ROWS, COLS), F32, kind="ExternalOutput").ap()
    build_program(nc, ins, out)
    r = run_bass_kernel_spmd(nc, [{"in_" + n: v for n, v in arrays.items()}], core_ids=[0])
    return r.results[0]["out"]
```
